# Optimizing a Trainium2 kernel written in Bass

```python
import numpy as np
import jax
import jax.numpy as jnp

def _softmax(x, axis=-1):
    return jax.nn.softmax(x, axis=axis)

def _gelu(x):
    return jax.nn.gelu(x, approximate=True)

def _silu(x):
    return jax.nn.silu(x)

def _sigmoid(x):
    return jax.nn.sigmoid(x)

def _layernorm(x, axis=-1, eps=1e-05):
    m = jnp.mean(x, axis=axis, keepdims=True)
    v = jnp.var(x, axis=axis, keepdims=True)
    return (x - m) / jnp.sqrt(v + eps)

def _scatter_add(tgt, idx, src, axis=0):
    return tgt.at[idx].add(src)

def _segment_sum(src, seg, n):
    return jax.ops.segment_sum(src, seg, n)
kernel_name = 'mk_macaron_d1_jaxref_r8_4d0f70'

def setup_inputs(seed: int=0):
    np.random.seed(seed)
    _w = jnp.asarray

    def _L0_attn_setup():
        import jax, jax.numpy as jnp
        import numpy as np
        N_LAYERS = 4
        D_MODEL = 128
        EXPAND = 2
        D_INNER = EXPAND * D_MODEL
        D_STATE = 16
        DT_RANK = 64
        K_CONV = 4
        OUT_DIM = 128
        BATCH = 2
        SEQ = 128
        EPS = 1e-05

        def _rmsnorm(x, w):
            return x * jax.lax.rsqrt(jnp.mean(x * x, axis=-1, keepdims=True) + EPS) * w

        def _causal_depthwise_conv(x, w, b):
            xt = jnp.pad(x, ((0, 0), (K_CONV - 1, 0), (0, 0))).transpose(0, 2, 1)
            y = jax.lax.conv_general_dilated(xt, w[:, None, :], window_strides=(1,), padding='VALID', feature_group_count=x.shape[-1], dimension_numbers=('NCH', 'OIH', 'NCH'))
            return y.transpose(0, 2, 1) + b

        def _selective_scan(u, delta, A, Bm, Cm, Dp):

            def step(h, inp):
                u_t, d_t, b_t, c_t = inp
                dA = jnp.exp(d_t[:, :, None] * A)
                h = dA * h + (d_t * u_t)[:, :, None] * b_t[:, None, :]
                y = jnp.einsum('bdn,bn->bd', h, c_t)
                return (h, y)
            h0 = jnp.zeros((u.shape[0], u.shape[2], A.shape[1]), u.dtype)
            xs = (u.transpose(1, 0, 2), delta.transpose(1, 0, 2), Bm.transpose(1, 0, 2), Cm.transpose(1, 0, 2))
            _, ys = jax.lax.scan(step, h0, xs)
            return ys.transpose(1, 0, 2) + u * Dp

        def _mamba_block(x, p):
            xn = _rmsnorm(x, p['norm_w'])
            xz = xn @ p['Win']
            xp, z = jnp.split(xz, 2, axis=-1)
            xc = jax.nn.silu(_causal_depthwise_conv(xp, p['conv_w'], p['conv_b']))
            dbc = xc @ p['Wx']
            dt, Bm, Cm = jnp.split(dbc, [DT_RANK, DT_RANK + D_STATE], axis=-1)
            delta = jax.nn.softplus(dt @ p['Wdt'] + p['bdt'])
            A = -jnp.exp(p['A_log'])
            y = _selective_scan(xc, delta, A, Bm, Cm, p['Dp'])
            y = y * jax.nn.silu(z)
            return x + y @ p['Wblk']
        key = jax.random.key(seed)
        ks = jax.random.split(key, 12)
        s = 0.02

        def rn(k, shape, scale=s):
            return jax.random.normal(k, shape, dtype=jnp.float32) * scale
        A_log = jnp.log(jnp.broadcast_to(jnp.arange(1, D_STATE + 1, dtype=jnp.float32), (N_LAYERS, D_INNER, D_STATE)))
        return {'x': jax.random.normal(ks[0], (BATCH, SEQ, D_MODEL), dtype=jnp.float32), 'norm_w': jnp.ones((N_LAYERS, D_MODEL), jnp.float32), 'Win': rn(ks[1], (N_LAYERS, D_MODEL, 2 * D_INNER)), 'conv_w': rn(ks[2], (N_LAYERS, D_INNER, K_CONV), 0.1), 'conv_b': jnp.zeros((N_LAYERS, D_INNER), jnp.float32), 'Wx': rn(ks[3], (N_LAYERS, D_INNER, DT_RANK + 2 * D_STATE)), 'Wdt': rn(ks[4], (N_LAYERS, DT_RANK, D_INNER), 0.1), 'bdt': rn(ks[5], (N_LAYERS, D_INNER), 0.1), 'A_log': A_log, 'Dp': jnp.ones((N_LAYERS, D_INNER), jnp.float32), 'Wblk': rn(ks[6], (N_LAYERS, D_INNER, D_MODEL)), 'Wout': rn(ks[7], (D_MODEL, OUT_DIM)), 'bout': jnp.zeros((OUT_DIM,), jnp.float32)}
    _L0_attn_in = _L0_attn_setup()

    def _L0_ffn_setup():
        import jax, jax.numpy as jnp
        import numpy as np
        D, F, E, K = (128, 344, 8, 2)
        key = jax.random.key(seed)
        k0, k1, k2, k3, k4 = jax.random.split(key, 5)
        s = 0.02
        x = jax.random.normal(k0, (2, 64, D), jnp.float32)
        Ws = jax.random.normal(k1, (D, E), jnp.float32) * s
        bs = jnp.zeros((E,), jnp.float32)
        Wg = jax.random.normal(k2, (E, D, F), jnp.float32) * s
        Wu = jax.random.normal(k3, (E, D, F), jnp.float32) * s
        Wd = jax.random.normal(k4, (E, F, D), jnp.float32) * s
        return {'x': x, 'Ws': Ws, 'bs': bs, 'Wg': Wg, 'Wu': Wu, 'Wd': Wd}
    _L0_ffn_in = _L0_ffn_setup()
    _d = {'L0_attn_x': _L0_attn_in['x'], 'L0_attn_norm_w': _L0_attn_in['norm_w'], 'L0_attn_Win': _L0_attn_in['Win'], 'L0_attn_conv_w': _L0_attn_in['conv_w'], 'L0_attn_conv_b': _L0_attn_in['conv_b'], 'L0_attn_Wx': _L0_attn_in['Wx'], 'L0_attn_Wdt': _L0_attn_in['Wdt'], 'L0_attn_bdt': _L0_attn_in['bdt'], 'L0_attn_A_log': _L0_attn_in['A_log'], 'L0_attn_Dp': _L0_attn_in['Dp'], 'L0_attn_Wblk': _L0_attn_in['Wblk'], 'L0_attn_Wout': _L0_attn_in['Wout'], 'L0_attn_bout': _L0_attn_in['bout'], 'L0_ffn_Ws': _L0_ffn_in['Ws'], 'L0_ffn_bs': _L0_ffn_in['bs'], 'L0_ffn_Wg': _L0_ffn_in['Wg'], 'L0_ffn_Wu': _L0_ffn_in['Wu'], 'L0_ffn_Wd': _L0_ffn_in['Wd']}
    _x0 = _d['L0_attn_x']
    _d['L0_attn_x'] = jax.random.normal(jax.random.fold_in(jax.random.key(seed), 1), (16, 512, 128), dtype=_x0.dtype)
    del _x0
    return _d

def reference(L0_attn_x, L0_attn_norm_w, L0_attn_Win, L0_attn_conv_w, L0_attn_conv_b, L0_attn_Wx, L0_attn_Wdt, L0_attn_bdt, L0_attn_A_log, L0_attn_Dp, L0_attn_Wblk, L0_attn_Wout, L0_attn_bout, L0_ffn_Ws, L0_ffn_bs, L0_ffn_Wg, L0_ffn_Wu, L0_ffn_Wd):

    def _L0_attn_ref(x, norm_w, Win, conv_w, conv_b, Wx, Wdt, bdt, A_log, Dp, Wblk, Wout, bout):
        import jax, jax.numpy as jnp
        import numpy as np
        N_LAYERS = 4
        D_MODEL = 128
        EXPAND = 2
        D_INNER = EXPAND * D_MODEL
        D_STATE = 16
        DT_RANK = 64
        K_CONV = 4
        OUT_DIM = 128
        BATCH = 2
        SEQ = 128
        EPS = 1e-05

        def _rmsnorm(x, w):
            return x * jax.lax.rsqrt(jnp.mean(x * x, axis=-1, keepdims=True) + EPS) * w

        def _causal_depthwise_conv(x, w, b):
            xt = jnp.pad(x, ((0, 0), (K_CONV - 1, 0), (0, 0))).transpose(0, 2, 1)
            y = jax.lax.conv_general_dilated(xt, w[:, None, :], window_strides=(1,), padding='VALID', feature_group_count=x.shape[-1], dimension_numbers=('NCH', 'OIH', 'NCH'))
            return y.transpose(0, 2, 1) + b

        def _selective_scan(u, delta, A, Bm, Cm, Dp):

            def step(h, inp):
                u_t, d_t, b_t, c_t = inp
                dA = jnp.exp(d_t[:, :, None] * A)
                h = dA * h + (d_t * u_t)[:, :, None] * b_t[:, None, :]
                y = jnp.einsum('bdn,bn->bd', h, c_t)
                return (h, y)
            h0 = jnp.zeros((u.shape[0], u.shape[2], A.shape[1]), u.dtype)
            xs = (u.transpose(1, 0, 2), delta.transpose(1, 0, 2), Bm.transpose(1, 0, 2), Cm.transpose(1, 0, 2))
            _, ys = jax.lax.scan(step, h0, xs)
            return ys.transpose(1, 0, 2) + u * Dp

        def _mamba_block(x, p):
            xn = _rmsnorm(x, p['norm_w'])
            xz = xn @ p['Win']
            xp, z = jnp.split(xz, 2, axis=-1)
            xc = jax.nn.silu(_causal_depthwise_conv(xp, p['conv_w'], p['conv_b']))
            dbc = xc @ p['Wx']
            dt, Bm, Cm = jnp.split(dbc, [DT_RANK, DT_RANK + D_STATE], axis=-1)
            delta = jax.nn.softplus(dt @ p['Wdt'] + p['bdt'])
            A = -jnp.exp(p['A_log'])
            y = _selective_scan(xc, delta, A, Bm, Cm, p['Dp'])
            y = y * jax.nn.silu(z)
            return x + y @ p['Wblk']
        layer_params = {'norm_w': norm_w, 'Win': Win, 'conv_w': conv_w, 'conv_b': conv_b, 'Wx': Wx, 'Wdt': Wdt, 'bdt': bdt, 'A_log': A_log, 'Dp': Dp, 'Wblk': Wblk}

        def layer_step(h, p):
            return (_mamba_block(h, p), None)
        h, _ = jax.lax.scan(layer_step, x, layer_params)
        return h @ Wout + bout

    def _L0_ffn_ref(x, Ws, bs, Wg, Wu, Wd):
        import jax, jax.numpy as jnp
        import numpy as np
        D, F, E, K = (128, 344, 8, 2)
        b, n, d = x.shape
        xt = x.reshape(-1, d)
        logits = xt @ Ws + bs
        topk_w, topk_idx = jax.lax.top_k(logits, K)
        topk_w = jax.nn.softmax(topk_w, axis=-1)
        combine = jnp.sum(jax.nn.one_hot(topk_idx, E, dtype=xt.dtype) * topk_w[..., None], axis=1)
        g = jnp.einsum('td,edf->tef', xt, Wg)
        u = jnp.einsum('td,edf->tef', xt, Wu)
        h = jax.nn.silu(g) * u
        y = jnp.einsum('tef,efd->ted', h, Wd)
        out = jnp.einsum('ted,te->td', y, combine)
        return out.reshape(b, n, d)
    x = L0_attn_x
    x = x + 0.5 * _L0_ffn_ref(_layernorm(x, axis=-1), L0_ffn_Ws, L0_ffn_bs, L0_ffn_Wg, L0_ffn_Wu, L0_ffn_Wd)
    x = x + _L0_attn_ref(_layernorm(x, axis=-1), L0_attn_norm_w, L0_attn_Win, L0_attn_conv_w, L0_attn_conv_b, L0_attn_Wx, L0_attn_Wdt, L0_attn_bdt, L0_attn_A_log, L0_attn_Dp, L0_attn_Wblk, L0_attn_Wout, L0_attn_bout)
    x = x + 0.5 * _L0_ffn_ref(_layernorm(x, axis=-1), L0_ffn_Ws, L0_ffn_bs, L0_ffn_Wg, L0_ffn_Wu, L0_ffn_Wd)
    return x

_drawn_inputs = setup_inputs


def setup_inputs(seed=0):
    import zlib

    import numpy as np

    out = dict(_drawn_inputs(seed))
    spreads = {'L0_attn_norm_w': (1.0, 0.2),
     'L0_attn_conv_b': (0.0, 0.1),
     'L0_attn_Dp': (1.0, 0.2),
     'L0_attn_bout': (0.0, 0.1),
     'L0_ffn_bs': (0.0, 0.1)}
    factors = {}
    for name, (base, spread) in spreads.items():
        noise = np.random.default_rng([zlib.crc32(name.encode()), seed]).standard_normal(out[name].shape)
        drawn = base * np.exp(spread * noise) if base else spread * noise
        out[name] = jnp.asarray(drawn.astype(out[name].dtype))
    for name, factor in factors.items():
        out[name] = (out[name] * factor).astype(out[name].dtype)
    return out
```

```python
from contextlib import ExitStack

import concourse.bass as bass
from concourse import mybir

F32 = mybir.dt.float32
BF16 = mybir.dt.bfloat16
U32 = mybir.dt.uint32
ALU = mybir.AluOpType
ACT = mybir.ActivationFunctionType

B, T, D = 16, 512, 128
NL, NS, KC, DTR = 4, 16, 4, 64
NBLK = 2
TB = T // 128
E, F = 8, 344
FT = [(0, 128), (128, 128), (256, 88)]
EPS = 1e-5
PAIRS = B // 2
PH = 2 * NL
SL = 2 * NS
US = 2 * SL
SPLUS = 40.0

SIDE = [
    (5, "wblk", 6), (8, "ms", 9), (10, "attn", 11), (11, "xp0", 12), (12, "xp1", 13), (13, "z0", 14),
    (15, "z1", 16), (18, "wx", 19), (20, "dt0", 21), (22, "dt1", 23),
]
EB = [2 + 7 * e for e in range(E)]
UNIT = sorted([(EB[e], f"cbc{e}", EB[e] + 1) for e in range(E)]
              + [(EB[e] + 10, f"down{e}", EB[e] + 11) for e in range(E - 1)]
              + [(60, "down7", 61), (62, "yt", 63)])
START = [(48, "xt", 49), (50, "lg", 51), (54, "ct", 56)]
LN2 = [(4, "ht", 5)]


class Signal:

    def __init__(self, sem, credit, pro, trip, step=1):
        self.sem, self.credit, self.pro, self.trip, self.step = sem, credit, pro, trip, step


class Section:
    def __init__(self, kind, it=None):
        self.kind, self.it = kind, it

    def v(self, s, n):
        if self.kind == "pro":
            return (s.credit + n + 1) * s.step
        before = s.credit + s.pro
        if self.kind == "epi":
            return (before + PAIRS * s.trip + n + 1) * s.step
        assert before + n + 1 >= 1, (s.sem, n)
        return self.it * (s.trip * s.step) + (before + n + 1) * s.step

    def after(self, s, n):
        val = self.v(s, n)
        return s.sem, (max(val, 0) if isinstance(val, int) else val)


def shared_bank_order():
    order = {}
    jobs = []
    for name in ("xt", "lg", "ct"):
        jobs.append(("s0", name))
    for u in range(2):
        for s in range(US):
            jobs += [(("u", u), n) for t, n, _ in UNIT if t == s]
            jobs += [(("st", u), n) for t, n, _ in START if t == s]
            if u == 1:
                jobs += [(("ln", 0), n) for t, n, _ in LN2 if t == s]
    jobs.append((("ln", 1), "ht"))
    jobs += [(("p", -1), n) for _, n, _ in SIDE if n not in ("wblk", "attn")]
    order["pro"] = {j: i for i, j in enumerate(jobs)}
    jobs = []
    last = -9
    for q in range(PH):
        for s in range(SL):
            u, S = q // 2, (q % 2) * SL + s
            here = [(("p", q), n, c) for t, n, c in SIDE if t == s and (n != "attn" or q in (0, PH - 1))]
            here += [(("u", u), n, c - S + s) for t, n, c in UNIT if t == S]
            here += [(("st", u), n, c - S + s) for t, n, c in START if t == S]
            if u in (1, 2):
                here += [(("ln", u - 1), n, c - S + s) for t, n, c in LN2 if t == S]
            for k, n, c in here:
                assert last <= q * SL + s + 1, ("the bank is read too late", k, n, last, q * SL + s)
                last = q * SL + c
                jobs.append((k, n))
    order["body"] = {j: i for i, j in enumerate(jobs)}
    jobs = [(("p", 0), "wblk"), (("p", 0), "attn")]
    jobs += [("s2", n) for n in ("xt", "lg", "ct")]
    for u in (2, 3):
        for s in range(US):
            jobs += [(("u", u), n) for t, n, _ in UNIT if t == s]
            if u == 2:
                jobs += [(("st", u), n) for t, n, _ in START if t == s]
    order["epi"] = {j: i for i, j in enumerate(jobs)}
    return order


def build(nc, x, norm_w, Win, conv_w, conv_b, Wx, Wdt, bdt, A_log, Dp, Wblk, Wout, bout,
          Ws, bs, Wg, Wu, Wd, out):
    JOBS = shared_bank_order()
    with ExitStack() as ctx:
        def sb(name, shape, dt=F32):
            return ctx.enter_context(nc.sbuf_tensor(name, shape, dt))

        def bank(name):
            return ctx.enter_context(nc.psum_tensor(name, [128, T], F32))

        wg_sb = sb("wg_sb", [128, E, F])
        wu_sb = sb("wu_sb", [128, E, F])
        wd_sb = sb("wd_sb", [128, E, len(FT), D])
        win_sb = sb("win_sb", [128, NL, 4 * 128])
        wx_sb = sb("wx_sb", [128, NL, NBLK, DTR + 2 * NS])
        wdt_sb = sb("wdt_sb", [DTR, NL, NBLK * 128])
        wblk_sb = sb("wblk_sb", [128, NL, NBLK, D])
        wout_sb = sb("wout_sb", [128, D])
        bout_sb = sb("bout_sb", [1, D])
        ws_sb = sb("ws_sb", [128, E])
        bs_sb = sb("bs_sb", [128, E])
        normw_sb = sb("normw_sb", [128, NL])
        cw_sb = sb("cw_sb", [128, NL, NBLK, KC])
        cb_sb = sb("cb_sb", [128, NL, NBLK])
        bdt_sb = sb("bdt_sb", [128, NL, NBLK])
        a_sb = sb("a_sb", [128, NL, NBLK, NS])
        dp_sb = sb("dp_sb", [128, NL, NBLK])
        ident = sb("ident", [128, 128])
        mean_w = sb("mean_w", [128, 128])
        ones_row = sb("ones_row", [1, 128])
        sel_bc = sb("sel_bc", [96, 2 * NS, 128], BF16)
        sel_e = sb("sel_e", [96, E, 128], BF16)
        iota_e = sb("iota_e", [128, E])
        neg_half = sb("neg_half", [128, TB])
        eps_sb = sb("eps_sb", [128, 1])
        eps4 = sb("eps4", [128, TB])
        credit = sb("credit", [128, 4])
        carrier = sb("carrier", [128, 1])
        b_sb = sb("b_sb", [128, 2, T])
        dbu_sb = sb("dbu_sb", [128, 4, T])
        st_sb = sb("st_sb", [128, 2, T])
        prod_sb = sb("prod_sb", [128, 3, T])
        delta_sb = sb("delta_sb", [128, 2, NBLK, T])
        du_sb = sb("du_sb", [128, 2, NBLK, T])
        xc_sb = sb("xc_sb", [128, 2, NBLK, T])
        zs_sb = sb("zs_sb", [128, 2, NBLK, T])
        bc3 = sb("bc3", [96, 2, T], BF16)
        y_sb = sb("y_sb", [128, NBLK, T])
        h_sb = sb("h_sb", [128, 2, T])
        hin_sb = sb("hin_sb", [128, 2, T])
        norm_t = sb("norm_t", [128, T])
        xn_sb = sb("xn_sb", [128, T])
        xpad = sb("xpad", [128, NBLK, KC - 1 + T])
        conv_sb = sb("conv_sb", [128, NBLK, T])
        th_c = sb("th_c", [128, NBLK, T])
        th_z = sb("th_z", [128, T])
        dt_sb = sb("dt_sb", [DTR, T])
        bc_rest = sb("bc_rest", [64, T])
        sp_x, sp_l = conv_sb, th_c
        xin_sb = sb("xin_sb", [128, 2, TB, D])
        x1_new = sb("x1_new", [128, 2, TB, D])
        x1_sb = sb("x1_sb", [128, 2, TB, D])
        x2_sb = sb("x2_sb", [128, 2, TB, D])
        xtok = sb("xtok", [128, TB, D])
        bn_sb = sb("bn_sb", [128, TB, 6])
        mv_sb = sb("mv_sb", [128, TB, 2])
        rs_sb = sb("rs_sb", [128, 2, TB])
        xT_sb = sb("xT_sb", [128, 2, T])
        xs_sb = sb("xs_sb", [128, T])
        acc_sb = sb("acc_sb", [128, T])
        th_g = sb("th_g", [128, 2, T])
        h1_sb = th_g
        uc_sb = sb("uc_sb", [128, 2, T])
        hh_sb = sb("hh_sb", [128, 6, T])
        lg_sb = sb("lg_sb", [128, TB, E])
        mx_sb = sb("mx_sb", [128, TB, E])
        mi_sb = sb("mi_sb", [128, TB, E], U32)
        mf_sb = sb("mf_sb", [128, TB, 2])
        wt_sb = sb("wt_sb", [128, 5, TB])
        eq_sb = sb("eq_sb", [128, 4, TB, E])
        comb_sb = sb("comb_sb", [128, TB, E])
        c3 = sb("c3", [96, 2, T], BF16)
        c_rest = sb("c_rest", [64, T])
        dA_ps, b_ps, c_ps = bank("dA_ps"), bank("b_ps"), bank("c_ps")
        y_ps = [bank("y0_ps"), bank("y1_ps")]
        g_ps, u_ps, sh = bank("g_ps"), bank("u_ps"), bank("sh")

        def signal(name, credit=0, pro=0, trip=0, step=1):
            return Signal(ctx.enter_context(nc.semaphore(name)), credit, pro, trip, step)

        NG, SG = PH * NS, PH * SL
        b_full, b_copied = signal("b_full", 0, 0, NG), signal("b_copied", 0, 0, NG)
        c_full = signal("c_full", 1, 0, NG)
        dA_ready = signal("dA_ready", 0, 0, SG)
        dbu_ready = signal("dbu_ready", 1, 0, SG)
        scanned = signal("scanned", 4, 0, SG)
        prod_ready = signal("prod_ready", 2, 0, SG)
        summed = signal("summed", 3, 0, SG)
        y_taken, y_gated = signal("y_taken", 0, 0, 2 * PH), signal("y_gated", 0, 0, 2 * PH)
        h_ready = signal("h_ready", 1, 0, PH)
        x2_ready = signal("x2_ready", 1, 0, 2)
        x1_moved = signal("x1_moved", 1, 0, 2)
        sq_ready, log_ready, rms_ready, xn_ready = (signal(n, 0, 1, PH) for n in ("sq_ready", "log_ready", "rms_ready", "xn_ready"))
        xp_ready, thc_ready, xc_ready, thz_ready, zs_ready = (
            signal(n, 0, 2, 2 * PH) for n in ("xp_ready", "thc_ready", "xc_ready", "thz_ready", "zs_ready"))
        conv_step = signal("conv_step", 0, 8, 8 * PH)
        dt_ready, bhi_ready, brest_ready, bmid_ready, blo_ready = (
            signal(n, 0, 1, PH) for n in ("dt_ready", "bhi_ready", "brest_ready", "bmid_ready", "blo_ready"))
        spx_ready, spm_ready, spe_ready, spl_ready, delta_ready, du_ready = (
            signal(n, 0, 2, 2 * PH) for n in ("spx_ready", "spm_ready", "spe_ready", "spl_ready", "delta_ready", "du_ready"))
        bn_done, mv_done, xtok_ready = (signal(n, 0, 5 * TB, 6 * TB) for n in ("bn_done", "mv_done", "xtok_ready"))
        ve_done, rs_done = signal("ve_done", 0, 5, 6), signal("rs_done", 0, 5, 6)
        xT_ready, lg_ready, dd_ready, we_ready, comb_ready, chi_ready, crest_ready, cmid_ready, clo_ready = (
            signal(n, 0, 3, 4) for n in ("xT_ready", "lg_ready", "dd_ready", "we_ready", "comb_ready",
                                         "chi_ready", "crest_ready", "cmid_ready", "clo_ready"))
        rt_step = signal("rt_step", 0, 3 * 17, 4 * 17)
        xs_ready, acc_ready = signal("xs_ready", 0, 2 * E, 4 * E), signal("acc_ready", 0, 2 * E, 4 * E)
        g_full, u_full, thg_ready, h1_ready, uc_ready, hh_ready = (
            signal(n, 0, 6 * E, 12 * E) for n in ("g_full", "u_full", "thg_ready", "h1_ready", "uc_ready", "hh_ready"))
        x1_ready, hin_ready = signal("x1_ready", 0, 2, 2), signal("hin_ready", 0, 2, 2)
        xo_ready = signal("xo_ready", 1, 0, 2)
        x_loaded = signal("x_loaded", 0, 3, 2, 16)
        stored = signal("stored", 1, 0, 2, 16)
        sh_full = signal("sh_full", 0, len(JOBS["pro"]), len(JOBS["body"]))
        w_loaded = ctx.enter_context(nc.semaphore("w_loaded"))
        consts = ctx.enter_context(nc.semaphore("consts"))
        vprep = ctx.enter_context(nc.semaphore("vprep"))
        aexp = ctx.enter_context(nc.semaphore("aexp"))
        cprep = ctx.enter_context(nc.semaphore("cprep"))

        LOADS = 19

        def filled(sec, key, name):
            return sec.after(sh_full, JOBS[sec.kind][(key, name)])

        def slot_of(q, s):
            return q // 2, (q % 2) * SL + s

        x_rows = x.rearrange("(p j) (k t) d -> p j t k d", j=2, t=128)
        out_rows = out.rearrange("(p j) (k t) d -> p j t k d", j=2, t=128)

        def unit_no(sec, u):
            return u - 2 if sec.kind == "epi" else u

        def start_no(sec, u):
            if sec.kind == "pro":
                return u
            if sec.kind == "body":
                return u - 1
            return u - 2

        def start_par(sec, u):
            return (u + 1) % 2 if sec.kind == "epi" else u % 2

        NORM_NO = {"pro": {"s0": 0, ("st", 0): 1, ("ln", 0): 2, ("st", 1): 3, ("ln", 1): 4},
                   "body": {("st", 0): 0, ("ln", 0): 1, ("st", 1): 2, ("ln", 1): 3, ("st", 2): 4, ("st", 3): 5},
                   "epi": {"s2": 0, ("st", 2): 1}}

        def served(sec, key):
            if key == "s0":
                return 0
            if key == "s2":
                return 2
            if sec.kind == "pro" and key[1] == 1:
                return 2
            return key[1] + 1

        def st_no(sec, key):
            if sec.kind == "pro":
                return served(sec, key)
            if sec.kind == "body":
                return key[1]
            return 0 if key == "s2" else 1

        def st_par(sec, key):
            if sec.kind == "pro":
                return st_no(sec, key) % 2
            if sec.kind == "body":
                return (key[1] + 1) % 2
            return (st_no(sec, key) + 1) % 2

        def st_src(sec, key):
            u = served(sec, key) % 4 if sec.kind != "pro" else served(sec, key) % 2
            return (xin_sb[:, u], None) if u < 2 else (x2_sb[:, u - 2], u - 2)

        block = ctx.enter_context(nc.Block())

        @block.sync
        def _(sp):
            sp.dma_start(xin_sb[:, 0], x_rows[0, 0]).then_inc(x_loaded.sem, 16)
            sp.dma_start(xin_sb[:, 1], x_rows[0, 1]).then_inc(x_loaded.sem, 16)
            for dst, src in (
                (ws_sb[:, :], Ws), (bs_sb[:, :], bs.broadcast_to([128, E])),
                (wg_sb[:, :, :], Wg), (wu_sb[:, :, :], Wu),
                (wd_sb[:, :, 0, :], Wd[0:128]), (wd_sb[:, :, 1, :], Wd[128:256]), (wd_sb[0:88, :, 2, :], Wd[256:344]),
                (win_sb[:, :, :], Win), (wx_sb[:, :, :, :], Wx), (wdt_sb[:, :, :], Wdt),
                (wblk_sb[:, :, :, :], Wblk), (wout_sb[:, :], Wout), (bout_sb[:, :], bout),
                (normw_sb[:, :], norm_w), (cw_sb[:, :, :, :], conv_w), (cb_sb[:, :, :], conv_b),
                (bdt_sb[:, :, :], bdt), (a_sb[:, :, :, :], A_log), (dp_sb[:, :, :], Dp),
            ):
                sp.dma_start(dst, src).then_inc(w_loaded, 16)
            pro = Section("pro")
            sp.wait_ge(*pro.after(x1_ready, 0))
            sp.dma_start(xin_sb[:, 0], x_rows[1, 0]).then_inc(x_loaded.sem, 16)

            sec = Section("epi")
            for j in range(2):
                sp.wait_ge(*sec.after(xo_ready, j))
                sp.dma_start(out_rows[PAIRS - 1, j], x2_sb[:, j]).then_inc(stored.sem, 16)
            sp.wait_ge(*sec.after(stored, 1))
            sp.wait_ge(*sec.after(x_loaded, -1))

        @block.tensor
        def _(pe):
            job_count = [0]
            bank_free = []

            def fill(sec, key, name, freed):
                assert JOBS[sec.kind][(key, name)] == job_count[0], (key, name)
                job_count[0] += 1
                for s, n in bank_free:
                    pe.wait_ge(*sec.after(s, n))
                bank_free[:] = [freed]

            def transposes(src):
                for k in range(TB):
                    last = pe.transpose(sh[:, k * 128:(k + 1) * 128], src(k), ident[:, :])
                last.then_inc(sh_full.sem, 1)

            def start_job(sec, key, name):
                a = st_no(sec, key)
                par = st_par(sec, key)
                if name == "xt":
                    fill(sec, key, name, (xT_ready, a))
                    pe.wait_ge(*sec.after(xtok_ready, NORM_NO[sec.kind][key] * TB + TB - 1))
                    transposes(lambda k: xtok[:, k, :])
                elif name == "lg":
                    fill(sec, key, name, (lg_ready, a))
                    pe.wait_ge(*sec.after(xT_ready, a))
                    for k in range(TB):
                        last = pe.matmul(sh[:, k * E:(k + 1) * E], xT_sb[:, par, k * 128:(k + 1) * 128],
                                         ws_sb[:, :], start=True, stop=True)
                    last.then_inc(sh_full.sem, 1)
                else:
                    fill(sec, key, name, (crest_ready, a))
                    pe.wait_ge(*sec.after(comb_ready, a))
                    for k in range(TB):
                        last = pe.transpose(sh[0:E, k * 128:(k + 1) * 128], comb_sb[:, k, :], ident[:, :])
                    last.then_inc(sh_full.sem, 1)

            def norm_job(sec, key):
                j = key[1]
                fill(sec, key, "ht", (hin_ready, j))
                pe.wait_ge(*sec.after(xtok_ready, NORM_NO[sec.kind][key] * TB + TB - 1))
                transposes(lambda k: xtok[:, k, :])

            def unit_slot(sec, u, S):
                un = unit_no(sec, u)
                par = start_par(sec, u)
                for e in range(E):
                    x_no = un * E + e
                    if S == EB[e]:
                        fill(sec, ("u", u), f"cbc{e}", (xs_ready, x_no))
                        pe.wait_ge(*sec.after(clo_ready, start_no(sec, u)))
                        pe.matmul(sh[:, :], sel_e[:, e, :], c3[:, par, :], start=True, stop=True).then_inc(sh_full.sem, 1)
                    for ft, (f0, fn) in enumerate(FT):
                        n = x_no * 3 + ft
                        if S == EB[e] + 1 + 2 * ft:
                            pe.wait_ge(*sec.after(xT_ready, start_no(sec, u)))
                            pe.wait_ge(*sec.after(h1_ready, n - 1))
                            pe.matmul(g_ps[0:fn, :], wg_sb[:, e, f0:f0 + fn], xT_sb[:, par, :],
                                      start=True, stop=True).then_inc(g_full.sem, 1)
                        if S == EB[e] + 2 + 2 * ft:
                            pe.wait_ge(*sec.after(xs_ready, x_no))
                            pe.wait_ge(*sec.after(uc_ready, n - 1))
                            pe.matmul(u_ps[0:fn, :], wu_sb[:, e, f0:f0 + fn], xs_sb[:, :],
                                      start=True, stop=True).then_inc(u_full.sem, 1)
                    if S == (EB[e] + 10 if e < E - 1 else 60):
                        fill(sec, ("u", u), f"down{e}", (acc_ready, x_no))
                        pe.wait_ge(*sec.after(hh_ready, x_no * 3 + 2))
                        for ft, (f0, fn) in enumerate(FT):
                            last = pe.matmul(sh[:, :], wd_sb[0:fn, e, ft, :], hh_sb[0:fn, (e % 2) * 3 + ft, :],
                                             start=(ft == 0), stop=(ft == 2))
                        last.then_inc(sh_full.sem, 1)
                if S == 62:
                    if u < 2:
                        fill(sec, ("u", u), "yt", (x1_ready, u))
                    else:
                        fill(sec, ("u", u), "yt", (xo_ready, u - 2))
                    pe.wait_ge(*sec.after(acc_ready, un * E + E - 1))
                    transposes(lambda k: acc_sb[:, k * 128:(k + 1) * 128])

            def side_job(sec, q, k, name):
                r = (q + 1) % PH
                l, j, par = r // 2, r % 2, r % 2
                pl, pj = ((q - 1) % PH) // 2, (q - 1) % 2
                key = ("p", q)
                if name == "wblk":
                    fill(sec, key, name, (h_ready, k))
                    pe.wait_ge(*sec.after(y_gated, 2 * k + 1))
                    for b in range(NBLK):
                        last = pe.matmul(sh[:, :], wblk_sb[:, pl, b, :], y_sb[:, b, :], start=(b == 0), stop=(b == 1))
                elif name == "attn":
                    fill(sec, key, name, (x2_ready, 0 if q == 0 else 1))
                    pe.wait_ge(*sec.after(h_ready, k))
                    for t in range(TB):
                        o = sh[:, t * D:(t + 1) * D]
                        pe.matmul(o, h_sb[:, pj, t * 128:(t + 1) * 128], wout_sb[:, :], start=True, stop=False)
                        last = pe.matmul(o, ones_row[:, :], bout_sb[:, :], start=False, stop=True)
                elif name == "ms":
                    fill(sec, key, name, (log_ready, k))
                    pe.wait_ge(*sec.after(sq_ready, k))
                    last = pe.matmul(sh[:, :], mean_w[:, :], norm_t[:, :], start=True, stop=True)
                elif name in ("xp0", "xp1", "z0", "z1"):
                    b = int(name[-1])
                    fill(sec, key, name, (xp_ready if name[0] == "x" else zs_ready, 2 * k + b))
                    pe.wait_ge(*sec.after(xn_ready, k))
                    c = (b if name[0] == "x" else NBLK + b) * 128
                    last = pe.matmul(sh[:, :], win_sb[:, l, c:c + 128], xn_sb[:, :], start=True, stop=True)
                elif name == "wx":
                    fill(sec, key, name, (brest_ready, k))
                    pe.wait_ge(*sec.after(xc_ready, 2 * k + 1))
                    for b in range(NBLK):
                        last = pe.matmul(sh[0:96, :], wx_sb[:, l, b, :], xc_sb[:, par, b, :], start=(b == 0), stop=(b == 1))
                else:
                    b = int(name[-1])
                    fill(sec, key, name, (spx_ready, 2 * k + b))
                    pe.wait_ge(*sec.after(dt_ready, k))
                    last = pe.matmul(sh[:, :], wdt_sb[:, l, b * 128:(b + 1) * 128], dt_sb[:, :], start=True, stop=True)
                last.then_inc(sh_full.sem, 1)

            def b_spread(sec, g, par):
                pe.matmul(b_ps[:, :], sel_bc[:, g % NS, :], bc3[:, par, :], start=True, stop=True).then_inc(b_full.sem, 1)

            def add_state(sec, g):
                q, s = g // SL, g % SL
                pe.wait_ge(*sec.after(prod_ready, g))
                if s < 2:
                    pe.wait_ge(*sec.after(y_taken, 2 * q + s))
                pe.matmul(y_ps[s % 2][:, :], ident[:, :], prod_sb[:, g % 3, :], start=(s < 2),
                          stop=(s >= SL - 2)).then_inc(summed.sem, 1)

            pe.wait_ge(w_loaded, 16 * LOADS)
            pe.wait_ge(consts, 5)
            pe.wait_ge(vprep, 10)
            for b in range(NBLK):
                pe.matmul(y_ps[b][:, :], ident[:, :], x2_sb[:, 0].rearrange("p k d -> p (k d)"), start=True, stop=True).then_inc(summed.sem, 1)
            pe.matmul(c_ps[:, :], ident[:, :], x2_sb[:, 0].rearrange("p k d -> p (k d)"), start=True, stop=True).then_inc(summed.sem, 1)
            pe.matmul(c_ps[:, :], ident[:, :], x2_sb[:, 0].rearrange("p k d -> p (k d)"), start=True, stop=True).then_inc(c_full.sem, 1)
            sec = Section("pro")
            for name in ("xt", "lg", "ct"):
                start_job(sec, "s0", name)
            for u in range(2):
                for S in range(US):
                    unit_slot(sec, u, S)
                    for t, name, _ in START:
                        if t == S:
                            start_job(sec, ("st", u), name)
                    if u == 1 and S == LN2[0][0]:
                        norm_job(sec, ("ln", 0))
            norm_job(sec, ("ln", 1))
            for _, name, _ in SIDE:
                if name not in ("wblk", "attn"):
                    side_job(sec, -1, 0, name)
            pe.wait_ge(*sec.after(blo_ready, 0))
            b_spread(sec, 0, 0)

            with pe.Fori(0, PAIRS) as it:
                sec = Section("body", it)
                job_count[0] = 0
                bank_free[:] = [(spx_ready, -1), (xo_ready, -1), (crest_ready, -1), (hin_ready, -1)]
                for q in range(PH):
                    for s in range(SL):
                        n, g, gn = s // 2, q * SL + s, q * NS + s // 2
                        u, S = slot_of(q, s)
                        if s % 2 == 0:
                            pe.wait_ge(*sec.after(blo_ready, q - 1))
                            pe.wait_ge(*sec.after(prod_ready, g - 1))
                            pe.matmul(c_ps[:, :], sel_bc[:, NS + n, :], bc3[:, q % 2, :], start=True,
                                      stop=True).then_inc(c_full.sem, 1)
                            pe.wait_ge(*sec.after(b_copied, gn))
                            if n == NS - 1:
                                pe.wait_ge(*sec.after(blo_ready, q))
                                b_spread(sec, gn + 1, (q + 1) % 2)
                            else:
                                b_spread(sec, gn + 1, q % 2)
                        if g > 0:
                            add_state(sec, g - 1)
                        if g == SG - 1:
                            add_state(sec, g)
                        for t, name, _ in SIDE:
                            if t == s and (name != "attn" or q in (0, PH - 1)):
                                side_job(sec, q, q, name)
                        unit_slot(sec, u, S)
                        for t, name, _ in START:
                            if t == S:
                                start_job(sec, ("st", u), name)
                        if u in (1, 2) and S == LN2[0][0]:
                            norm_job(sec, ("ln", u - 1))

            sec = Section("epi")
            job_count[0] = 0
            bank_free[:] = [(spx_ready, -1), (xo_ready, -1), (crest_ready, -1)]
            side_job(sec, 0, 0, "wblk")
            side_job(sec, 0, 0, "attn")
            for name in ("xt", "lg", "ct"):
                start_job(sec, "s2", name)
            for u in (2, 3):
                for S in range(US):
                    unit_slot(sec, u, S)
                    if u == 2:
                        for t, name, _ in START:
                            if t == S:
                                start_job(sec, ("st", u), name)

        @block.scalar
        def _(act):
            def start_act(sec, key, step):
                a, par = st_no(sec, key), st_par(sec, key)
                if step == 49:
                    act.wait_ge(*filled(sec, key, "xt"))
                    done = (unit_no(sec, key[1]) * 24 - 1) if isinstance(key, tuple) else -1
                    act.wait_ge(*sec.after(u_full, done))
                    act.activation(xT_sb[:, par, :], sh[:, :], ACT.Copy).then_inc(xT_ready.sem, 1)
                elif step == 52:
                    act.wait_ge(*sec.after(dd_ready, a))
                    act.wait_ge(*sec.after(rt_step, a * 17 - 1))
                    act.activation(wt_sb[:, 1, :], wt_sb[:, 0, :], ACT.Exp).then_inc(we_ready.sem, 1)
                elif step == 55:
                    act.wait_ge(*filled(sec, key, "ct"))
                    act.activation(c3[0:E, par, :], sh[0:E, :], ACT.Copy).then_inc(chi_ready.sem, 1)
                elif step == 57:
                    act.wait_ge(*sec.after(crest_ready, a))
                    act.activation(c3[32:32 + E, par, :], c_rest[32:32 + E, :], ACT.Copy).then_inc(cmid_ready.sem, 1)

            def unit_act(sec, u, S):
                un = unit_no(sec, u)
                for e in range(E):
                    for ft, (f0, fn) in enumerate(FT):
                        n = (un * E + e) * 3 + ft
                        if S == EB[e] + 2 + 2 * ft:
                            act.wait_ge(*sec.after(g_full, n))
                            act.wait_ge(*sec.after(hh_ready, n - 2))
                            act.activation(th_g[0:fn, n % 2, :], g_ps[0:fn, :], ACT.Tanh, scale=0.5).then_inc(thg_ready.sem, 1)
                        if S == EB[e] + 3 + 2 * ft:
                            act.wait_ge(*sec.after(u_full, n))
                            act.wait_ge(*sec.after(hh_ready, n - 2))
                            act.activation(uc_sb[0:fn, n % 2, :], u_ps[0:fn, :], ACT.Copy).then_inc(uc_ready.sem, 1)

            def norm_act(sec, key):
                j = key[1]
                act.wait_ge(*filled(sec, key, "ht"))
                if sec.kind == "body":
                    act.wait_ge(*sec.after(h_ready, j + 1))
                act.activation(hin_sb[:, j, :], sh[:, :], ACT.Copy).then_inc(hin_ready.sem, 1)

            def side_act(sec, q, k, s):
                r = (q + 1) % PH
                l, j, par = r // 2, r % 2, r % 2
                key = ("p", q)
                if s == 7:
                    if l == 0:
                        src = hin_sb[:, j, :]
                        act.wait_ge(*sec.after(hin_ready, j - 2 if sec.kind == "body" and q == 0 else j))
                    else:
                        src = h_sb[:, j, :]
                        act.wait_ge(*sec.after(h_ready, k))
                    act.wait_ge(*sec.after(xn_ready, k - 1))
                    act.activation(norm_t[:, :], src, ACT.Square).then_inc(sq_ready.sem, 1)
                elif s == 9:
                    act.wait_ge(*filled(sec, key, "ms"))
                    act.activation(norm_t[:, :], sh[:, :], ACT.Ln, bias=eps_sb[:, 0:1]).then_inc(log_ready.sem, 1)
                    act.wait_ge(*sec.after(log_ready, k))
                    act.activation(norm_t[:, :], norm_t[:, :], ACT.Exp, scale=-0.5).then_inc(rms_ready.sem, 1)
                elif s in (12, 13):
                    b = s - 12
                    act.wait_ge(*filled(sec, key, f"xp{b}"))
                    act.wait_ge(*sec.after(conv_step, 8 * (k - 1) + 4 * b + 3))
                    act.activation(xpad[:, b, KC - 1:], sh[:, :], ACT.Copy).then_inc(xp_ready.sem, 1)
                elif s in (14, 16):
                    b = (s - 14) // 2
                    act.wait_ge(*filled(sec, key, f"z{b}"))
                    act.wait_ge(*sec.after(zs_ready, 2 * k + b - 1))
                    act.activation(th_z[:, :], sh[:, :], ACT.Tanh, scale=0.5).then_inc(thz_ready.sem, 1)
                if s in (15, 17):
                    b = (s - 15) // 2
                    act.wait_ge(*sec.after(conv_step, 8 * k + 4 * b + 3))
                    act.wait_ge(*sec.after(delta_ready, 2 * (k - 1) + b))
                    act.activation(th_c[:, b, :], conv_sb[:, b, :], ACT.Tanh).then_inc(thc_ready.sem, 1)
                elif s == 19:
                    act.wait_ge(*filled(sec, key, "wx"))
                    if sec.kind == "body":
                        act.wait_ge(*sec.after(c_full, q * NS - 1))
                    act.activation(bc3[0:32, par, :], sh[64:96, :], ACT.Copy).then_inc(bhi_ready.sem, 1)
                    act.wait_ge(*sec.after(sh_full, (JOBS[sec.kind][(key, "wx")])))
                    act.activation(dt_sb[:, :], sh[0:DTR, :], ACT.Copy).then_inc(dt_ready.sem, 1)
                elif s == 20:
                    act.wait_ge(*sec.after(brest_ready, k))
                    act.activation(bc3[32:64, par, :], bc_rest[32:64, :], ACT.Copy).then_inc(bmid_ready.sem, 1)
                elif s in (22, 24):
                    b = (s - 22) // 2
                    act.wait_ge(*sec.after(spm_ready, 2 * k + b))
                    act.activation(sp_l[:, b, :], sp_l[:, b, :], ACT.Exp).then_inc(spe_ready.sem, 1)
                    if b == 1:
                        for b in range(NBLK):
                            act.wait_ge(*sec.after(spe_ready, 2 * k + b))
                            act.activation(sp_l[:, b, :], sp_l[:, b, :], ACT.Ln, bias=1.0).then_inc(spl_ready.sem, 1)

            def copy_b(sec, g):
                act.wait_ge(*sec.after(b_full, g))
                act.activation(b_sb[:, g % 2, :], b_ps[:, :], ACT.Copy).then_inc(b_copied.sem, 1)

            act.wait_ge(w_loaded, 16 * LOADS)
            act.wait_ge(vprep, 10)
            act.activation(a_sb[:, :, :, :], a_sb[:, :, :, :], ACT.Exp).then_inc(aexp, 1)
            act.activation(credit[:, 3:4], eps_sb[:, :], ACT.Copy).then_inc(x1_moved.sem, 1)
            sec = Section("pro")
            for S in (49, 52, 55, 57):
                start_act(sec, "s0", S)
            for u in range(2):
                for S in range(US):
                    unit_act(sec, u, S)
                    start_act(sec, ("st", u), S)
                    if u == 1 and S == LN2[0][0] + 1:
                        norm_act(sec, ("ln", 0))
            norm_act(sec, ("ln", 1))
            for s in range(7, SL):
                side_act(sec, -1, 0, s)
            copy_b(sec, 0)

            with act.Fori(0, PAIRS) as it:
                sec = Section("body", it)
                for q in range(PH):
                    l = q // 2
                    for s in range(SL):
                        n, g, gn = s // 2, q * SL + s, q * NS + s // 2
                        u, S = slot_of(q, s)
                        b = s % 2
                        if s < 2:
                            act.wait_ge(*sec.after(delta_ready, 2 * (q - 1) + b))
                        act.wait_ge(*sec.after(scanned, g - 1))
                        act.activation(dA_ps[:, :], delta_sb[:, q % 2, b, :], ACT.Exp,
                                       scale=a_sb[:, l, b, n:n + 1]).then_inc(dA_ready.sem, 1)
                        if b == 1:
                            act.wait_ge(*sec.after(dbu_ready, 2 * gn - 1))
                            copy_b(sec, gn + 1)
                        side_act(sec, q, q, s)
                        if q == PH - 2 and s == 2:
                            act.wait_ge(*sec.after(xo_ready, 0))
                            act.dma_start(out_rows[(it + PAIRS - 1) & (PAIRS - 1), 0], x2_sb[:, 0]).then_inc(stored.sem, 16)
                        if q in (0, 2) and s == 4:
                            j = 1 - q // 2
                            act.wait_ge(*sec.after(x1_ready, -1 if q == 0 else 0))
                            rows = x_rows[(it + 1 if q == 0 else it + 2) & (PAIRS - 1), j]
                            act.dma_start(xin_sb[:, j], rows).then_inc(x_loaded.sem, 16)
                        if q in (0, 2) and s == 3:
                            j = q // 2
                            act.wait_ge(*sec.after(x2_ready, -1 if j == 0 else 0))
                            act.wait_ge(*sec.after(x1_ready, j - 2))
                            act.activation(x1_sb[:, j], x1_new[:, j], ACT.Copy).then_inc(x1_moved.sem, 1)
                        unit_act(sec, u, S)
                        start_act(sec, ("st", u), S)
                        if u in (1, 2) and S == LN2[0][0] + 1:
                            norm_act(sec, ("ln", u - 1))
                act.wait_ge(*sec.after(xo_ready, 1))
                act.dma_start(out_rows[(it + PAIRS - 1) & (PAIRS - 1), 1], x2_sb[:, 1]).then_inc(stored.sem, 16)
            sec = Section("epi")
            for S in (49, 52, 55, 57):
                start_act(sec, "s2", S)
            for u in (2, 3):
                for S in range(US):
                    unit_act(sec, u, S)
                    if u == 2:
                        start_act(sec, ("st", u), S)

        @block.vector
        def _(dve):
            def norm_dve(sec, key, src, step):
                m = NORM_NO[sec.kind][key]
                if step == 0:
                    for k in range(TB):
                        if k == 0:
                            dve.wait_ge(*sec.after(mv_done, m * TB - 1))
                        dve.bn_stats(bn_sb[:, k, :], src[:, k, :]).then_inc(bn_done.sem, 1)
                    dve.wait_ge(*sec.after(bn_done, m * TB + TB - 1))
                    dve.wait_ge(*sec.after(xtok_ready, m * TB - 1))
                    dve.wait_ge(*sec.after(ve_done, m - 1))
                    dve.memset(carrier[:, :], 0.0)
                    for k in range(TB):
                        dve.bn_aggr(mv_sb[:, k, :], bn_sb[:, k, :]).then_inc(mv_done.sem, 1)
                else:
                    dve.wait_ge(*sec.after(rs_done, m))
                    for k in range(TB):
                        dve.tensor_scalar(xtok[:, k, :], src[:, k, :], mv_sb[:, k, 0:1], rs_sb[:, 1, k:k + 1],
                                          ALU.subtract, ALU.mult).then_inc(xtok_ready.sem, 1)

            def start_dve(sec, key, step):
                a, par = st_no(sec, key), st_par(sec, key)
                src, j = st_src(sec, key)
                R = [a * 17]

                def link(inst):
                    inst.then_inc(rt_step.sem, 1)
                    dve.wait_ge(*sec.after(rt_step, R[0]))
                    R[0] += 1

                if step == 44:
                    if j is None:
                        load_no = {"pro": {0: 0, 1: 1, 2: 2}, "body": {1: 0, 4: 1}}[sec.kind][served(sec, key)]
                        dve.wait_ge(*sec.after(x_loaded, load_no))
                    elif sec.kind == "body":
                        dve.wait_ge(*sec.after(x2_ready, -1 if j == 0 else 0))
                    else:
                        dve.wait_ge(*sec.after(x2_ready, -1 if j == 0 else 0))
                    norm_dve(sec, key, src, 0)
                elif step == 47:
                    norm_dve(sec, key, src, 1)
                elif step == 51:
                    dve.wait_ge(*filled(sec, key, "lg"))
                    dve.tensor_tensor(lg_sb[:, :, :], sh[:, 0:TB * E].rearrange("p (k e) -> p k e", e=E),
                                      bs_sb[:, :].unsqueeze(1).broadcast_to([128, TB, E]), ALU.add).then_inc(lg_ready.sem, 1)
                    dve.wait_ge(*sec.after(lg_ready, a))
                    dve.memset(carrier[:, :], 0.0)
                    for k in range(TB):
                        dve.max(mx_sb[:, k, :], lg_sb[:, k, :]).then_inc(rt_step.sem, 1)
                    R[0] += TB
                    dve.wait_ge(*sec.after(rt_step, R[0] - 1))
                    dve.tensor_tensor(wt_sb[:, 0, :], mx_sb[:, :, 1], mx_sb[:, :, 0], ALU.subtract).then_inc(dd_ready.sem, 1)
                    for k in range(TB):
                        dve.max_index(mi_sb[:, k, :], mx_sb[:, k, :], lg_sb[:, k, :]).then_inc(rt_step.sem, 1)
                    R[0] += TB
                    dve.wait_ge(*sec.after(rt_step, R[0] - 1))
                    link(dve.tensor_copy(mf_sb[:, :, :], mi_sb[:, :, 0:2]))
                elif step == 53:
                    R[0] = a * 17 + 9
                    dve.wait_ge(*sec.after(we_ready, a))
                    link(dve.tensor_scalar(wt_sb[:, 2, :], wt_sb[:, 1, :], 4.0, 4.0, ALU.mult, ALU.add))
                    link(dve.reciprocal(wt_sb[:, 3, :], wt_sb[:, 2, :]))
                    link(dve.tensor_tensor(wt_sb[:, 4, :], wt_sb[:, 1, :], wt_sb[:, 3, :], ALU.mult))
                    iota = iota_e[:, :].unsqueeze(1).broadcast_to([128, TB, E])
                    for i in range(2):
                        at = mf_sb[:, :, i].unsqueeze(2).broadcast_to([128, TB, E])
                        w = wt_sb[:, 3 + i, :].unsqueeze(2).broadcast_to([128, TB, E])
                        link(dve.tensor_tensor(eq_sb[:, i], iota, at, ALU.is_equal))
                        link(dve.tensor_tensor(eq_sb[:, 2 + i], eq_sb[:, i], w, ALU.mult))
                    dve.tensor_tensor(comb_sb[:, :, :], eq_sb[:, 2], eq_sb[:, 3], ALU.add).then_inc(comb_ready.sem, 1)
                    link(dve.memset(eq_sb[:, 0, 0, 0:1], 0.0))
                elif step == 56:
                    dve.wait_ge(*sec.after(chi_ready, a))
                    dve.wait_ge(*sec.after(clo_ready, a - 1))
                    dve.tensor_tensor(c_rest[32:32 + E, :], sh[0:E, :], c3[0:E, par, :], ALU.subtract).then_inc(crest_ready.sem, 1)
                elif step == 58:
                    dve.wait_ge(*sec.after(cmid_ready, a))
                    dve.tensor_tensor(c3[64:64 + E, par, :], c_rest[32:32 + E, :], c3[32:32 + E, par, :],
                                      ALU.subtract).then_inc(clo_ready.sem, 1)

            def unit_dve(sec, u, S):
                un, par = unit_no(sec, u), start_par(sec, u)
                for e in range(E):
                    x_no = un * E + e
                    if S == EB[e] + 1:
                        dve.wait_ge(*filled(sec, ("u", u), f"cbc{e}"))
                        dve.wait_ge(*sec.after(u_full, x_no * 3 - 1))
                        dve.tensor_tensor(xs_sb[:, :], xT_sb[:, par, :], sh[:, :], ALU.mult).then_inc(xs_ready.sem, 1)
                    for ft, (f0, fn) in enumerate(FT):
                        n = x_no * 3 + ft
                        if S == EB[e] + 3 + 2 * ft:
                            dve.wait_ge(*sec.after(thg_ready, n))
                            dve.wait_ge(*sec.after(hh_ready, n - 2))
                            dve.scalar_tensor_tensor(h1_sb[0:fn, n % 2, :], th_g[0:fn, n % 2, :], 1.0, g_ps[0:fn, :],
                                                     ALU.add, ALU.mult).then_inc(h1_ready.sem, 1)
                    if S == (EB[e] + 11 if e < E - 1 else 61):
                        dve.wait_ge(*filled(sec, ("u", u), f"down{e}"))
                        dve.wait_ge(*sec.after(acc_ready, x_no - 1))
                        if e == 0:
                            dve.tensor_copy(acc_sb[:, :], sh[:, :]).then_inc(acc_ready.sem, 1)
                        else:
                            dve.tensor_tensor(acc_sb[:, :], acc_sb[:, :], sh[:, :], ALU.add).then_inc(acc_ready.sem, 1)
                if S == 63:
                    dve.wait_ge(*filled(sec, ("u", u), "yt"))
                    y = sh[:, :].rearrange("p (k d) -> p k d", k=TB)
                    if u < 2:
                        if sec.kind == "body":
                            dve.wait_ge(*sec.after(x1_moved, u))
                        dve.tensor_tensor(x1_new[:, u], xin_sb[:, u], y, ALU.add).then_inc(x1_ready.sem, 1)
                    else:
                        dve.tensor_tensor(x2_sb[:, u - 2], x2_sb[:, u - 2], y, ALU.add).then_inc(xo_ready.sem, 1)

            def ln2_dve(sec, j, step):
                if step == 0:
                    dve.wait_ge(*sec.after(x1_ready, j))
                norm_dve(sec, ("ln", j), x1_new[:, j], step)

            def side_dve(sec, q, k, s):
                r = (q + 1) % PH
                l, j, par = r // 2, r % 2, r % 2
                p = (q - 1) % PH
                pl, pj, ppar = p // 2, p % 2, p % 2
                key = ("p", q)
                has_post = sec.kind != "pro"
                if has_post and s < 2:
                    dve.wait_ge(*sec.after(summed, (q * SL if sec.kind == "body" else 0) - 2 + s))
                    dve.wait_ge(*sec.after(h_ready, k - 1))
                    dve.scalar_tensor_tensor(y_sb[:, s, :], xc_sb[:, ppar, s, :], dp_sb[:, pl, s:s + 1],
                                             y_ps[s][:, :], ALU.mult, ALU.add).then_inc(y_taken.sem, 1)
                elif has_post and s == 6:
                    dve.wait_ge(*filled(sec, key, "wblk"))
                    if pl == 0:
                        src = hin_sb[:, pj, :]
                        dve.wait_ge(*sec.after(x2_ready, -1 if pj == 0 else 0))
                    else:
                        src = h_sb[:, pj, :]
                    dve.wait_ge(*sec.after(h_ready, k - 1))
                    dve.tensor_tensor(h_sb[:, pj, :], src, sh[:, :], ALU.add).then_inc(h_ready.sem, 1)
                elif s == 11 and q in (0, PH - 1):
                    dve.wait_ge(*filled(sec, key, "attn"))
                    if sec.kind == "body":
                        dve.wait_ge(*sec.after(x1_moved, -1 if q == 0 else 0))
                    dve.wait_ge(*sec.after(stored, -1 if q == 0 else 0))
                    dve.tensor_tensor(x2_sb[:, pj], x1_sb[:, pj], sh[:, :].rearrange("p (k d) -> p k d", k=TB),
                                      ALU.add).then_inc(x2_ready.sem, 1)
                if sec.kind == "epi":
                    return
                if s == 10:
                    dve.wait_ge(*sec.after(rms_ready, k))
                    if l == 0:
                        dve.wait_ge(*sec.after(hin_ready, j - 2 if sec.kind == "body" and q == 0 else j))
                        src = hin_sb[:, j, :]
                    else:
                        dve.wait_ge(*sec.after(h_ready, k))
                        src = h_sb[:, j, :]
                    dve.scalar_tensor_tensor(xn_sb[:, :], src, normw_sb[:, l:l + 1], norm_t[:, :],
                                             ALU.mult, ALU.mult).then_inc(xn_ready.sem, 1)
                for b in range(NBLK):
                    if s in (13 + 2 * b, 14 + 2 * b):
                        for t in ((0, 1) if s == 13 + 2 * b else (2, 3)):
                            if t == 0:
                                dve.wait_ge(*sec.after(xp_ready, 2 * k + b))
                                dve.wait_ge(*sec.after(delta_ready, 2 * (k - 1) + b))
                                c = dve.tensor_scalar(conv_sb[:, b, :], xpad[:, b, 0:T], cw_sb[:, l, b, 0:1],
                                                      cb_sb[:, l, b:b + 1], ALU.mult, ALU.add)
                            else:
                                dve.wait_ge(*sec.after(conv_step, 8 * k + 4 * b + t - 1))
                                c = dve.scalar_tensor_tensor(conv_sb[:, b, :], xpad[:, b, t:t + T], cw_sb[:, l, b, t:t + 1],
                                                             conv_sb[:, b, :], ALU.mult, ALU.add)
                            c.then_inc(conv_step.sem, 1)
                    if s == 16 + 2 * b - (1 if b else 0) * 0:
                        dve.wait_ge(*sec.after(thc_ready, 2 * k + b))
                        if has_post:
                            dve.wait_ge(*sec.after(y_taken, 2 * k + b))
                        dve.scalar_tensor_tensor(xc_sb[:, par, b, :], th_c[:, b, :], 1.0, conv_sb[:, b, :],
                                                 ALU.add, ALU.mult).then_inc(xc_ready.sem, 1)
                    if s == 14 + 2 * b:
                        dve.wait_ge(*sec.after(thz_ready, 2 * k + b))
                        dve.scalar_tensor_tensor(zs_sb[:, par, b, :], th_z[:, :], 1.0, sh[:, :],
                                                 ALU.add, ALU.mult).then_inc(zs_ready.sem, 1)
                    if s == 21 + 2 * b:
                        dve.wait_ge(*filled(sec, key, f"dt{b}"))
                        dve.wait_ge(*sec.after(xc_ready, 2 * k + b))
                        dve.tensor_scalar(sp_x[:, b, :], sh[:, :], bdt_sb[:, l, b:b + 1], None, ALU.add).then_inc(spx_ready.sem, 1)
                        dve.wait_ge(*sec.after(spx_ready, 2 * k + b))
                        dve.tensor_scalar(sp_l[:, b, :], sp_x[:, b, :], SPLUS, None, ALU.min).then_inc(spm_ready.sem, 1)
                    if s == 25 + b:
                        dve.wait_ge(*sec.after(spl_ready, 2 * k + b))
                        dve.tensor_tensor(delta_sb[:, par, b, :], sp_x[:, b, :], sp_l[:, b, :], ALU.max).then_inc(delta_ready.sem, 1)
                if s == 19:
                    dve.wait_ge(*sec.after(bhi_ready, k))
                    dve.wait_ge(*sec.after(dt_ready, k))
                    dve.wait_ge(*sec.after(blo_ready, k - 1))
                    dve.tensor_tensor(bc_rest[32:64, :], sh[64:96, :], bc3[0:32, par, :], ALU.subtract).then_inc(brest_ready.sem, 1)
                if s == 22:
                    dve.wait_ge(*sec.after(bmid_ready, k))
                    dve.tensor_tensor(bc3[64:96, par, :], bc_rest[32:64, :], bc3[32:64, par, :], ALU.subtract).then_inc(blo_ready.sem, 1)

            def read_out(sec, g):
                dve.wait_ge(*sec.after(scanned, g))
                dve.wait_ge(*sec.after(c_full, g // 2))
                dve.wait_ge(*sec.after(summed, g - 3))
                dve.tensor_tensor(prod_sb[:, g % 3, :], st_sb[:, g % 2, :], c_ps[:, :], ALU.mult).then_inc(prod_ready.sem, 1)

            dve.memset(mean_w[:, :], 1.0 / D).then_inc(vprep, 1)
            dve.memset(ones_row[:, :], 1.0).then_inc(vprep, 1)
            for e in range(E):
                last = dve.memset(iota_e[:, e:e + 1], float(e))
            last.then_inc(vprep, 1)
            dve.memset(x2_sb[:, :, :, :], 0.0).then_inc(vprep, 1)
            dve.memset(x1_sb[:, :, :, :], 0.0).then_inc(vprep, 1)
            dve.memset(xpad[:, :, :], 0.0).then_inc(vprep, 1)
            dve.memset(xc_sb[:, :, :, :], 0.0).then_inc(vprep, 1)
            dve.memset(zs_sb[:, :, :, :], 0.0).then_inc(vprep, 1)
            dve.memset(c3[:, :, :], 0.0).then_inc(vprep, 1)
            dve.memset(eps_sb[:, :], EPS).then_inc(vprep, 1)
            dve.memset(st_sb[:, :, :], 0.0).then_inc(scanned.sem, 4)
            dve.memset(prod_sb[:, :, :], 0.0).then_inc(prod_ready.sem, 2)
            dve.memset(h_sb[:, :, :], 0.0).then_inc(h_ready.sem, 1)
            dve.wait_ge(vprep, 10)
            dve.memset(credit[:, 0:1], 0.0).then_inc(x2_ready.sem, 1)
            dve.memset(credit[:, 1:2], 0.0).then_inc(xo_ready.sem, 1)
            dve.memset(credit[:, 2:3], 0.0).then_inc(stored.sem, 16)
            dve.wait_ge(w_loaded, 16 * LOADS)
            dve.wait_ge(aexp, 1)
            dve.tensor_scalar(a_sb[:, :, :, :], a_sb[:, :, :, :], -1.0, None, ALU.mult).then_inc(vprep, 1)
            dve.tensor_scalar(cw_sb[:, :, :, :], cw_sb[:, :, :, :], 0.5, None, ALU.mult).then_inc(vprep, 1)
            dve.tensor_scalar(cb_sb[:, :, :], cb_sb[:, :, :], 0.5, None, ALU.mult).then_inc(vprep, 1)
            dve.tensor_scalar(wblk_sb[:, :, :, :], wblk_sb[:, :, :, :], 0.5, None, ALU.mult).then_inc(vprep, 1)
            dve.wait_ge(vprep, 14)
            sec = Section("pro")
            for S in (44, 47, 51, 53, 56, 58):
                start_dve(sec, "s0", S)
            for u in range(2):
                for S in range(US):
                    unit_dve(sec, u, S)
                    start_dve(sec, ("st", u), S)
                    if u == 1 and S in (0, 3):
                        ln2_dve(sec, 0, S)
            ln2_dve(sec, 1, 0)
            ln2_dve(sec, 1, 3)
            for s in range(10, SL):
                side_dve(sec, -1, 0, s)

            with dve.Fori(0, PAIRS) as it:
                sec = Section("body", it)
                for q in range(PH):
                    for s in range(SL):
                        g = q * SL + s
                        u, S = slot_of(q, s)
                        dve.wait_ge(*sec.after(dA_ready, g))
                        dve.wait_ge(*sec.after(dbu_ready, g))
                        dve.wait_ge(*sec.after(prod_ready, g - 2))
                        dve.tensor_tensor_scan(st_sb[:, g % 2, :], dA_ps[:, :], dbu_sb[:, g % 4, :], 0.0,
                                               ALU.mult, ALU.add).then_inc(scanned.sem, 1)
                        if g > 0:
                            read_out(sec, g - 1)
                        if g == SG - 1:
                            read_out(sec, g)
                        side_dve(sec, q, q, s)
                        unit_dve(sec, u, S)
                        start_dve(sec, ("st", u), S)
                        if u in (1, 2) and S in (0, 3):
                            ln2_dve(sec, u - 1, S)
            sec = Section("epi")
            for s in (0, 1, 6, 11):
                side_dve(sec, 0, 0, s)
            for S in (44, 47, 51, 53, 56, 58):
                start_dve(sec, "s2", S)
            for u in (2, 3):
                for S in range(US):
                    unit_dve(sec, u, S)
                    if u == 2:
                        start_dve(sec, ("st", u), S)

        @block.gpsimd
        def _(pool):
            def norm_pool(sec, key):
                m = NORM_NO[sec.kind][key]
                pool.wait_ge(*sec.after(mv_done, m * TB + TB - 1))
                pool.wait_ge(*sec.after(rs_done, m - 1))
                pool.tensor_tensor(rs_sb[:, 0, :], mv_sb[:, :, 1], eps4[:, :], ALU.add).then_inc(ve_done.sem, 1)
                pool.wait_ge(*sec.after(ve_done, m))
                pool.wait_ge(*sec.after(xtok_ready, m * TB - 1))
                pool.tensor_tensor(rs_sb[:, 1, :], rs_sb[:, 0, :], neg_half[:, :], ALU.pow).then_inc(rs_done.sem, 1)

            def unit_pool(sec, u, S):
                un = unit_no(sec, u)
                for e in range(E):
                    for ft, (f0, fn) in enumerate(FT):
                        n = (un * E + e) * 3 + ft
                        if S == EB[e] + 4 + 2 * ft:
                            pool.wait_ge(*sec.after(h1_ready, n))
                            pool.wait_ge(*sec.after(uc_ready, n))
                            pool.wait_ge(*sec.after(acc_ready, un * E + e - 2))
                            pool.tensor_tensor(hh_sb[0:fn, (e % 2) * 3 + ft, :], h1_sb[0:fn, n % 2, :],
                                               uc_sb[0:fn, n % 2, :], ALU.mult).then_inc(hh_ready.sem, 1)

            def side_pool(sec, q, k, s):
                par = (q + 1) % 2
                ppar = (q - 1) % 2
                if sec.kind != "pro" and s in (1, 2):
                    b = s - 1
                    pool.wait_ge(*sec.after(y_taken, 2 * k + b))
                    pool.tensor_tensor(y_sb[:, b, :], y_sb[:, b, :], zs_sb[:, ppar, b, :], ALU.mult).then_inc(y_gated.sem, 1)
                if sec.kind != "epi" and s in (26, 27):
                    b = s - 26
                    pool.wait_ge(*sec.after(delta_ready, 2 * k + b))
                    if sec.kind == "body":
                        pool.wait_ge(*sec.after(dbu_ready, q * SL - 1))
                    pool.tensor_tensor(du_sb[:, par, b, :], delta_sb[:, par, b, :], xc_sb[:, par, b, :],
                                       ALU.mult).then_inc(du_ready.sem, 1)

            pool.memset(eps4[:, :], EPS).then_inc(consts, 1)
            pool.memset(dbu_sb[:, :, :], 0.0).then_inc(dbu_ready.sem, 1)
            pool.memset(ident[:, :], 0.0).then_inc(cprep, 1)
            pool.memset(sel_bc[:, :, :], 0.0).then_inc(cprep, 1)
            pool.memset(sel_e[:, :, :], 0.0).then_inc(cprep, 1)
            pool.wait_ge(cprep, 3)
            pool.affine_select(out=ident[:, :], in_=ident[:, :], compare_op=ALU.not_equal, fill=1.0, base=0,
                               pattern=[[-1, 128]], channel_multiplier=1).then_inc(consts, 1)
            for a in range(3):
                pool.affine_select(out=sel_bc[:, :, :], in_=sel_bc[:, :, :], compare_op=ALU.not_equal, fill=1.0,
                                   base=-32 * a, pattern=[[-1, 2 * NS], [0, 128]], channel_multiplier=1).then_inc(cprep, 1)
                pool.affine_select(out=sel_e[:, :, :], in_=sel_e[:, :, :], compare_op=ALU.not_equal, fill=1.0,
                                   base=-32 * a, pattern=[[-1, E], [0, 128]], channel_multiplier=1).then_inc(cprep, 1)
                pool.wait_ge(cprep, 5 + 2 * a)
            pool.memset(neg_half[:, :], -0.5).then_inc(consts, 3)
            sec = Section("pro")
            norm_pool(sec, "s0")
            for u in range(2):
                for S in range(US):
                    unit_pool(sec, u, S)
                    if S == 45:
                        norm_pool(sec, ("st", u))
                    if u == 1 and S == 1:
                        norm_pool(sec, ("ln", 0))
            norm_pool(sec, ("ln", 1))
            for s in (26, 27):
                side_pool(sec, -1, 0, s)

            with pool.Fori(0, PAIRS) as it:
                sec = Section("body", it)
                for q in range(PH):
                    for s in range(SL):
                        g, gn, b = q * SL + s, q * NS + s // 2, s % 2
                        u, S = slot_of(q, s)
                        if s < 2:
                            pool.wait_ge(*sec.after(du_ready, 2 * (q - 1) + b))
                        pool.wait_ge(*sec.after(b_copied, gn))
                        pool.wait_ge(*sec.after(scanned, g - 4))
                        pool.tensor_tensor(dbu_sb[:, g % 4, :], du_sb[:, q % 2, b, :], b_sb[:, gn % 2, :],
                                           ALU.mult).then_inc(dbu_ready.sem, 1)
                        side_pool(sec, q, q, s)
                        unit_pool(sec, u, S)
                        if S == 45:
                            norm_pool(sec, ("st", u))
                        if u in (1, 2) and S == 1:
                            norm_pool(sec, ("ln", u - 1))
            sec = Section("epi")
            for s in (1, 2):
                side_pool(sec, 0, 0, s)
            norm_pool(sec, "s2")
            for u in (2, 3):
                for S in range(US):
                    unit_pool(sec, u, S)
                    if u == 2 and S == 45:
                        norm_pool(sec, ("st", u))


def laid_out(name, a):
    name = name.split("_", 2)[2]
    if name in ("Win", "Wdt", "Wg", "Wu", "Wd"):
        return a.transpose(1, 0, 2)
    if name in ("Wx", "Wblk", "conv_w", "A_log"):
        return a.reshape(NL, NBLK, 128, -1).transpose(2, 0, 1, 3)
    if name in ("conv_b", "bdt", "Dp"):
        return a.reshape(NL, NBLK, 128).transpose(2, 0, 1)
    if name == "norm_w":
        return a.T
    if name in ("bout", "bs"):
        return a.reshape(1, -1)
    return a


_ARGS = ["L0_attn_x", "L0_attn_norm_w", "L0_attn_Win", "L0_attn_conv_w", "L0_attn_conv_b", "L0_attn_Wx",
         "L0_attn_Wdt", "L0_attn_bdt", "L0_attn_A_log", "L0_attn_Dp", "L0_attn_Wblk", "L0_attn_Wout",
         "L0_attn_bout", "L0_ffn_Ws", "L0_ffn_bs", "L0_ffn_Wg", "L0_ffn_Wu", "L0_ffn_Wd"]


def kernel(**inputs):
    import numpy as np
    import concourse.bacc as bacc
    from concourse.bass_utils import run_bass_kernel_spmd

    nc = bacc.Bacc("TRN2", target_bir_lowering=False, num_devices=1)
    arrays, args = {}, []
    for name in _ARGS:
        a = np.ascontiguousarray(laid_out(name, np.asarray(inputs[name])))
        arrays[f"in_{name}"] = a
        args.append(nc.dram_tensor(f"in_{name}", a.shape, F32, kind="ExternalInput").ap())
    args.append(nc.dram_tensor("out_0", (B, T, D), F32, kind="ExternalOutput").ap())
    build(nc, *args)
    r = run_bass_kernel_spmd(nc, [arrays], core_ids=[0])
    return r.results[0]["out_0"]
```

```python
from contextlib import ExitStack

import concourse.bass as bass
from concourse import mybir

F32 = mybir.dt.float32
BF16 = mybir.dt.bfloat16
U32 = mybir.dt.uint32
ALU = mybir.AluOpType
ACT = mybir.ActivationFunctionType

B, T, D = 16, 512, 128
NL, NS, KC, DTR = 4, 16, 4, 64
NBLK = 2
TB = T // 128
E, F = 8, 344
FT = [(0, 128), (128, 128), (256, 88)]
EPS = 1e-5
PAIRS = B // 2
PH = 2 * NL
SL = 2 * NS
US = 2 * SL
SPLUS = 40.0

SIDE = [
    (6, "wblk", 8), (9, "attn", 11), (10, "ms", 12), (13, "xp0", 15), (14, "xp1", 16), (16, "z0", 18), (18, "z1", 20), (20, "wx", 23),
    (24, "dt0", 25), (25, "dt1", 27),
]
EB = [1 + 7 * e for e in range(E)]
DOWN = [12, 19, 26, 33, 40, 47, 56, 60]
UNIT = [(DOWN[e], f"down{e}", DOWN[e] + 2) for e in range(E)] + [(62, "yt", 63)]
START = [(44, "xt", 46), (49, "lg", 51), (53, "ct", 55)]
LN2 = [(4, "ht", 6)]
LAG = 3
LEAD = 2
NPROD, NDBU, NB = 4, 4, 4
NGATE = 2
GATE = [57] + [EB[e] - 6 for e in range(1, E)]


class Signal:

    def __init__(self, sem, credit, pro, trip, step=1):
        self.sem, self.credit, self.pro, self.trip, self.step = sem, credit, pro, trip, step


class Section:
    def __init__(self, kind, it=None):
        self.kind, self.it = kind, it

    def v(self, s, n):
        if self.kind == "pro":
            return (s.credit + n + 1) * s.step
        before = s.credit + s.pro
        if self.kind == "epi":
            return (before + PAIRS * s.trip + n + 1) * s.step
        assert before + n + 1 >= 1, (s.sem, n)
        return self.it * (s.trip * s.step) + (before + n + 1) * s.step

    def after(self, s, n):
        val = self.v(s, n)
        return s.sem, (max(val, 0) if isinstance(val, int) else val)


def shared_bank_order():
    order = {}
    jobs = []
    for name in ("xt", "lg", "ct"):
        jobs.append(("s0", name))
    for u in range(2):
        for s in range(US):
            jobs += [(("u", u), n) for t, n, _ in UNIT if t == s]
            jobs += [(("st", u), n) for t, n, _ in START if t == s]
            if u == 1:
                jobs += [(("ln", 0), n) for t, n, _ in LN2 if t == s]
    jobs.append((("ln", 1), "ht"))
    jobs += [(("p", -1), n) for _, n, _ in SIDE if n not in ("wblk", "attn")]
    order["pro"] = {j: i for i, j in enumerate(jobs)}
    jobs = []
    last = -9, 0
    for q in range(PH):
        for s in range(SL):
            u, S = q // 2, (q % 2) * SL + s
            here = [(("p", q), n, c) for t, n, c in SIDE if t == s and (n != "attn" or q in (0, PH - 1))]
            here += [(("u", u), n, c - S + s) for t, n, c in UNIT if t == S]
            here += [(("st", u), n, c - S + s) for t, n, c in START if t == S]
            if u in (1, 2):
                here += [(("ln", u - 1), n, c - S + s) for t, n, c in LN2 if t == S]
            for k, n, c in here:
                rank = ("p", "u", "st", "ln").index(k[0])
                assert last[0] <= q * SL + s + 2 and last < (q * SL + c, rank), ("the bank is read too late", k, n, last, q * SL + s)
                last = q * SL + c, rank
                jobs.append((k, n))
    order["body"] = {j: i for i, j in enumerate(jobs)}
    jobs = [(("p", 0), "wblk"), (("p", 0), "attn")]
    jobs += [("s2", n) for n in ("xt", "lg", "ct")]
    for u in (2, 3):
        for s in range(US):
            jobs += [(("u", u), n) for t, n, _ in UNIT if t == s]
            if u == 2:
                jobs += [(("st", u), n) for t, n, _ in START if t == s]
    order["epi"] = {j: i for i, j in enumerate(jobs)}
    return order


def build(nc, x, norm_w, Win, conv_w, conv_b, Wx, Wdt, bdt, A_log, Dp, Wblk, Wout, bout,
          Ws, bs, Wg, Wu, Wd, out):
    JOBS = shared_bank_order()
    with ExitStack() as ctx:
        def sb(name, shape, dt=F32):
            return ctx.enter_context(nc.sbuf_tensor(name, shape, dt))

        def bank(name):
            return ctx.enter_context(nc.psum_tensor(name, [128, T], F32))

        wg_sb = sb("wg_sb", [128, E, F])
        wu_sb = sb("wu_sb", [128, E, F])
        wd_sb = sb("wd_sb", [128, E, len(FT), D])
        win_sb = sb("win_sb", [128, NL, 4 * 128])
        wx_sb = sb("wx_sb", [128, NL, NBLK, DTR + 2 * NS])
        wdt_sb = sb("wdt_sb", [DTR, NL, NBLK * 128])
        wblk_sb = sb("wblk_sb", [128, NL, NBLK, D])
        wout_sb = sb("wout_sb", [128, D])
        bout_sb = sb("bout_sb", [1, D])
        ws_sb = sb("ws_sb", [128, E])
        bs_sb = sb("bs_sb", [128, E])
        normw_sb = sb("normw_sb", [128, NL])
        cw_sb = sb("cw_sb", [128, NL, NBLK, KC])
        cb_sb = sb("cb_sb", [128, NL, NBLK])
        bdt_sb = sb("bdt_sb", [128, NL, NBLK])
        a_sb = sb("a_sb", [128, NL, NBLK, NS])
        dp_sb = sb("dp_sb", [128, NL, NBLK])
        ident = sb("ident", [128, 128])
        mean_w = sb("mean_w", [128, 128])
        ones_row = sb("ones_row", [1, 128])
        sel_c = sb("sel_c", [96, NS, 128], BF16)
        iota_e = sb("iota_e", [128, E])
        neg_half = sb("neg_half", [128, TB])
        eps_sb = sb("eps_sb", [128, 1])
        eps4 = sb("eps4", [128, TB])
        credit = sb("credit", [128, 4])
        carrier = sb("carrier", [128, 1])
        b_sb = sb("b_sb", [128, NB, T])
        dbu_sb = sb("dbu_sb", [128, NDBU, T])
        st_sb = sb("st_sb", [128, 2, T])
        prod_sb = sb("prod_sb", [128, NPROD, T])
        delta_sb = sb("delta_sb", [128, 2, NBLK, T])
        du_sb = sb("du_sb", [128, 2, NBLK, T])
        xc_sb = sb("xc_sb", [128, 2, NBLK, T])
        zs_sb = sb("zs_sb", [128, 2, NBLK, T])
        cs3 = sb("cs3", [96, 2, T], BF16)
        y_sb = sb("y_sb", [128, NBLK, T])
        h_sb = sb("h_sb", [128, 2, T])
        hin_sb = sb("hin_sb", [128, 2, T])
        norm_t, xn_sb = y_sb[:, 0, :], y_sb[:, 1, :]
        xpad = sb("xpad", [128, NBLK, KC - 1 + T])
        conv_sb = sb("conv_sb", [128, NBLK, T])
        th_c = sb("th_c", [128, NBLK, T])
        th_z = sb("th_z", [128, T])
        dbc_sb = sb("dbc_sb", [DTR + 2 * NS, 2, T])
        rest_sb = sb("rest_sb", [NS, T])
        sp_x, sp_l = conv_sb, th_c
        xin_sb = sb("xin_sb", [128, 2, TB, D])
        x1_new = sb("x1_new", [128, 2, TB, D])
        x1_sb = sb("x1_sb", [128, 2, TB, D])
        x2_sb = sb("x2_sb", [128, 2, TB, D])
        xtok = sb("xtok", [128, TB, D])
        bn_sb = sb("bn_sb", [128, TB, 6])
        mv_sb = sb("mv_sb", [128, TB, 2])
        rs_sb = sb("rs_sb", [128, 2, TB])
        xT_sb = sb("xT_sb", [128, 2, T])
        xs_sb = sb("xs_sb", [128, T])
        acc_sb = sb("acc_sb", [128, T])
        th_g = sb("th_g", [128, 2, T])
        h1_sb = th_g
        uc_sb = sb("uc_sb", [128, 2, T])
        hh_sb = sb("hh_sb", [128, 6, T])
        lg_sb = sb("lg_sb", [128, TB, E])
        mx_sb = sb("mx_sb", [128, TB, E])
        mi_sb = sb("mi_sb", [128, TB, E], U32)
        mf_sb = sb("mf_sb", [128, TB, 2])
        wt_sb = sb("wt_sb", [128, 5, TB])
        eq_sb = sb("eq_sb", [128, 4, TB, E])
        comb_sb = sb("comb_sb", [128, TB, E])
        gates_sb = sb("gates_sb", [E, T])
        gate_sb = sb("gate_sb", [128, NGATE, T])
        dA_ps, c_ps = bank("dA_ps"), [bank("c0_ps"), bank("c1_ps")]
        y_ps = [bank("y0_ps"), bank("y1_ps")]
        g_ps, u_ps, sh = bank("g_ps"), bank("u_ps"), bank("sh")

        def signal(name, credit=0, pro=0, trip=0, step=1):
            return Signal(ctx.enter_context(nc.semaphore(name)), credit, pro, trip, step)

        NG, SG = PH * NS, PH * SL
        b_spread = [signal(f"b_spread{i}", 0, 0, NG // NB, 16) for i in range(NB)]
        c_full = signal("c_full", 0, 0, NG)
        dA_ready = signal("dA_ready", 0, 0, SG)
        dbu_ready = signal("dbu_ready", 1, 0, SG)
        scanned = signal("scanned", 4, 0, SG)
        prod_ready = signal("prod_ready", 2, 0, SG)
        summed = signal("summed", NPROD, 0, SG)
        y_taken, y_gated = signal("y_taken", 0, 0, 2 * PH), signal("y_gated", 0, 0, 2 * PH)
        h_ready = signal("h_ready", 1, 0, PH)
        x2_ready = signal("x2_ready", 1, 0, 2)
        x1_moved = signal("x1_moved", 1, 0, 2)
        sq_ready, log_ready, rms_ready, xn_ready = (signal(n, 0, 1, PH) for n in ("sq_ready", "log_ready", "rms_ready", "xn_ready"))
        xp_ready, thc_ready, xc_ready, thz_ready, zs_ready = (
            signal(n, 0, 2, 2 * PH) for n in ("xp_ready", "thc_ready", "xc_ready", "thz_ready", "zs_ready"))
        conv_step = signal("conv_step", 0, 8, 8 * PH)
        dt_ready, bhi_ready, brest_ready, bmid_ready, blo_ready = (
            signal(n, 0, 1, PH) for n in ("dt_ready", "bhi_ready", "brest_ready", "bmid_ready", "blo_ready"))
        spx_ready, spm_ready, spe_ready, spl_ready, delta_ready, du_ready = (
            signal(n, 0, 2, 2 * PH) for n in ("spx_ready", "spm_ready", "spe_ready", "spl_ready", "delta_ready", "du_ready"))
        bn_done, mv_done, xtok_ready = (signal(n, 0, 5 * TB, 6 * TB) for n in ("bn_done", "mv_done", "xtok_ready"))
        ve_done, rs_done = signal("ve_done", 0, 5, 6), signal("rs_done", 0, 5, 6)
        xT_ready, lg_ready, dd_ready, we_ready, comb_ready, gates_ready = (
            signal(n, 0, 3, 4) for n in ("xT_ready", "lg_ready", "dd_ready", "we_ready", "comb_ready", "gates_ready"))
        gate_spread = [signal(f"gate_spread{i}", 0, 2 * E // NGATE + (i == 0), 4 * E // NGATE, 16) for i in range(NGATE)]
        rt_step = signal("rt_step", 0, 3 * 17, 4 * 17)
        xs_ready, acc_ready = signal("xs_ready", 0, 2 * E, 4 * E), signal("acc_ready", 0, 2 * E, 4 * E)
        g_full, u_full, thg_ready, h1_ready, uc_ready, hh_ready = (
            signal(n, 0, 6 * E, 12 * E) for n in ("g_full", "u_full", "thg_ready", "h1_ready", "uc_ready", "hh_ready"))
        x1_ready, hin_ready = signal("x1_ready", 0, 2, 2), signal("hin_ready", 0, 2, 2)
        xo_ready = signal("xo_ready", 1, 0, 2)
        x_loaded = signal("x_loaded", 0, 3, 2, 16)
        stored = signal("stored", 1, 0, 2, 16)
        sh_full = signal("sh_full", 0, len(JOBS["pro"]), len(JOBS["body"]))
        w_loaded = ctx.enter_context(nc.semaphore("w_loaded"))
        consts = ctx.enter_context(nc.semaphore("consts"))
        vprep = ctx.enter_context(nc.semaphore("vprep"))
        aexp = ctx.enter_context(nc.semaphore("aexp"))
        cprep = ctx.enter_context(nc.semaphore("cprep"))

        LOADS = 19

        def filled(sec, key, name):
            return sec.after(sh_full, JOBS[sec.kind][(key, name)])

        def gate_on_chip(sec, x_no):
            return sec.after(gate_spread[x_no % NGATE], x_no // NGATE - (sec.kind == "body" and x_no % NGATE == 0))

        def ups_before(u, S):
            return u * 3 * E + sum(EB[e] + 2 + 2 * ft < S for e in range(E) for ft in range(3))

        def slot_of(q, s):
            return q // 2, (q % 2) * SL + s

        x_rows = x.rearrange("(p j) (k t) d -> p j t k d", j=2, t=128)
        out_rows = out.rearrange("(p j) (k t) d -> p j t k d", j=2, t=128)

        def unit_no(sec, u):
            return u - 2 if sec.kind == "epi" else u

        def start_no(sec, u):
            if sec.kind == "pro":
                return u
            if sec.kind == "body":
                return u - 1
            return u - 2

        def start_par(sec, u):
            return (u + 1) % 2 if sec.kind == "epi" else u % 2

        NORM_NO = {"pro": {"s0": 0, ("st", 0): 1, ("ln", 0): 2, ("st", 1): 3, ("ln", 1): 4},
                   "body": {("st", 0): 0, ("ln", 0): 1, ("st", 1): 2, ("ln", 1): 3, ("st", 2): 4, ("st", 3): 5},
                   "epi": {"s2": 0, ("st", 2): 1}}

        def served(sec, key):
            if key == "s0":
                return 0
            if key == "s2":
                return 2
            if sec.kind == "pro" and key[1] == 1:
                return 2
            return key[1] + 1

        def st_no(sec, key):
            if sec.kind == "pro":
                return served(sec, key)
            if sec.kind == "body":
                return key[1]
            return 0 if key == "s2" else 1

        def st_par(sec, key):
            if sec.kind == "pro":
                return st_no(sec, key) % 2
            if sec.kind == "body":
                return (key[1] + 1) % 2
            return (st_no(sec, key) + 1) % 2

        def st_src(sec, key):
            u = served(sec, key) % 4 if sec.kind != "pro" else served(sec, key) % 2
            return (xin_sb[:, u], None) if u < 2 else (x2_sb[:, u - 2], u - 2)

        block = ctx.enter_context(nc.Block())

        @block.sync
        def _(sp):
            sp.dma_start(xin_sb[:, 0], x_rows[0, 0]).then_inc(x_loaded.sem, 16)
            sp.dma_start(xin_sb[:, 1], x_rows[0, 1]).then_inc(x_loaded.sem, 16)
            for dst, src in (
                (ws_sb[:, :], Ws), (bs_sb[:, :], bs.broadcast_to([128, E])),
                (wg_sb[:, :, :], Wg), (wu_sb[:, :, :], Wu),
                (wd_sb[:, :, 0, :], Wd[0:128]), (wd_sb[:, :, 1, :], Wd[128:256]), (wd_sb[0:88, :, 2, :], Wd[256:344]),
                (win_sb[:, :, :], Win), (wx_sb[:, :, :, :], Wx), (wdt_sb[:, :, :], Wdt),
                (wblk_sb[:, :, :, :], Wblk), (wout_sb[:, :], Wout), (bout_sb[:, :], bout),
                (normw_sb[:, :], norm_w), (cw_sb[:, :, :, :], conv_w), (cb_sb[:, :, :], conv_b),
                (bdt_sb[:, :, :], bdt), (a_sb[:, :, :, :], A_log), (dp_sb[:, :, :], Dp),
            ):
                sp.dma_start(dst, src).then_inc(w_loaded, 16)
            pro = Section("pro")

            def spread_b(sec, g, par):
                n = g % NS
                sp.dma_start(b_sb[:, g % NB, :], dbc_sb[DTR + NS + n:DTR + NS + n + 1, par, :].unsqueeze(1).broadcast_to([1, 128, T])
                             ).then_inc(b_spread[g % NB].sem, 16)

            def spread_gate(sec, e, x_no):
                if e == 0:
                    start = x_no // E - (sec.kind == "body")
                    sp.wait_ge(*sec.after(gates_ready, start))
                else:
                    sp.wait_ge(*sec.after(xs_ready, x_no - NGATE))
                sp.dma_start(gate_sb[:, e % NGATE, :], gates_sb[e:e + 1, :].unsqueeze(1).broadcast_to([1, 128, T])
                             ).then_inc(gate_spread[e % NGATE].sem, 16)

            for x_no in range(2 * E + 1):
                if x_no == E + 2:
                    sp.wait_ge(*pro.after(x1_ready, 0))
                    sp.dma_start(xin_sb[:, 0], x_rows[1, 0]).then_inc(x_loaded.sem, 16)
                spread_gate(pro, x_no % E, x_no)
            for n in range(NB):
                if n == 0:
                    sp.wait_ge(*pro.after(dt_ready, 0))
                spread_b(pro, n, 0)
            with sp.Fori(0, PAIRS) as it:
                sec = Section("body", it)
                for q in range(PH):
                    for n in range(NS):
                        g = q * NS + n
                        u, S = slot_of(q, 2 * n)
                        for e in range(E):
                            if GATE[e] // 2 == S // 2:
                                spread_gate(sec, e, (u + (e == 0)) * E + e)
                        if n == NS - NB:
                            sp.wait_ge(*sec.after(scanned, 2 * g + 1))
                        else:
                            sp.wait_ge(*sec.after(dbu_ready, 2 * g + 1))
                        spread_b(sec, g + NB, (q + (n >= NS - NB)) % 2)
            sec = Section("epi")
            for x_no in range(2 * E):
                spread_gate(sec, x_no % E, x_no)
            for j in range(2):
                sp.wait_ge(*sec.after(xo_ready, j))
                sp.dma_start(out_rows[PAIRS - 1, j], x2_sb[:, j]).then_inc(stored.sem, 16)
            sp.wait_ge(*sec.after(stored, 1))
            sp.wait_ge(*sec.after(x_loaded, -1))
            for i in range(NGATE):
                sp.wait_ge(*sec.after(gate_spread[i], 2 * E // NGATE - 1))
            for i in range(NB):
                sp.wait_ge(b_spread[i].sem, 16 * (1 + PAIRS * NG // NB))

        @block.tensor
        def _(pe):
            job_count = [0]
            bank_free = []

            def fill(sec, key, name, freed):
                assert JOBS[sec.kind][(key, name)] == job_count[0], (key, name)
                job_count[0] += 1
                for s, n in bank_free:
                    pe.wait_ge(*sec.after(s, n))
                bank_free[:] = [freed]

            def transposes(src):
                for k in range(TB):
                    last = pe.transpose(sh[:, k * 128:(k + 1) * 128], src(k), ident[:, :])
                last.then_inc(sh_full.sem, 1)

            def start_job(sec, key, name):
                a = st_no(sec, key)
                par = st_par(sec, key)
                if name == "xt":
                    fill(sec, key, name, (xT_ready, a))
                    pe.wait_ge(*sec.after(xtok_ready, NORM_NO[sec.kind][key] * TB + TB - 1))
                    transposes(lambda k: xtok[:, k, :])
                elif name == "lg":
                    fill(sec, key, name, (lg_ready, a))
                    pe.wait_ge(*sec.after(xT_ready, a))
                    for k in range(TB):
                        last = pe.matmul(sh[:, k * E:(k + 1) * E], xT_sb[:, par, k * 128:(k + 1) * 128],
                                         ws_sb[:, :], start=True, stop=True)
                    last.then_inc(sh_full.sem, 1)
                else:
                    fill(sec, key, name, (gates_ready, a))
                    pe.wait_ge(*sec.after(comb_ready, a))
                    for k in range(TB):
                        last = pe.transpose(sh[0:E, k * 128:(k + 1) * 128], comb_sb[:, k, :], ident[:, :])
                    last.then_inc(sh_full.sem, 1)

            def norm_job(sec, key):
                j = key[1]
                fill(sec, key, "ht", (hin_ready, j))
                pe.wait_ge(*sec.after(xtok_ready, NORM_NO[sec.kind][key] * TB + TB - 1))
                transposes(lambda k: xtok[:, k, :])

            def unit_tiles(sec, u, S):
                un = unit_no(sec, u)
                par = start_par(sec, u)
                for e in range(E):
                    x_no = un * E + e
                    for ft, (f0, fn) in enumerate(FT):
                        n = x_no * 3 + ft
                        if S == EB[e] + 1 + 2 * ft:
                            pe.wait_ge(*sec.after(xT_ready, start_no(sec, u)))
                            pe.wait_ge(*sec.after(h1_ready, n - 1))
                            pe.matmul(g_ps[0:fn, :], wg_sb[:, e, f0:f0 + fn], xT_sb[:, par, :],
                                      start=True, stop=True).then_inc(g_full.sem, 1)
                        if S == EB[e] + 3 + 2 * ft:
                            pe.wait_ge(*sec.after(xs_ready, x_no))
                            pe.wait_ge(*sec.after(uc_ready, n - 1))
                            pe.matmul(u_ps[0:fn, :], wu_sb[:, e, f0:f0 + fn], xs_sb[:, :],
                                      start=True, stop=True).then_inc(u_full.sem, 1)

            def unit_fills(sec, u, S):
                un = unit_no(sec, u)
                par = start_par(sec, u)
                for e in range(E):
                    x_no = un * E + e
                    if S == DOWN[e]:
                        fill(sec, ("u", u), f"down{e}", (acc_ready, x_no))
                        pe.wait_ge(*sec.after(hh_ready, x_no * 3 + 2))
                        for ft, (f0, fn) in enumerate(FT):
                            last = pe.matmul(sh[:, :], wd_sb[0:fn, e, ft, :], hh_sb[0:fn, (e % 2) * 3 + ft, :],
                                             start=(ft == 0), stop=(ft == 2))
                        last.then_inc(sh_full.sem, 1)
                if S == 62:
                    if u < 2:
                        fill(sec, ("u", u), "yt", (x1_ready, u))
                    else:
                        fill(sec, ("u", u), "yt", (xo_ready, u - 2))
                    pe.wait_ge(*sec.after(acc_ready, un * E + E - 1))
                    transposes(lambda k: acc_sb[:, k * 128:(k + 1) * 128])

            def side_job(sec, q, k, name):
                r = (q + 1) % PH
                l, j, par = r // 2, r % 2, r % 2
                pl, pj = ((q - 1) % PH) // 2, (q - 1) % 2
                key = ("p", q)
                if name == "wblk":
                    fill(sec, key, name, (h_ready, k))
                    pe.wait_ge(*sec.after(y_gated, 2 * k + 1))
                    for b in range(NBLK):
                        last = pe.matmul(sh[:, :], wblk_sb[:, pl, b, :], y_sb[:, b, :], start=(b == 0), stop=(b == 1))
                elif name == "attn":
                    fill(sec, key, name, (x2_ready, 0 if q == 0 else 1))
                    pe.wait_ge(*sec.after(h_ready, k))
                    for t in range(TB):
                        o = sh[:, t * D:(t + 1) * D]
                        pe.matmul(o, h_sb[:, pj, t * 128:(t + 1) * 128], wout_sb[:, :], start=True, stop=False)
                        last = pe.matmul(o, ones_row[:, :], bout_sb[:, :], start=False, stop=True)
                elif name == "ms":
                    fill(sec, key, name, (log_ready, k))
                    pe.wait_ge(*sec.after(sq_ready, k))
                    last = pe.matmul(sh[:, :], mean_w[:, :], norm_t[:, :], start=True, stop=True)
                elif name in ("xp0", "xp1", "z0", "z1"):
                    b = int(name[-1])
                    fill(sec, key, name, (xp_ready if name[0] == "x" else zs_ready, 2 * k + b))
                    pe.wait_ge(*sec.after(xn_ready, k))
                    c = (b if name[0] == "x" else NBLK + b) * 128
                    last = pe.matmul(sh[:, :], win_sb[:, l, c:c + 128], xn_sb[:, :], start=True, stop=True)
                elif name == "wx":
                    fill(sec, key, name, (brest_ready, k))
                    pe.wait_ge(*sec.after(xc_ready, 2 * k + 1))
                    for b in range(NBLK):
                        last = pe.matmul(sh[0:96, :], wx_sb[:, l, b, :], xc_sb[:, par, b, :], start=(b == 0), stop=(b == 1))
                else:
                    b = int(name[-1])
                    fill(sec, key, name, (spx_ready, 2 * k + b))
                    pe.wait_ge(*sec.after(dt_ready, k))
                    last = pe.matmul(sh[:, :], wdt_sb[:, l, b * 128:(b + 1) * 128], dbc_sb[0:DTR, par, :], start=True, stop=True)
                last.then_inc(sh_full.sem, 1)

            def spread_c(sec, g, par):
                pe.matmul(c_ps[g % 2][:, :], sel_c[:, g % NS, :], cs3[:, par, :], start=True, stop=True).then_inc(c_full.sem, 1)

            def add_state(sec, g):
                q, s = g // SL, g % SL
                pe.wait_ge(*sec.after(prod_ready, g))
                if s < 2:
                    pe.wait_ge(*sec.after(y_taken, 2 * q + s))
                pe.matmul(y_ps[s % 2][:, :], ident[:, :], prod_sb[:, g % NPROD, :], start=(s < 2),
                          stop=(s >= SL - 2)).then_inc(summed.sem, 1)

            pe.wait_ge(w_loaded, 16 * LOADS)
            pe.wait_ge(consts, 5)
            pe.wait_ge(vprep, 10)
            for b in range(NBLK):
                pe.matmul(y_ps[b][:, :], ident[:, :], x2_sb[:, 0].rearrange("p k d -> p (k d)"), start=True, stop=True).then_inc(summed.sem, 1)
            pe.matmul(c_ps[0][:, :], ident[:, :], x2_sb[:, 0].rearrange("p k d -> p (k d)"), start=True, stop=True).then_inc(summed.sem, NPROD - 2)
            sec = Section("pro")
            for name in ("xt", "lg", "ct"):
                start_job(sec, "s0", name)
            for u in range(2):
                for S in range(US):
                    unit_tiles(sec, u, S)
                    unit_fills(sec, u, S)
                    for t, name, _ in START:
                        if t == S:
                            start_job(sec, ("st", u), name)
                    if u == 1 and S == LN2[0][0]:
                        norm_job(sec, ("ln", 0))
            norm_job(sec, ("ln", 1))
            for _, name, _ in SIDE:
                if name not in ("wblk", "attn"):
                    side_job(sec, -1, 0, name)
            pe.wait_ge(*sec.after(blo_ready, 0))
            spread_c(sec, 0, 0)

            with pe.Fori(0, PAIRS) as it:
                sec = Section("body", it)
                job_count[0] = 0
                bank_free[:] = [(zs_ready, -1), (spx_ready, -1), (xo_ready, -1), (gates_ready, -1), (hin_ready, -1)]
                for q in range(PH):
                    for s in range(SL):
                        n, g, gn = s // 2, q * SL + s, q * NS + s // 2
                        u, S = slot_of(q, s)
                        if s % 2 == 0:
                            if n == NS - 1:
                                pe.wait_ge(*sec.after(blo_ready, q))
                            if g > 0:
                                pe.wait_ge(*sec.after(prod_ready, g - 1))
                            else:
                                pe.wait_ge(*sec.after(prod_ready, -1))
                            spread_c(sec, gn + 1, (q + (n == NS - 1)) % 2)
                        if g >= LAG:
                            add_state(sec, g - LAG)
                        if g == SG - 1:
                            for behind in range(LAG - 1, -1, -1):
                                add_state(sec, g - behind)
                        unit_tiles(sec, u, S)
                        for t, name, _ in SIDE:
                            if t == s and (name != "attn" or q in (0, PH - 1)):
                                side_job(sec, q, q, name)
                        unit_fills(sec, u, S)
                        for t, name, _ in START:
                            if t == S:
                                start_job(sec, ("st", u), name)
                        if u in (1, 2) and S == LN2[0][0]:
                            norm_job(sec, ("ln", u - 1))

            sec = Section("epi")
            job_count[0] = 0
            bank_free[:] = [(zs_ready, -1), (spx_ready, -1), (xo_ready, -1), (gates_ready, -1)]
            side_job(sec, 0, 0, "wblk")
            side_job(sec, 0, 0, "attn")
            for name in ("xt", "lg", "ct"):
                start_job(sec, "s2", name)
            for u in (2, 3):
                for S in range(US):
                    unit_tiles(sec, u, S)
                    unit_fills(sec, u, S)
                    if u == 2:
                        for t, name, _ in START:
                            if t == S:
                                start_job(sec, ("st", u), name)

        @block.scalar
        def _(act):
            def start_act(sec, key, step):
                a, par = st_no(sec, key), st_par(sec, key)
                if step == 46:
                    act.wait_ge(*filled(sec, key, "xt"))
                    done = (unit_no(sec, key[1]) * 24 - 1) if isinstance(key, tuple) else -1
                    act.wait_ge(*sec.after(u_full, done))
                    act.activation(xT_sb[:, par, :], sh[:, :], ACT.Copy).then_inc(xT_ready.sem, 1)
                elif step == 52:
                    act.wait_ge(*sec.after(dd_ready, a))
                    act.wait_ge(*sec.after(rt_step, a * 17 - 1))
                    act.activation(wt_sb[:, 1, :], wt_sb[:, 0, :], ACT.Exp).then_inc(we_ready.sem, 1)
                elif step == 55:
                    act.wait_ge(*filled(sec, key, "ct"))
                    act.wait_ge(*sec.after(xs_ready, (unit_no(sec, key[1]) + 1) * E - 1 if isinstance(key, tuple) else -1))
                    if key == "s2":
                        act.wait_ge(*sec.after(gate_spread[0], -1))
                    act.activation(gates_sb[:, :], sh[0:E, :], ACT.Copy).then_inc(gates_ready.sem, 1)

            def unit_act(sec, u, S):
                un = unit_no(sec, u)
                for e in range(E):
                    for ft, (f0, fn) in enumerate(FT):
                        n = (un * E + e) * 3 + ft
                        if S == EB[e] + 3 + 2 * ft:
                            act.wait_ge(*sec.after(g_full, n))
                            act.wait_ge(*sec.after(hh_ready, n - 2))
                            act.activation(th_g[0:fn, n % 2, :], g_ps[0:fn, :], ACT.Tanh, scale=0.5).then_inc(thg_ready.sem, 1)
                        if S == EB[e] + 5 + 2 * ft:
                            act.wait_ge(*sec.after(u_full, n))
                            act.wait_ge(*sec.after(hh_ready, n - 2))
                            act.activation(uc_sb[0:fn, n % 2, :], u_ps[0:fn, :], ACT.Copy).then_inc(uc_ready.sem, 1)

            def norm_act(sec, key):
                j = key[1]
                act.wait_ge(*filled(sec, key, "ht"))
                if sec.kind == "body":
                    act.wait_ge(*sec.after(h_ready, j + 1))
                act.activation(hin_sb[:, j, :], sh[:, :], ACT.Copy).then_inc(hin_ready.sem, 1)

            def side_act(sec, q, k, s):
                r = (q + 1) % PH
                l, j, par = r // 2, r % 2, r % 2
                key = ("p", q)
                if s == 9:
                    if l == 0:
                        src = hin_sb[:, j, :]
                        act.wait_ge(*sec.after(hin_ready, j - 2 if sec.kind == "body" and q == 0 else j))
                    else:
                        src = h_sb[:, j, :]
                    if sec.kind == "body":
                        act.wait_ge(*sec.after(h_ready, k))
                    act.wait_ge(*sec.after(xn_ready, k - 1))
                    act.activation(norm_t[:, :], src, ACT.Square).then_inc(sq_ready.sem, 1)
                elif s == 12:
                    act.wait_ge(*filled(sec, key, "ms"))
                    act.activation(norm_t[:, :], sh[:, :], ACT.Ln, bias=eps_sb[:, 0:1]).then_inc(log_ready.sem, 1)
                    act.wait_ge(*sec.after(log_ready, k))
                    act.activation(norm_t[:, :], norm_t[:, :], ACT.Exp, scale=-0.5).then_inc(rms_ready.sem, 1)
                elif s in (15, 16):
                    b = s - 15
                    act.wait_ge(*filled(sec, key, f"xp{b}"))
                    act.wait_ge(*sec.after(conv_step, 8 * (k - 1) + 4 * b + 3))
                    act.activation(xpad[:, b, KC - 1:], sh[:, :], ACT.Copy).then_inc(xp_ready.sem, 1)
                if s in (18, 20):
                    b = int(s == 20)
                    act.wait_ge(*filled(sec, key, f"z{b}"))
                    act.wait_ge(*sec.after(zs_ready, 2 * k + b - 1))
                    act.activation(th_z[:, :], sh[:, :], ACT.Tanh, scale=0.5).then_inc(thz_ready.sem, 1)
                if s in (17, 18):
                    b = s - 17
                    act.wait_ge(*sec.after(conv_step, 8 * k + 4 * b + 3))
                    act.wait_ge(*sec.after(delta_ready, 2 * (k - 1) + b))
                    act.activation(th_c[:, b, :], conv_sb[:, b, :], ACT.Tanh).then_inc(thc_ready.sem, 1)
                elif s == 22:
                    act.wait_ge(*filled(sec, key, "wx"))
                    if sec.kind == "body":
                        act.wait_ge(*sec.after(c_full, q * NS))
                        act.wait_ge(*sec.after(b_spread[(q * NS - 1) % NB], (q * NS - 1) // NB + 1))
                    act.activation(dbc_sb[:, par, :], sh[0:DTR + 2 * NS, :], ACT.Copy).then_inc(dt_ready.sem, 1)
                    act.activation(cs3[32:32 + NS, par, :], sh[DTR:DTR + NS, :], ACT.Copy).then_inc(bhi_ready.sem, 1)
                elif s == 24:
                    act.wait_ge(*sec.after(brest_ready, k))
                    act.activation(cs3[0:NS, par, :], rest_sb[0:NS, :], ACT.Copy).then_inc(bmid_ready.sem, 1)
                if s in (26, 28):
                    b = (s - 26) // 2
                    act.wait_ge(*sec.after(spm_ready, 2 * k + b))
                    act.activation(sp_l[:, b, :], sp_l[:, b, :], ACT.Exp).then_inc(spe_ready.sem, 1)
                    if b == 1:
                        for b in range(NBLK):
                            act.wait_ge(*sec.after(spe_ready, 2 * k + b))
                            act.activation(sp_l[:, b, :], sp_l[:, b, :], ACT.Ln, bias=1.0).then_inc(spl_ready.sem, 1)

            act.wait_ge(w_loaded, 16 * LOADS)
            act.wait_ge(vprep, 10)
            act.activation(a_sb[:, :, :, :], a_sb[:, :, :, :], ACT.Exp).then_inc(aexp, 1)
            act.activation(credit[:, 3:4], eps_sb[:, :], ACT.Copy).then_inc(x1_moved.sem, 1)
            sec = Section("pro")
            for S in (46, 52, 55):
                start_act(sec, "s0", S)
            for u in range(2):
                for S in range(US):
                    unit_act(sec, u, S)
                    start_act(sec, ("st", u), S)
                    if u == 1 and S == LN2[0][2]:
                        norm_act(sec, ("ln", 0))
            norm_act(sec, ("ln", 1))
            for s in range(9, SL):
                side_act(sec, -1, 0, s)

            with act.Fori(0, PAIRS) as it:
                sec = Section("body", it)
                for q in range(PH):
                    l = q // 2
                    for s in range(SL):
                        n, g, gn = s // 2, q * SL + s, q * NS + s // 2
                        u, S = slot_of(q, s)
                        b = s % 2
                        if s < 2:
                            act.wait_ge(*sec.after(delta_ready, 2 * (q - 1) + b))
                        act.wait_ge(*sec.after(scanned, g - 1))
                        act.activation(dA_ps[:, :], delta_sb[:, q % 2, b, :], ACT.Exp,
                                       scale=a_sb[:, l, b, n:n + 1]).then_inc(dA_ready.sem, 1)
                        unit_act(sec, u, S)
                        side_act(sec, q, q, s)
                        if q == PH - 2 and s == 2:
                            act.wait_ge(*sec.after(xo_ready, 0))
                            act.dma_start(out_rows[(it + PAIRS - 1) & (PAIRS - 1), 0], x2_sb[:, 0]).then_inc(stored.sem, 16)
                        if q in (0, 2) and s == 4:
                            j = 1 - q // 2
                            act.wait_ge(*sec.after(x1_ready, -1 if q == 0 else 0))
                            rows = x_rows[(it + 1 if q == 0 else it + 2) & (PAIRS - 1), j]
                            act.dma_start(xin_sb[:, j], rows).then_inc(x_loaded.sem, 16)
                        if q in (0, 2) and s == 3:
                            j = q // 2
                            act.wait_ge(*sec.after(x2_ready, -1 if j == 0 else 0))
                            act.wait_ge(*sec.after(x1_ready, j - 2))
                            act.activation(x1_sb[:, j], x1_new[:, j], ACT.Copy).then_inc(x1_moved.sem, 1)
                        start_act(sec, ("st", u), S)
                        if u in (1, 2) and S == LN2[0][2]:
                            norm_act(sec, ("ln", u - 1))
                act.wait_ge(*sec.after(xo_ready, 1))
                act.dma_start(out_rows[(it + PAIRS - 1) & (PAIRS - 1), 1], x2_sb[:, 1]).then_inc(stored.sem, 16)
            sec = Section("epi")
            for S in (46, 52, 55):
                start_act(sec, "s2", S)
            for u in (2, 3):
                for S in range(US):
                    unit_act(sec, u, S)
                    if u == 2:
                        start_act(sec, ("st", u), S)

        @block.vector
        def _(dve):
            def norm_dve(sec, key, src, step):
                m = NORM_NO[sec.kind][key]
                if step == 0:
                    for k in range(TB):
                        if k == 0:
                            dve.wait_ge(*sec.after(mv_done, m * TB - 1))
                        dve.bn_stats(bn_sb[:, k, :], src[:, k, :]).then_inc(bn_done.sem, 1)
                    dve.wait_ge(*sec.after(bn_done, m * TB + TB - 1))
                    dve.wait_ge(*sec.after(xtok_ready, m * TB - 1))
                    dve.wait_ge(*sec.after(ve_done, m - 1))
                    dve.memset(carrier[:, :], 0.0)
                    for k in range(TB):
                        dve.bn_aggr(mv_sb[:, k, :], bn_sb[:, k, :]).then_inc(mv_done.sem, 1)
                else:
                    dve.wait_ge(*sec.after(rs_done, m))
                    for k in range(TB):
                        dve.tensor_scalar(xtok[:, k, :], src[:, k, :], mv_sb[:, k, 0:1], rs_sb[:, 1, k:k + 1],
                                          ALU.subtract, ALU.mult).then_inc(xtok_ready.sem, 1)

            def start_dve(sec, key, step):
                a, par = st_no(sec, key), st_par(sec, key)
                src, j = st_src(sec, key)
                R = [a * 17]

                def link(inst):
                    inst.then_inc(rt_step.sem, 1)
                    dve.wait_ge(*sec.after(rt_step, R[0]))
                    R[0] += 1

                if step == 40:
                    if j is None:
                        load_no = {"pro": {0: 0, 1: 1, 2: 2}, "body": {1: 0, 4: 1}}[sec.kind][served(sec, key)]
                        dve.wait_ge(*sec.after(x_loaded, load_no))
                    elif sec.kind == "body":
                        dve.wait_ge(*sec.after(x2_ready, -1 if j == 0 else 0))
                    else:
                        dve.wait_ge(*sec.after(x2_ready, -1 if j == 0 else 0))
                    norm_dve(sec, key, src, 0)
                elif step == 43:
                    norm_dve(sec, key, src, 1)
                elif step == 51:
                    dve.wait_ge(*filled(sec, key, "lg"))
                    dve.tensor_tensor(lg_sb[:, :, :], sh[:, 0:TB * E].rearrange("p (k e) -> p k e", e=E),
                                      bs_sb[:, :].unsqueeze(1).broadcast_to([128, TB, E]), ALU.add).then_inc(lg_ready.sem, 1)
                    dve.wait_ge(*sec.after(lg_ready, a))
                    dve.memset(carrier[:, :], 0.0)
                    for k in range(TB):
                        dve.max(mx_sb[:, k, :], lg_sb[:, k, :]).then_inc(rt_step.sem, 1)
                    R[0] += TB
                    dve.wait_ge(*sec.after(rt_step, R[0] - 1))
                    dve.tensor_tensor(wt_sb[:, 0, :], mx_sb[:, :, 1], mx_sb[:, :, 0], ALU.subtract).then_inc(dd_ready.sem, 1)
                    for k in range(TB):
                        dve.max_index(mi_sb[:, k, :], mx_sb[:, k, :], lg_sb[:, k, :]).then_inc(rt_step.sem, 1)
                    R[0] += TB
                    dve.wait_ge(*sec.after(rt_step, R[0] - 1))
                    link(dve.tensor_copy(mf_sb[:, :, :], mi_sb[:, :, 0:2]))
                elif step == 53:
                    R[0] = a * 17 + 9
                    dve.wait_ge(*sec.after(we_ready, a))
                    link(dve.tensor_scalar(wt_sb[:, 2, :], wt_sb[:, 1, :], 4.0, 4.0, ALU.mult, ALU.add))
                    link(dve.reciprocal(wt_sb[:, 3, :], wt_sb[:, 2, :]))
                    link(dve.tensor_tensor(wt_sb[:, 4, :], wt_sb[:, 1, :], wt_sb[:, 3, :], ALU.mult))
                    iota = iota_e[:, :].unsqueeze(1).broadcast_to([128, TB, E])
                    for i in range(2):
                        at = mf_sb[:, :, i].unsqueeze(2).broadcast_to([128, TB, E])
                        w = wt_sb[:, 3 + i, :].unsqueeze(2).broadcast_to([128, TB, E])
                        link(dve.tensor_tensor(eq_sb[:, i], iota, at, ALU.is_equal))
                        link(dve.tensor_tensor(eq_sb[:, 2 + i], eq_sb[:, i], w, ALU.mult))
                    dve.tensor_tensor(comb_sb[:, :, :], eq_sb[:, 2], eq_sb[:, 3], ALU.add).then_inc(comb_ready.sem, 1)
                    link(dve.memset(eq_sb[:, 0, 0, 0:1], 0.0))

            def unit_dve(sec, u, S):
                un, par = unit_no(sec, u), start_par(sec, u)
                for e in range(E):
                    x_no = un * E + e
                    if S == EB[e] + 2:
                        dve.wait_ge(*gate_on_chip(sec, x_no))
                        dve.wait_ge(*sec.after(u_full, x_no * 3 - 1))
                        dve.tensor_tensor(xs_sb[:, :], xT_sb[:, par, :], gate_sb[:, e % NGATE, :], ALU.mult).then_inc(xs_ready.sem, 1)
                    for ft, (f0, fn) in enumerate(FT):
                        n = x_no * 3 + ft
                        if S == EB[e] + 3 + 2 * ft:
                            dve.wait_ge(*sec.after(thg_ready, n))
                            dve.wait_ge(*sec.after(hh_ready, n - 2))
                            dve.scalar_tensor_tensor(h1_sb[0:fn, n % 2, :], th_g[0:fn, n % 2, :], 1.0, g_ps[0:fn, :],
                                                     ALU.add, ALU.mult).then_inc(h1_ready.sem, 1)
                    if S == DOWN[e] + 2:
                        dve.wait_ge(*filled(sec, ("u", u), f"down{e}"))
                        dve.wait_ge(*sec.after(acc_ready, x_no - 1))
                        if e == 0:
                            dve.tensor_copy(acc_sb[:, :], sh[:, :]).then_inc(acc_ready.sem, 1)
                        else:
                            dve.tensor_tensor(acc_sb[:, :], acc_sb[:, :], sh[:, :], ALU.add).then_inc(acc_ready.sem, 1)
                if S == 63:
                    dve.wait_ge(*filled(sec, ("u", u), "yt"))
                    y = sh[:, :].rearrange("p (k d) -> p k d", k=TB)
                    if u < 2:
                        if sec.kind == "body":
                            dve.wait_ge(*sec.after(x1_moved, u))
                        dve.tensor_tensor(x1_new[:, u], xin_sb[:, u], y, ALU.add).then_inc(x1_ready.sem, 1)
                    else:
                        dve.tensor_tensor(x2_sb[:, u - 2], x2_sb[:, u - 2], y, ALU.add).then_inc(xo_ready.sem, 1)

            def ln2_dve(sec, j, step):
                if step == 0:
                    dve.wait_ge(*sec.after(x1_ready, j))
                norm_dve(sec, ("ln", j), x1_new[:, j], step)

            def side_dve(sec, q, k, s):
                r = (q + 1) % PH
                l, j, par = r // 2, r % 2, r % 2
                p = (q - 1) % PH
                pl, pj, ppar = p // 2, p % 2, p % 2
                key = ("p", q)
                has_post = sec.kind != "pro"
                if has_post and s in (3, 4):
                    b = s - 3
                    dve.wait_ge(*sec.after(summed, (q * SL if sec.kind == "body" else 0) - 2 + b))
                    dve.wait_ge(*sec.after(h_ready, k - 1))
                    dve.scalar_tensor_tensor(y_sb[:, b, :], xc_sb[:, ppar, b, :], dp_sb[:, pl, b:b + 1],
                                             y_ps[b][:, :], ALU.mult, ALU.add).then_inc(y_taken.sem, 1)
                elif has_post and s == 8:
                    dve.wait_ge(*filled(sec, key, "wblk"))
                    if pl == 0:
                        src = hin_sb[:, pj, :]
                        dve.wait_ge(*sec.after(x2_ready, -1 if pj == 0 else 0))
                    else:
                        src = h_sb[:, pj, :]
                    dve.wait_ge(*sec.after(h_ready, k - 1))
                    dve.tensor_tensor(h_sb[:, pj, :], src, sh[:, :], ALU.add).then_inc(h_ready.sem, 1)
                elif s == 11 and q in (0, PH - 1):
                    dve.wait_ge(*filled(sec, key, "attn"))
                    if sec.kind == "body":
                        dve.wait_ge(*sec.after(x1_moved, -1 if q == 0 else 0))
                    dve.wait_ge(*sec.after(stored, -1 if q == 0 else 0))
                    dve.tensor_tensor(x2_sb[:, pj], x1_sb[:, pj], sh[:, :].rearrange("p (k d) -> p k d", k=TB),
                                      ALU.add).then_inc(x2_ready.sem, 1)
                if sec.kind == "epi":
                    return
                if s == 13:
                    dve.wait_ge(*sec.after(rms_ready, k))
                    if l == 0:
                        dve.wait_ge(*sec.after(hin_ready, j - 2 if sec.kind == "body" and q == 0 else j))
                        src = hin_sb[:, j, :]
                    else:
                        dve.wait_ge(*sec.after(h_ready, k))
                        src = h_sb[:, j, :]
                    dve.scalar_tensor_tensor(xn_sb[:, :], src, normw_sb[:, l:l + 1], norm_t[:, :],
                                             ALU.mult, ALU.mult).then_inc(xn_ready.sem, 1)
                for b in range(NBLK):
                    if s == 16 + b:
                        for t in range(KC):
                            if t == 0:
                                dve.wait_ge(*sec.after(xp_ready, 2 * k + b))
                                dve.wait_ge(*sec.after(delta_ready, 2 * (k - 1) + b))
                                c = dve.tensor_scalar(conv_sb[:, b, :], xpad[:, b, 0:T], cw_sb[:, l, b, 0:1],
                                                      cb_sb[:, l, b:b + 1], ALU.mult, ALU.add)
                            else:
                                dve.wait_ge(*sec.after(conv_step, 8 * k + 4 * b + t - 1))
                                c = dve.scalar_tensor_tensor(conv_sb[:, b, :], xpad[:, b, t:t + T], cw_sb[:, l, b, t:t + 1],
                                                             conv_sb[:, b, :], ALU.mult, ALU.add)
                            c.then_inc(conv_step.sem, 1)
                    if s == 18 + b:
                        dve.wait_ge(*sec.after(thc_ready, 2 * k + b))
                        if has_post:
                            dve.wait_ge(*sec.after(y_taken, 2 * k + b))
                        dve.scalar_tensor_tensor(xc_sb[:, par, b, :], th_c[:, b, :], 1.0, conv_sb[:, b, :],
                                                 ALU.add, ALU.mult).then_inc(xc_ready.sem, 1)
                    if s == (18, 20)[b]:
                        dve.wait_ge(*sec.after(thz_ready, 2 * k + b))
                        dve.scalar_tensor_tensor(zs_sb[:, par, b, :], th_z[:, :], 1.0, sh[:, :],
                                                 ALU.add, ALU.mult).then_inc(zs_ready.sem, 1)
                    if s == 25 + 2 * b:
                        dve.wait_ge(*filled(sec, key, f"dt{b}"))
                        dve.wait_ge(*sec.after(xc_ready, 2 * k + b))
                        dve.tensor_scalar(sp_x[:, b, :], sh[:, :], bdt_sb[:, l, b:b + 1], None, ALU.add).then_inc(spx_ready.sem, 1)
                        dve.wait_ge(*sec.after(spx_ready, 2 * k + b))
                        dve.tensor_scalar(sp_l[:, b, :], sp_x[:, b, :], SPLUS, None, ALU.min).then_inc(spm_ready.sem, 1)
                    if s == 29 + b:
                        dve.wait_ge(*sec.after(spl_ready, 2 * k + b))
                        dve.tensor_tensor(delta_sb[:, par, b, :], sp_x[:, b, :], sp_l[:, b, :], ALU.max).then_inc(delta_ready.sem, 1)
                if s == 23:
                    dve.wait_ge(*sec.after(bhi_ready, k))
                    dve.wait_ge(*sec.after(dt_ready, k))
                    dve.wait_ge(*sec.after(blo_ready, k - 1))
                    dve.tensor_tensor(rest_sb[0:NS, :], sh[DTR:DTR + NS, :], cs3[32:32 + NS, par, :], ALU.subtract).then_inc(brest_ready.sem, 1)
                if s == 25:
                    dve.wait_ge(*sec.after(bmid_ready, k))
                    dve.tensor_tensor(cs3[64:64 + NS, par, :], rest_sb[0:NS, :], cs3[0:NS, par, :], ALU.subtract).then_inc(blo_ready.sem, 1)

            def read_out(sec, g):
                dve.wait_ge(*sec.after(scanned, g))
                dve.wait_ge(*sec.after(c_full, g // 2))
                dve.wait_ge(*sec.after(summed, g - NPROD))
                dve.tensor_tensor(prod_sb[:, g % NPROD, :], st_sb[:, g % 2, :], c_ps[(g // 2) % 2][:, :], ALU.mult).then_inc(prod_ready.sem, 1)

            dve.memset(mean_w[:, :], 1.0 / D).then_inc(vprep, 1)
            dve.memset(ones_row[:, :], 1.0).then_inc(vprep, 1)
            for e in range(E):
                last = dve.memset(iota_e[:, e:e + 1], float(e))
            last.then_inc(vprep, 1)
            dve.memset(x2_sb[:, :, :, :], 0.0).then_inc(vprep, 1)
            dve.memset(x1_sb[:, :, :, :], 0.0).then_inc(vprep, 1)
            dve.memset(xpad[:, :, :], 0.0).then_inc(vprep, 1)
            dve.memset(xc_sb[:, :, :, :], 0.0).then_inc(vprep, 1)
            dve.memset(zs_sb[:, :, :, :], 0.0).then_inc(vprep, 1)
            dve.memset(cs3[:, :, :], 0.0).then_inc(vprep, 1)
            dve.memset(eps_sb[:, :], EPS).then_inc(vprep, 1)
            dve.memset(st_sb[:, :, :], 0.0).then_inc(scanned.sem, 4)
            dve.memset(prod_sb[:, :, :], 0.0).then_inc(prod_ready.sem, 2)
            dve.memset(h_sb[:, :, :], 0.0).then_inc(h_ready.sem, 1)
            dve.wait_ge(vprep, 10)
            dve.memset(credit[:, 0:1], 0.0).then_inc(x2_ready.sem, 1)
            dve.memset(credit[:, 1:2], 0.0).then_inc(xo_ready.sem, 1)
            dve.memset(credit[:, 2:3], 0.0).then_inc(stored.sem, 16)
            dve.wait_ge(w_loaded, 16 * LOADS)
            dve.wait_ge(aexp, 1)
            dve.tensor_scalar(a_sb[:, :, :, :], a_sb[:, :, :, :], -1.0, None, ALU.mult).then_inc(vprep, 1)
            dve.tensor_scalar(cw_sb[:, :, :, :], cw_sb[:, :, :, :], 0.5, None, ALU.mult).then_inc(vprep, 1)
            dve.tensor_scalar(cb_sb[:, :, :], cb_sb[:, :, :], 0.5, None, ALU.mult).then_inc(vprep, 1)
            dve.tensor_scalar(wblk_sb[:, :, :, :], wblk_sb[:, :, :, :], 0.5, None, ALU.mult).then_inc(vprep, 1)
            dve.wait_ge(vprep, 14)
            sec = Section("pro")
            for S in (40, 43, 51, 53):
                start_dve(sec, "s0", S)
            for u in range(2):
                for S in range(US):
                    unit_dve(sec, u, S)
                    start_dve(sec, ("st", u), S)
                    if u == 1 and S in (0, 3):
                        ln2_dve(sec, 0, S)
            ln2_dve(sec, 1, 0)
            ln2_dve(sec, 1, 3)
            for s in range(13, SL):
                side_dve(sec, -1, 0, s)

            with dve.Fori(0, PAIRS) as it:
                sec = Section("body", it)
                for q in range(PH):
                    for s in range(SL):
                        g = q * SL + s
                        u, S = slot_of(q, s)
                        dve.wait_ge(*sec.after(dA_ready, g))
                        dve.wait_ge(*sec.after(dbu_ready, g))
                        dve.wait_ge(*sec.after(prod_ready, g - 2))
                        dve.tensor_tensor_scan(st_sb[:, g % 2, :], dA_ps[:, :], dbu_sb[:, g % NDBU, :], 0.0,
                                               ALU.mult, ALU.add).then_inc(scanned.sem, 1)
                        if g > 0:
                            read_out(sec, g - 1)
                        if g == SG - 1:
                            read_out(sec, g)
                        side_dve(sec, q, q, s)
                        unit_dve(sec, u, S)
                        start_dve(sec, ("st", u), S)
                        if u in (1, 2) and S in (0, 3):
                            ln2_dve(sec, u - 1, S)
            sec = Section("epi")
            for s in (3, 4, 8, 11):
                side_dve(sec, 0, 0, s)
            for S in (40, 43, 51, 53):
                start_dve(sec, "s2", S)
            for u in (2, 3):
                for S in range(US):
                    unit_dve(sec, u, S)
                    if u == 2:
                        start_dve(sec, ("st", u), S)

        @block.gpsimd
        def _(pool):
            def norm_pool(sec, key):
                m = NORM_NO[sec.kind][key]
                pool.wait_ge(*sec.after(mv_done, m * TB + TB - 1))
                pool.wait_ge(*sec.after(rs_done, m - 1))
                pool.tensor_tensor(rs_sb[:, 0, :], mv_sb[:, :, 1], eps4[:, :], ALU.add).then_inc(ve_done.sem, 1)
                pool.wait_ge(*sec.after(ve_done, m))
                pool.wait_ge(*sec.after(xtok_ready, m * TB - 1))
                pool.tensor_tensor(rs_sb[:, 1, :], rs_sb[:, 0, :], neg_half[:, :], ALU.pow).then_inc(rs_done.sem, 1)

            def unit_pool(sec, u, S):
                un = unit_no(sec, u)
                for e in range(E):
                    for ft, (f0, fn) in enumerate(FT):
                        n = (un * E + e) * 3 + ft
                        if S == EB[e] + 6 + 2 * ft:
                            pool.wait_ge(*sec.after(h1_ready, n))
                            pool.wait_ge(*sec.after(uc_ready, n))
                            pool.wait_ge(*sec.after(acc_ready, un * E + e - 2))
                            pool.tensor_tensor(hh_sb[0:fn, (e % 2) * 3 + ft, :], h1_sb[0:fn, n % 2, :],
                                               uc_sb[0:fn, n % 2, :], ALU.mult).then_inc(hh_ready.sem, 1)

            def side_pool(sec, q, k, s):
                par = (q + 1) % 2
                ppar = (q - 1) % 2
                if sec.kind != "pro" and s in (4, 5):
                    b = s - 4
                    pool.wait_ge(*sec.after(y_taken, 2 * k + b))
                    pool.tensor_tensor(y_sb[:, b, :], y_sb[:, b, :], zs_sb[:, ppar, b, :], ALU.mult).then_inc(y_gated.sem, 1)
                if sec.kind != "epi" and s == 29:
                    for b in range(NBLK):
                        pool.wait_ge(*sec.after(delta_ready, 2 * k + b))
                        if sec.kind == "body":
                            pool.wait_ge(*sec.after(dbu_ready, q * SL - 1 + LEAD))
                        pool.tensor_tensor(du_sb[:, par, b, :], delta_sb[:, par, b, :], xc_sb[:, par, b, :],
                                           ALU.mult).then_inc(du_ready.sem, 1)

            def scale_b(sec, g):
                gn, b = g // 2, g % 2
                if g % SL < 2:
                    pool.wait_ge(*sec.after(du_ready, 2 * (g // SL - 1) + b if sec.kind == "body" else b))
                if sec.kind == "body":
                    pool.wait_ge(*sec.after(b_spread[gn % NB], gn // NB))
                    pool.wait_ge(*sec.after(scanned, g - NDBU))
                else:
                    pool.wait_ge(*sec.after(b_spread[gn % NB], gn // NB))
                pool.tensor_tensor(dbu_sb[:, g % NDBU, :], du_sb[:, (g // SL) % 2, b, :], b_sb[:, gn % NB, :],
                                   ALU.mult).then_inc(dbu_ready.sem, 1)

            pool.memset(eps4[:, :], EPS).then_inc(consts, 1)
            pool.memset(dbu_sb[:, :, :], 0.0).then_inc(dbu_ready.sem, 1)
            pool.memset(ident[:, :], 0.0).then_inc(cprep, 1)
            pool.memset(sel_c[:, :, :], 0.0).then_inc(cprep, 1)
            pool.wait_ge(cprep, 2)
            pool.affine_select(out=ident[:, :], in_=ident[:, :], compare_op=ALU.not_equal, fill=1.0, base=0,
                               pattern=[[-1, 128]], channel_multiplier=1).then_inc(consts, 1)
            for a in range(3):
                pool.affine_select(out=sel_c[:, :, :], in_=sel_c[:, :, :], compare_op=ALU.not_equal, fill=1.0,
                                   base=-32 * a, pattern=[[-1, NS], [0, 128]], channel_multiplier=1).then_inc(cprep, 1)
                pool.wait_ge(cprep, 3 + a)
            pool.memset(neg_half[:, :], -0.5).then_inc(consts, 3)
            sec = Section("pro")
            norm_pool(sec, "s0")
            for u in range(2):
                for S in range(US):
                    unit_pool(sec, u, S)
                    if S == 41:
                        norm_pool(sec, ("st", u))
                    if u == 1 and S == 1:
                        norm_pool(sec, ("ln", 0))
            norm_pool(sec, ("ln", 1))
            side_pool(sec, -1, 0, 29)
            for g in range(LEAD):
                scale_b(sec, g)

            with pool.Fori(0, PAIRS) as it:
                sec = Section("body", it)
                for q in range(PH):
                    for s in range(SL):
                        g, gn, b = q * SL + s, q * NS + s // 2, s % 2
                        u, S = slot_of(q, s)
                        scale_b(sec, g + LEAD)
                        side_pool(sec, q, q, s)
                        unit_pool(sec, u, S)
                        if S == 41:
                            norm_pool(sec, ("st", u))
                        if u in (1, 2) and S == 1:
                            norm_pool(sec, ("ln", u - 1))
            sec = Section("epi")
            for s in (4, 5):
                side_pool(sec, 0, 0, s)
            norm_pool(sec, "s2")
            for u in (2, 3):
                for S in range(US):
                    unit_pool(sec, u, S)
                    if u == 2 and S == 41:
                        norm_pool(sec, ("st", u))


def laid_out(name, a):
    import numpy as np

    name = name.split("_", 2)[2]
    if name in ("Win", "Wdt", "Wg", "Wu", "Wd"):
        return a.transpose(1, 0, 2)
    if name == "Wx":
        a = np.concatenate([a[..., :DTR], a[..., DTR + NS:], a[..., DTR:DTR + NS]], -1)
    if name in ("Wx", "Wblk", "conv_w", "A_log"):
        return a.reshape(NL, NBLK, 128, -1).transpose(2, 0, 1, 3)
    if name in ("conv_b", "bdt", "Dp"):
        return a.reshape(NL, NBLK, 128).transpose(2, 0, 1)
    if name == "norm_w":
        return a.T
    if name in ("bout", "bs"):
        return a.reshape(1, -1)
    return a


_ARGS = ["L0_attn_x", "L0_attn_norm_w", "L0_attn_Win", "L0_attn_conv_w", "L0_attn_conv_b", "L0_attn_Wx",
         "L0_attn_Wdt", "L0_attn_bdt", "L0_attn_A_log", "L0_attn_Dp", "L0_attn_Wblk", "L0_attn_Wout",
         "L0_attn_bout", "L0_ffn_Ws", "L0_ffn_bs", "L0_ffn_Wg", "L0_ffn_Wu", "L0_ffn_Wd"]


def kernel(**inputs):
    import numpy as np
    import concourse.bacc as bacc
    from concourse.bass_utils import run_bass_kernel_spmd

    nc = bacc.Bacc("TRN2", target_bir_lowering=False, num_devices=1)
    arrays, args = {}, []
    for name in _ARGS:
        a = np.ascontiguousarray(laid_out(name, np.asarray(inputs[name])))
        arrays[f"in_{name}"] = a
        args.append(nc.dram_tensor(f"in_{name}", a.shape, F32, kind="ExternalInput").ap())
    args.append(nc.dram_tensor("out_0", (B, T, D), F32, kind="ExternalOutput").ap())
    build(nc, *args)
    r = run_bass_kernel_spmd(nc, [arrays], core_ids=[0])
    return r.results[0]["out_0"]
```

```python
from contextlib import ExitStack

import concourse.bass as bass
from concourse import mybir

F32 = mybir.dt.float32
BF16 = mybir.dt.bfloat16
U32 = mybir.dt.uint32
ALU = mybir.AluOpType
ACT = mybir.ActivationFunctionType

B, T, D = 16, 512, 128
NL, NS, KC, DTR = 4, 16, 4, 64
NBLK = 2
TB = T // 128
E, F = 8, 344
FT = [(0, 128), (128, 128), (256, 88)]
EPS = 1e-5
PAIRS = B // 2
PH = 2 * NL
SL = 2 * NS
US = 2 * SL
SPLUS = 40.0

SIDE = [
    (6, "wblk", 8), (9, "attn", 11), (10, "ms", 12), (13, "xp0", 15), (14, "xp1", 16), (16, "z0", 18), (18, "z1", 20), (20, "wx", 23),
    (23, "dt0", 25), (25, "dt1", 27),
]
EB = [1 + 7 * e for e in range(E)]
DOWN = [12, 19, 26, 33, 40, 47, 56, 60]
UNIT = [(DOWN[e], f"down{e}", DOWN[e] + 2) for e in range(E)] + [(62, "yt", 63)]
START = [(44, "xt", 46), (49, "lg", 51), (53, "ct", 55)]
LN2 = [(4, "ht", 6)]
LAG = 3
LEAD = 2
NPROD, NDBU, NB = 4, 4, 4
NGATE = 2
GATE = [57] + [EB[e] - 6 for e in range(1, E)]


UNITS = {"first": (0, 1), "body": (0, 1, 2, 3), "last": (2, 3), "epi": (2, 3)}
STARTS = {"first": (0, 3), "body": (0, 1, 2, 3), "last": (1, 2)}
FIRST_PAIR = {"first": 0, "body": 1, "last": PAIRS - 1}


class Signal:

    def __init__(self, sem, credit, pro, trip, step=1, first=None, last=None):
        self.sem, self.credit, self.pro, self.trip, self.step = sem, credit, pro, trip, step
        self.first = trip if first is None else first
        self.last = trip if last is None else last


class Section:

    def __init__(self, kind, it=0):
        self.kind, self.it = kind, it
        self.trip = kind in ("first", "body", "last")

    def pair(self, ahead):
        return (self.it + (FIRST_PAIR[self.kind] + ahead + PAIRS)) & (PAIRS - 1)

    def pre_runs(self, q):
        return self.kind != "epi" and not (self.kind == "last" and q == PH - 1)

    def v(self, s, n):
        if self.kind == "pro":
            return (s.credit + n + 1) * s.step
        before = s.credit + s.pro
        if self.kind != "first":
            before += s.first
        if self.kind in ("last", "epi"):
            before += (PAIRS - 2) * s.trip
        if self.kind == "epi":
            before += s.last
        if self.kind != "body":
            return (before + n + 1) * s.step
        assert before + n + 1 >= 1, (s.sem, n)
        return self.it * (s.trip * s.step) + (before + n + 1) * s.step

    def after(self, s, n):
        val = self.v(s, n)
        return s.sem, (max(val, 0) if isinstance(val, int) else val)


def shared_bank_order():
    order = {}
    jobs = []
    for name in ("xt", "lg", "ct"):
        jobs.append(("s0", name))
    for u in range(2):
        for s in range(US):
            jobs += [(("u", u), n) for t, n, _ in UNIT if t == s]
            jobs += [(("st", u), n) for t, n, _ in START if t == s]
            if u == 1:
                jobs += [(("ln", 0), n) for t, n, _ in LN2 if t == s]
    jobs.append((("ln", 1), "ht"))
    jobs += [(("p", -1), n) for _, n, _ in SIDE if n not in ("wblk", "attn")]
    order["pro"] = {j: i for i, j in enumerate(jobs)}
    for kind in ("first", "body", "last"):
        jobs = []
        last = -9, 0
        for q in range(PH):
            for s in range(SL):
                u, S = q // 2, (q % 2) * SL + s
                here = [(("p", q), n, c) for t, n, c in SIDE if t == s and (n != "attn" or q in (0, PH - 1))
                        and (n in ("wblk", "attn") or Section(kind).pre_runs(q))]
                if u in UNITS[kind]:
                    here += [(("u", u), n, c - S + s) for t, n, c in UNIT if t == S]
                if u in STARTS[kind]:
                    here += [(("st", u), n, c - S + s) for t, n, c in START if t == S]
                if u in (1, 2) and kind != "last":
                    here += [(("ln", u - 1), n, c - S + s) for t, n, c in LN2 if t == S]
                for k, n, c in here:
                    rank = ("p", "u", "st", "ln").index(k[0])
                    assert last[0] <= q * SL + s + 2 and last < (q * SL + c, rank), (
                        "the bank is read too late", k, n, last, q * SL + s)
                    last = q * SL + c, rank
                    jobs.append((k, n))
        order[kind] = {j: i for i, j in enumerate(jobs)}
    jobs = [(("p", 0), "wblk"), (("p", 0), "attn")]
    jobs += [("s2", n) for n in ("xt", "lg", "ct")]
    for u in (2, 3):
        for s in range(US):
            jobs += [(("u", u), n) for t, n, _ in UNIT if t == s]
            if u == 2:
                jobs += [(("st", u), n) for t, n, _ in START if t == s]
    order["epi"] = {j: i for i, j in enumerate(jobs)}
    return order


def build(nc, x, norm_w, Win, conv_w, conv_b, Wx, Wdt, bdt, A_log, Dp, Wblk, Wout, bout,
          Ws, bs, Wg, Wu, Wd, out):
    JOBS = shared_bank_order()
    with ExitStack() as ctx:
        def sb(name, shape, dt=F32):
            return ctx.enter_context(nc.sbuf_tensor(name, shape, dt))

        def bank(name):
            return ctx.enter_context(nc.psum_tensor(name, [128, T], F32))

        wg_sb = sb("wg_sb", [128, E, F])
        wu_sb = sb("wu_sb", [128, E, F])
        wd_sb = sb("wd_sb", [128, E, len(FT), D])
        win_sb = sb("win_sb", [128, NL, 4 * 128])
        wx_sb = sb("wx_sb", [128, NL, NBLK, DTR + 2 * NS])
        wdt_sb = sb("wdt_sb", [DTR, NL, NBLK * 128])
        wblk_sb = sb("wblk_sb", [128, NL, NBLK, D])
        wout_sb = sb("wout_sb", [128, D])
        bout_sb = sb("bout_sb", [1, D])
        ws_sb = sb("ws_sb", [128, E])
        bs_sb = sb("bs_sb", [128, E])
        normw_sb = sb("normw_sb", [128, NL])
        cw_sb = sb("cw_sb", [128, NL, NBLK, KC])
        cb_sb = sb("cb_sb", [128, NL, NBLK])
        bdt_sb = sb("bdt_sb", [128, NL, NBLK])
        a_sb = sb("a_sb", [128, NL, NBLK, NS])
        dp_sb = sb("dp_sb", [128, NL, NBLK])
        ident = sb("ident", [128, 128])
        mean_w = sb("mean_w", [128, 128])
        ones_row = sb("ones_row", [1, 128])
        sel_c = sb("sel_c", [96, NS, 128], BF16)
        iota_e = sb("iota_e", [128, E])
        neg_half = sb("neg_half", [128, TB])
        eps_sb = sb("eps_sb", [128, 1])
        eps4 = sb("eps4", [128, TB])
        credit = sb("credit", [128, 4])
        carrier = sb("carrier", [128, 1])
        b_sb = sb("b_sb", [128, NB, T])
        dbu_sb = sb("dbu_sb", [128, NDBU, T])
        st_sb = sb("st_sb", [128, 2, T])
        prod_sb = sb("prod_sb", [128, NPROD, T])
        delta_sb = sb("delta_sb", [128, 2, NBLK, T])
        du_sb = sb("du_sb", [128, 2, NBLK, T])
        xc_sb = sb("xc_sb", [128, 2, NBLK, T])
        zs_sb = sb("zs_sb", [128, 2, NBLK, T])
        cs3 = sb("cs3", [96, 2, T], BF16)
        y_sb = sb("y_sb", [128, NBLK, T])
        h_sb = sb("h_sb", [128, 2, T])
        hin_sb = sb("hin_sb", [128, 2, T])
        norm_t, xn_sb = y_sb[:, 0, :], y_sb[:, 1, :]
        xpad = sb("xpad", [128, NBLK, KC - 1 + T])
        conv_sb = sb("conv_sb", [128, NBLK, T])
        th_c = sb("th_c", [128, NBLK, T])
        th_z = sb("th_z", [128, T])
        dbc_sb = sb("dbc_sb", [DTR + 2 * NS, 2, T])
        rest_sb = sb("rest_sb", [NS, T])
        sp_x, sp_l = conv_sb, th_c
        xin_sb = sb("xin_sb", [128, 2, TB, D])
        x1_new = sb("x1_new", [128, 2, TB, D])
        x1_sb = sb("x1_sb", [128, 2, TB, D])
        x2_sb = sb("x2_sb", [128, 2, TB, D])
        xtok = sb("xtok", [128, TB, D])
        bn_sb = sb("bn_sb", [128, TB, 6])
        mv_sb = sb("mv_sb", [128, TB, 2])
        rs_sb = sb("rs_sb", [128, 2, TB])
        xT_sb = sb("xT_sb", [128, 2, T])
        xs_sb = sb("xs_sb", [128, T])
        acc_sb = sb("acc_sb", [128, T])
        th_g = sb("th_g", [128, 2, T])
        h1_sb = th_g
        uc_sb = sb("uc_sb", [128, 2, T])
        hh_sb = sb("hh_sb", [128, 6, T])
        lg_sb = sb("lg_sb", [128, TB, E])
        mx_sb = sb("mx_sb", [128, TB, E])
        mi_sb = sb("mi_sb", [128, TB, E], U32)
        mf_sb = sb("mf_sb", [128, TB, 2])
        wt_sb = sb("wt_sb", [128, 5, TB])
        eq_sb = sb("eq_sb", [128, 4, TB, E])
        comb_sb = sb("comb_sb", [128, TB, E])
        gates_sb = sb("gates_sb", [E, T])
        gate_sb = sb("gate_sb", [128, NGATE, T])
        dA_ps, c_ps = bank("dA_ps"), [bank("c0_ps"), bank("c1_ps")]
        y_ps = [bank("y0_ps"), bank("y1_ps")]
        g_ps, u_ps, sh = bank("g_ps"), bank("u_ps"), bank("sh")

        def signal(name, credit=0, pro=0, trip=0, step=1, first=None, last=None):
            return Signal(ctx.enter_context(nc.semaphore(name)), credit, pro, trip, step, first, last)

        NG, SG = PH * NS, PH * SL
        b_spread = [signal(f"b_spread{i}", 0, 0, NG // NB, 16) for i in range(NB)]
        c_full = signal("c_full", 0, 0, NG)
        dA_ready = signal("dA_ready", 0, 0, SG)
        dbu_ready = signal("dbu_ready", 1, 0, SG)
        scanned = signal("scanned", 4, 0, SG)
        prod_ready = signal("prod_ready", 2, 0, SG)
        summed = signal("summed", NPROD, 0, SG)
        y_taken, y_gated = signal("y_taken", 0, 0, 2 * PH), signal("y_gated", 0, 0, 2 * PH)
        h_ready = signal("h_ready", 1, 0, PH)
        x2_ready = signal("x2_ready", 1, 0, 2)
        x1_moved = signal("x1_moved", 1, 0, 2)
        sq_ready, log_ready, rms_ready, xn_ready = (
            signal(n, 0, 1, PH, last=PH - 1) for n in ("sq_ready", "log_ready", "rms_ready", "xn_ready"))
        xp_ready, thc_ready, xc_ready, thz_ready, zs_ready = (
            signal(n, 0, 2, 2 * PH, last=2 * PH - 2) for n in ("xp_ready", "thc_ready", "xc_ready", "thz_ready", "zs_ready"))
        conv_start = signal("conv_start", 0, 2, 2 * PH, last=2 * PH - 2)
        conv_step = signal("conv_step", 0, 6, 6 * PH, last=6 * PH - 6)
        dt_ready, bhi_ready, brest_ready, bmid_ready, blo_ready = (
            signal(n, 0, 1, PH, last=PH - 1) for n in ("dt_ready", "bhi_ready", "brest_ready", "bmid_ready", "blo_ready"))
        spx_ready, spm_ready, spe_ready, spl_ready, delta_ready, du_ready = (
            signal(n, 0, 2, 2 * PH, last=2 * PH - 2) for n in ("spx_ready", "spm_ready", "spe_ready", "spl_ready", "delta_ready", "du_ready"))
        bn_done, mv_done, xtok_ready = (
            signal(n, 0, 5 * TB, 6 * TB, first=4 * TB, last=2 * TB) for n in ("bn_done", "mv_done", "xtok_ready"))
        ve_done, rs_done = (signal(n, 0, 5, 6, first=4, last=2) for n in ("ve_done", "rs_done"))
        xT_ready, lg_ready, dd_ready, we_ready, comb_ready, gates_ready = (
            signal(n, 0, 3, 4, first=2, last=2) for n in ("xT_ready", "lg_ready", "dd_ready", "we_ready", "comb_ready", "gates_ready"))
        gate_spread = [signal(f"gate_spread{i}", 0, 2 * E // NGATE + (i == 0), 4 * E // NGATE, 16, 2 * E // NGATE, 2 * E // NGATE) for i in range(NGATE)]
        rt_step = signal("rt_step", 0, 3 * 17, 4 * 17, first=2 * 17, last=2 * 17)
        xs_ready, acc_ready = (
            signal(n, 0, 2 * E, 4 * E, first=2 * E, last=2 * E) for n in ("xs_ready", "acc_ready"))
        g_full, u_full, thg_ready, h1_ready, uc_ready, hh_ready = (
            signal(n, 0, 6 * E, 12 * E, first=6 * E, last=6 * E) for n in ("g_full", "u_full", "thg_ready", "h1_ready", "uc_ready", "hh_ready"))
        x1_ready, hin_ready = (signal(n, 0, 2, 2, last=0) for n in ("x1_ready", "hin_ready"))
        xo_ready = signal("xo_ready", 1, 0, 2, first=0)
        x_loaded = signal("x_loaded", 0, 3, 2, 16, last=0)
        stored = signal("stored", 1, 0, 2, 16, first=0)
        sh_full = signal("sh_full", 0, len(JOBS["pro"]), len(JOBS["body"]), 1, len(JOBS["first"]), len(JOBS["last"]))
        w_loaded = ctx.enter_context(nc.semaphore("w_loaded"))
        consts = ctx.enter_context(nc.semaphore("consts"))
        vprep = ctx.enter_context(nc.semaphore("vprep"))
        aexp = ctx.enter_context(nc.semaphore("aexp"))
        cprep = ctx.enter_context(nc.semaphore("cprep"))

        LOADS = 19

        def filled(sec, key, name):
            return sec.after(sh_full, JOBS[sec.kind][(key, name)])

        def gate_on_chip(sec, x_no):
            return sec.after(gate_spread[x_no % NGATE], x_no // NGATE - (sec.kind in ("first", "body") and x_no % NGATE == 0))

        def tile_banks(sec, n):
            return (g_ps, u_ps) if sec.trip or n % 2 == 0 else (c_ps[0], c_ps[1])

        def bank_back(sec, n):
            return n - 1 if sec.trip else n - 2

        def slot_of(q, s):
            return q // 2, (q % 2) * SL + s

        x_rows = x.rearrange("(p j) (k t) d -> p j t k d", j=2, t=128)
        out_rows = out.rearrange("(p j) (k t) d -> p j t k d", j=2, t=128)

        def unit_no(sec, u):
            return u - 2 if sec.kind in ("last", "epi") else u

        def start_no(sec, u):
            if sec.kind == "pro":
                return u
            if sec.kind in ("first", "body"):
                return u - 1
            return u - 2

        def start_par(sec, u):
            return (u + 1) % 2 if sec.kind == "epi" else u % 2

        NORM_NO = {"pro": {"s0": 0, ("st", 0): 1, ("ln", 0): 2, ("st", 1): 3, ("ln", 1): 4},
                   "body": {("st", 0): 0, ("ln", 0): 1, ("st", 1): 2, ("ln", 1): 3, ("st", 2): 4, ("st", 3): 5},
                   "first": {("st", 0): 0, ("ln", 0): 1, ("ln", 1): 2, ("st", 3): 3},
                   "last": {("st", 1): 0, ("st", 2): 1},
                   "epi": {"s2": 0, ("st", 2): 1}}

        def units_done(sec, u):
            return 2 if sec.kind == "first" and u > 2 else unit_no(sec, u)

        def served(sec, key):
            if key == "s0":
                return 0
            if key == "s2":
                return 2
            if sec.kind == "pro" and key[1] == 1:
                return 2
            return key[1] + 1

        def st_no(sec, key):
            if sec.kind == "pro":
                return served(sec, key)
            if sec.trip:
                return STARTS[sec.kind].index(key[1])
            return 0 if key == "s2" else 1

        def st_par(sec, key):
            if sec.kind == "pro":
                return st_no(sec, key) % 2
            if sec.trip:
                return (key[1] + 1) % 2
            return (st_no(sec, key) + 1) % 2

        def st_src(sec, key):
            u = served(sec, key) % 4 if sec.kind != "pro" else served(sec, key) % 2
            return (xin_sb[:, u], None) if u < 2 else (x2_sb[:, u - 2], u - 2)

        block = ctx.enter_context(nc.Block())

        @block.sync
        def _(sp):
            sp.dma_start(xin_sb[:, 0], x_rows[0, 0]).then_inc(x_loaded.sem, 16)
            sp.dma_start(xin_sb[:, 1], x_rows[0, 1]).then_inc(x_loaded.sem, 16)
            for dst, src in (
                (ws_sb[:, :], Ws), (bs_sb[:, :], bs.broadcast_to([128, E])),
                (wg_sb[:, :, :], Wg), (wu_sb[:, :, :], Wu),
                (wd_sb[:, :, 0, :], Wd[0:128]), (wd_sb[:, :, 1, :], Wd[128:256]), (wd_sb[0:88, :, 2, :], Wd[256:344]),
                (win_sb[:, :, :], Win), (wx_sb[:, :, :, :], Wx), (wdt_sb[:, :, :], Wdt),
                (wblk_sb[:, :, :, :], Wblk), (wout_sb[:, :], Wout), (bout_sb[:, :], bout),
                (normw_sb[:, :], norm_w), (cw_sb[:, :, :, :], conv_w), (cb_sb[:, :, :], conv_b),
                (bdt_sb[:, :, :], bdt), (a_sb[:, :, :, :], A_log), (dp_sb[:, :, :], Dp),
            ):
                sp.dma_start(dst, src).then_inc(w_loaded, 16)
            pro = Section("pro")

            def spread_b(sec, g, par):
                n = g % NS
                sp.dma_start(b_sb[:, g % NB, :], dbc_sb[DTR + NS + n:DTR + NS + n + 1, par, :].unsqueeze(1).broadcast_to([1, 128, T])
                             ).then_inc(b_spread[g % NB].sem, 16)

            def spread_gate(sec, e, x_no):
                if e == 0:
                    start = x_no // E - (sec.kind in ("first", "body"))
                    sp.wait_ge(*sec.after(gates_ready, start))
                else:
                    sp.wait_ge(*sec.after(xs_ready, x_no - NGATE))
                sp.dma_start(gate_sb[:, e % NGATE, :], gates_sb[e:e + 1, :].unsqueeze(1).broadcast_to([1, 128, T])
                             ).then_inc(gate_spread[e % NGATE].sem, 16)

            for x_no in range(2 * E + 1):
                if x_no == E + 2:
                    sp.wait_ge(*pro.after(x1_ready, 0))
                    sp.dma_start(xin_sb[:, 0], x_rows[1, 0]).then_inc(x_loaded.sem, 16)
                spread_gate(pro, x_no % E, x_no)
            for n in range(NB):
                if n == 0:
                    sp.wait_ge(*pro.after(dt_ready, 0))
                spread_b(pro, n, 0)
            def trip(sec):
                for q in range(PH):
                    for n in range(NS):
                        g = q * NS + n
                        u, S = slot_of(q, 2 * n)
                        for e in range(E):
                            if GATE[e] // 2 == S // 2:
                                if e > 0 and u in UNITS[sec.kind]:
                                    spread_gate(sec, e, unit_no(sec, u) * E + e)
                                if e == 0 and u in STARTS[sec.kind]:
                                    nxt = STARTS[sec.kind].index(u) + (sec.kind != "last")
                                    spread_gate(sec, e, nxt * E)
                        if sec.kind == "last" and g + NB >= NG:
                            continue
                        if n == NS - NB:
                            sp.wait_ge(*sec.after(scanned, 2 * g + 1))
                        else:
                            sp.wait_ge(*sec.after(dbu_ready, 2 * g + 1))
                        spread_b(sec, g + NB, (q + (n >= NS - NB)) % 2)
            trip(Section("first"))
            with sp.Fori(0, PAIRS - 2) as it:
                trip(Section("body", it))
            trip(Section("last"))
            sec = Section("epi")
            for x_no in range(2 * E):
                spread_gate(sec, x_no % E, x_no)
            for j in range(2):
                sp.wait_ge(*sec.after(xo_ready, j))
                sp.dma_start(out_rows[PAIRS - 1, j], x2_sb[:, j]).then_inc(stored.sem, 16)
            sp.wait_ge(*sec.after(stored, 1))
            sp.wait_ge(*sec.after(x_loaded, -1))
            for i in range(NGATE):
                sp.wait_ge(*sec.after(gate_spread[i], 2 * E // NGATE - 1))
            for i in range(NB):
                sp.wait_ge(b_spread[i].sem, 16 * (PAIRS * NG // NB))

        @block.tensor
        def _(pe):
            job_count = [0]
            bank_free = []

            def fill(sec, key, name, freed):
                assert JOBS[sec.kind][(key, name)] == job_count[0], (key, name)
                job_count[0] += 1
                for s, n in bank_free:
                    pe.wait_ge(*sec.after(s, n))
                bank_free[:] = [freed]

            def transposes(src):
                for k in range(TB):
                    last = pe.transpose(sh[:, k * 128:(k + 1) * 128], src(k), ident[:, :])
                last.then_inc(sh_full.sem, 1)

            def start_job(sec, key, name):
                a = st_no(sec, key)
                par = st_par(sec, key)
                if name == "xt":
                    fill(sec, key, name, (xT_ready, a))
                    pe.wait_ge(*sec.after(xtok_ready, NORM_NO[sec.kind][key] * TB + TB - 1))
                    transposes(lambda k: xtok[:, k, :])
                elif name == "lg":
                    fill(sec, key, name, (lg_ready, a))
                    pe.wait_ge(*sec.after(xT_ready, a))
                    for k in range(TB):
                        last = pe.matmul(sh[:, k * E:(k + 1) * E], xT_sb[:, par, k * 128:(k + 1) * 128],
                                         ws_sb[:, :], start=True, stop=True)
                    last.then_inc(sh_full.sem, 1)
                else:
                    fill(sec, key, name, (gates_ready, a))
                    pe.wait_ge(*sec.after(comb_ready, a))
                    for k in range(TB):
                        last = pe.transpose(sh[0:E, k * 128:(k + 1) * 128], comb_sb[:, k, :], ident[:, :])
                    last.then_inc(sh_full.sem, 1)

            def norm_job(sec, key):
                j = key[1]
                fill(sec, key, "ht", (hin_ready, j))
                pe.wait_ge(*sec.after(xtok_ready, NORM_NO[sec.kind][key] * TB + TB - 1))
                transposes(lambda k: xtok[:, k, :])

            def unit_tiles(sec, u, S):
                un = unit_no(sec, u)
                par = start_par(sec, u)
                for e in range(E):
                    x_no = un * E + e
                    for ft, (f0, fn) in enumerate(FT):
                        n = x_no * 3 + ft
                        if S == EB[e] + 1 + 2 * ft:
                            pe.wait_ge(*sec.after(xT_ready, start_no(sec, u)))
                            pe.wait_ge(*sec.after(h1_ready, bank_back(sec, n)))
                            pe.matmul(tile_banks(sec, n)[0][0:fn, :], wg_sb[:, e, f0:f0 + fn], xT_sb[:, par, :],
                                      start=True, stop=True).then_inc(g_full.sem, 1)
                        if S == EB[e] + 2 + 2 * ft:
                            pe.wait_ge(*sec.after(xs_ready, x_no))
                            pe.wait_ge(*sec.after(uc_ready, bank_back(sec, n)))
                            pe.matmul(tile_banks(sec, n)[1][0:fn, :], wu_sb[:, e, f0:f0 + fn], xs_sb[:, :],
                                      start=True, stop=True).then_inc(u_full.sem, 1)

            def unit_fills(sec, u, S):
                un = unit_no(sec, u)
                par = start_par(sec, u)
                for e in range(E):
                    x_no = un * E + e
                    if S == DOWN[e]:
                        fill(sec, ("u", u), f"down{e}", (acc_ready, x_no))
                        pe.wait_ge(*sec.after(hh_ready, x_no * 3 + 2))
                        for ft, (f0, fn) in enumerate(FT):
                            last = pe.matmul(sh[:, :], wd_sb[0:fn, e, ft, :], hh_sb[0:fn, (e % 2) * 3 + ft, :],
                                             start=(ft == 0), stop=(ft == 2))
                        last.then_inc(sh_full.sem, 1)
                if S == 62:
                    if u < 2:
                        fill(sec, ("u", u), "yt", (x1_ready, u))
                    else:
                        fill(sec, ("u", u), "yt", (xo_ready, u - 2))
                    pe.wait_ge(*sec.after(acc_ready, un * E + E - 1))
                    transposes(lambda k: acc_sb[:, k * 128:(k + 1) * 128])

            def side_job(sec, q, k, name):
                r = (q + 1) % PH
                l, j, par = r // 2, r % 2, r % 2
                pl, pj = ((q - 1) % PH) // 2, (q - 1) % 2
                key = ("p", q)
                if name == "wblk":
                    fill(sec, key, name, (h_ready, k))
                    pe.wait_ge(*sec.after(y_gated, 2 * k + 1))
                    for b in range(NBLK):
                        last = pe.matmul(sh[:, :], wblk_sb[:, pl, b, :], y_sb[:, b, :], start=(b == 0), stop=(b == 1))
                elif name == "attn":
                    fill(sec, key, name, (x2_ready, 0 if q == 0 else 1))
                    pe.wait_ge(*sec.after(h_ready, k))
                    for t in range(TB):
                        o = sh[:, t * D:(t + 1) * D]
                        pe.matmul(o, h_sb[:, pj, t * 128:(t + 1) * 128], wout_sb[:, :], start=True, stop=False)
                        last = pe.matmul(o, ones_row[:, :], bout_sb[:, :], start=False, stop=True)
                elif name == "ms":
                    fill(sec, key, name, (log_ready, k))
                    pe.wait_ge(*sec.after(sq_ready, k))
                    last = pe.matmul(sh[:, :], mean_w[:, :], norm_t[:, :], start=True, stop=True)
                elif name in ("xp0", "xp1", "z0", "z1"):
                    b = int(name[-1])
                    fill(sec, key, name, (xp_ready if name[0] == "x" else zs_ready, 2 * k + b))
                    pe.wait_ge(*sec.after(xn_ready, k))
                    c = (b if name[0] == "x" else NBLK + b) * 128
                    last = pe.matmul(sh[:, :], win_sb[:, l, c:c + 128], xn_sb[:, :], start=True, stop=True)
                elif name == "wx":
                    fill(sec, key, name, (brest_ready, k))
                    pe.wait_ge(*sec.after(xc_ready, 2 * k + 1))
                    for b in range(NBLK):
                        last = pe.matmul(sh[0:96, :], wx_sb[:, l, b, :], xc_sb[:, par, b, :], start=(b == 0), stop=(b == 1))
                else:
                    b = int(name[-1])
                    fill(sec, key, name, (spx_ready, 2 * k + b))
                    pe.wait_ge(*sec.after(dt_ready, k))
                    last = pe.matmul(sh[:, :], wdt_sb[:, l, b * 128:(b + 1) * 128], dbc_sb[0:DTR, par, :], start=True, stop=True)
                last.then_inc(sh_full.sem, 1)

            def spread_c(sec, g, par):
                pe.matmul(c_ps[g % 2][:, :], sel_c[:, g % NS, :], cs3[:, par, :], start=True, stop=True).then_inc(c_full.sem, 1)

            def add_state(sec, g):
                q, s = g // SL, g % SL
                pe.wait_ge(*sec.after(prod_ready, g))
                if s < 2:
                    pe.wait_ge(*sec.after(y_taken, 2 * q + s))
                pe.matmul(y_ps[s % 2][:, :], ident[:, :], prod_sb[:, g % NPROD, :], start=(s < 2),
                          stop=(s >= SL - 2)).then_inc(summed.sem, 1)

            pe.wait_ge(w_loaded, 16 * LOADS)
            pe.wait_ge(consts, 5)
            pe.wait_ge(vprep, 10)
            for b in range(NBLK):
                pe.matmul(y_ps[b][:, :], ident[:, :], x2_sb[:, 0].rearrange("p k d -> p (k d)"), start=True, stop=True).then_inc(summed.sem, 1)
            pe.matmul(c_ps[0][:, :], ident[:, :], x2_sb[:, 0].rearrange("p k d -> p (k d)"), start=True, stop=True).then_inc(summed.sem, NPROD - 2)
            sec = Section("pro")
            for name in ("xt", "lg", "ct"):
                start_job(sec, "s0", name)
            for u in range(2):
                for S in range(US):
                    unit_tiles(sec, u, S)
                    unit_fills(sec, u, S)
                    for t, name, _ in START:
                        if t == S:
                            start_job(sec, ("st", u), name)
                    if u == 1 and S == LN2[0][0]:
                        norm_job(sec, ("ln", 0))
            norm_job(sec, ("ln", 1))
            for _, name, _ in SIDE:
                if name not in ("wblk", "attn"):
                    side_job(sec, -1, 0, name)
            pe.wait_ge(*sec.after(h1_ready, 6 * E - 1))
            pe.wait_ge(*sec.after(uc_ready, 6 * E - 1))
            pe.wait_ge(*sec.after(blo_ready, 0))
            spread_c(sec, 0, 0)

            def trip(sec):
                job_count[0] = 0
                bank_free[:] = [(zs_ready, -1), (spx_ready, -1), (xo_ready, -1), (gates_ready, -1), (hin_ready, -1)]
                for q in range(PH):
                    for s in range(SL):
                        n, g, gn = s // 2, q * SL + s, q * NS + s // 2
                        u, S = slot_of(q, s)
                        if s % 2 == 0:
                            if n == NS - 1 and sec.pre_runs(q):
                                pe.wait_ge(*sec.after(blo_ready, q))
                            if g > 0:
                                pe.wait_ge(*sec.after(prod_ready, g - 1))
                            else:
                                pe.wait_ge(*sec.after(prod_ready, -1))
                            if gn + 1 < NG or sec.kind != "last":
                                spread_c(sec, gn + 1, (q + (n == NS - 1)) % 2)
                        if g >= LAG:
                            add_state(sec, g - LAG)
                        if g == SG - 1:
                            for behind in range(LAG - 1, -1, -1):
                                add_state(sec, g - behind)
                        if u in UNITS[sec.kind]:
                            unit_tiles(sec, u, S)
                        for t, name, _ in SIDE:
                            if t == s and (name != "attn" or q in (0, PH - 1)) and (
                                    name in ("wblk", "attn") or sec.pre_runs(q)):
                                side_job(sec, q, q, name)
                        if u in UNITS[sec.kind]:
                            unit_fills(sec, u, S)
                        for t, name, _ in START:
                            if t == S and u in STARTS[sec.kind]:
                                start_job(sec, ("st", u), name)
                        if u in (1, 2) and sec.kind != "last" and S == LN2[0][0]:
                            norm_job(sec, ("ln", u - 1))

            trip(Section("first"))
            with pe.Fori(0, PAIRS - 2) as it:
                trip(Section("body", it))
            trip(Section("last"))
            sec = Section("epi")
            job_count[0] = 0
            bank_free[:] = [(zs_ready, -1), (spx_ready, -1), (xo_ready, -1), (gates_ready, -1)]
            side_job(sec, 0, 0, "wblk")
            side_job(sec, 0, 0, "attn")
            for name in ("xt", "lg", "ct"):
                start_job(sec, "s2", name)
            for u in (2, 3):
                for S in range(US):
                    unit_tiles(sec, u, S)
                    unit_fills(sec, u, S)
                    if u == 2:
                        for t, name, _ in START:
                            if t == S:
                                start_job(sec, ("st", u), name)

        @block.scalar
        def _(act):
            def start_act(sec, key, step):
                a, par = st_no(sec, key), st_par(sec, key)
                if step == 46:
                    act.wait_ge(*filled(sec, key, "xt"))
                    done = (units_done(sec, key[1]) * 3 * E - 1) if isinstance(key, tuple) else -1
                    act.wait_ge(*sec.after(u_full, done))
                    act.activation(xT_sb[:, par, :], sh[:, :], ACT.Copy).then_inc(xT_ready.sem, 1)
                elif step == 52:
                    act.wait_ge(*sec.after(dd_ready, a))
                    act.wait_ge(*sec.after(rt_step, a * 17 - 1))
                    act.activation(wt_sb[:, 1, :], wt_sb[:, 0, :], ACT.Exp).then_inc(we_ready.sem, 1)
                elif step == 55:
                    act.wait_ge(*filled(sec, key, "ct"))
                    act.wait_ge(*sec.after(xs_ready, min(unit_no(sec, key[1]) + 1, units_done(sec, key[1] + 1)) * E - 1 if isinstance(key, tuple) else -1))
                    if key == "s2" or (sec.kind == "last" and key[1] == 1):
                        act.wait_ge(*sec.after(gate_spread[0], -1))
                    act.activation(gates_sb[:, :], sh[0:E, :], ACT.Copy).then_inc(gates_ready.sem, 1)

            def unit_act(sec, u, S):
                un = unit_no(sec, u)
                for e in range(E):
                    for ft, (f0, fn) in enumerate(FT):
                        n = (un * E + e) * 3 + ft
                        if S == EB[e] + 3 + 2 * ft:
                            act.wait_ge(*sec.after(g_full, n))
                            act.wait_ge(*sec.after(hh_ready, n - 2))
                            act.activation(th_g[0:fn, n % 2, :], tile_banks(sec, n)[0][0:fn, :], ACT.Tanh, scale=0.5).then_inc(thg_ready.sem, 1)
                        if S == EB[e] + 5 + 2 * ft:
                            act.wait_ge(*sec.after(u_full, n))
                            act.wait_ge(*sec.after(hh_ready, n - 2))
                            act.activation(uc_sb[0:fn, n % 2, :], tile_banks(sec, n)[1][0:fn, :], ACT.Copy).then_inc(uc_ready.sem, 1)

            def norm_act(sec, key):
                j = key[1]
                act.wait_ge(*filled(sec, key, "ht"))
                if sec.trip:
                    act.wait_ge(*sec.after(h_ready, j + 1))
                act.activation(hin_sb[:, j, :], sh[:, :], ACT.Copy).then_inc(hin_ready.sem, 1)

            def side_act(sec, q, k, s):
                if not sec.pre_runs(q):
                    return
                r = (q + 1) % PH
                l, j, par = r // 2, r % 2, r % 2
                key = ("p", q)
                if s == 9:
                    if l == 0:
                        src = hin_sb[:, j, :]
                        act.wait_ge(*sec.after(hin_ready, j - 2 if sec.trip and q == 0 else j))
                    else:
                        src = h_sb[:, j, :]
                    if sec.trip:
                        act.wait_ge(*sec.after(h_ready, k))
                    act.wait_ge(*sec.after(xn_ready, k - 1))
                    act.activation(norm_t[:, :], src, ACT.Square).then_inc(sq_ready.sem, 1)
                elif s == 12:
                    act.wait_ge(*filled(sec, key, "ms"))
                    act.activation(norm_t[:, :], sh[:, :], ACT.Ln, bias=eps_sb[:, 0:1]).then_inc(log_ready.sem, 1)
                    act.wait_ge(*sec.after(log_ready, k))
                    act.activation(norm_t[:, :], norm_t[:, :], ACT.Exp, scale=-0.5).then_inc(rms_ready.sem, 1)
                elif s in (15, 16):
                    b = s - 15
                    act.wait_ge(*filled(sec, key, f"xp{b}"))
                    act.wait_ge(*sec.after(delta_ready, 2 * (k - 1) + b))
                    act.activation(conv_sb[:, b, :], sh[:, :], ACT.Identity, bias=cb_sb[:, l, b:b + 1],
                                   scale=cw_sb[:, l, b, KC - 1:KC]).then_inc(conv_start.sem, 1)
                    act.wait_ge(*sec.after(conv_step, 6 * (k - 1) + 3 * b + 2))
                    act.activation(xpad[:, b, KC - 1:], sh[:, :], ACT.Copy).then_inc(xp_ready.sem, 1)
                if s in (18, 20):
                    b = int(s == 20)
                    act.wait_ge(*filled(sec, key, f"z{b}"))
                    act.wait_ge(*sec.after(zs_ready, 2 * k + b - 1))
                    act.activation(th_z[:, :], sh[:, :], ACT.Tanh, scale=0.5).then_inc(thz_ready.sem, 1)
                if s in (17, 18):
                    b = s - 17
                    act.wait_ge(*sec.after(conv_step, 6 * k + 3 * b + 2))
                    act.wait_ge(*sec.after(delta_ready, 2 * (k - 1) + b))
                    act.activation(th_c[:, b, :], conv_sb[:, b, :], ACT.Tanh).then_inc(thc_ready.sem, 1)
                elif s == 22:
                    act.wait_ge(*filled(sec, key, "wx"))
                    if sec.trip:
                        act.wait_ge(*sec.after(c_full, q * NS))
                        act.wait_ge(*sec.after(b_spread[(q * NS - 1) % NB], (q * NS - 1) // NB + 1))
                    act.activation(dbc_sb[:, par, :], sh[0:DTR + 2 * NS, :], ACT.Copy).then_inc(dt_ready.sem, 1)
                    act.activation(cs3[32:32 + NS, par, :], sh[DTR:DTR + NS, :], ACT.Copy).then_inc(bhi_ready.sem, 1)
                elif s == 24:
                    act.wait_ge(*sec.after(brest_ready, k))
                    act.activation(cs3[0:NS, par, :], rest_sb[0:NS, :], ACT.Copy).then_inc(bmid_ready.sem, 1)
                if s in (26, 28):
                    b = (s - 26) // 2
                    act.wait_ge(*sec.after(spm_ready, 2 * k + b))
                    act.activation(sp_l[:, b, :], sp_l[:, b, :], ACT.Exp).then_inc(spe_ready.sem, 1)
                    if b == 1:
                        for b in range(NBLK):
                            act.wait_ge(*sec.after(spe_ready, 2 * k + b))
                            act.activation(sp_l[:, b, :], sp_l[:, b, :], ACT.Ln, bias=1.0).then_inc(spl_ready.sem, 1)

            act.wait_ge(w_loaded, 16 * LOADS)
            act.wait_ge(vprep, 10)
            act.activation(a_sb[:, :, :, :], a_sb[:, :, :, :], ACT.Exp).then_inc(aexp, 1)
            act.activation(credit[:, 3:4], eps_sb[:, :], ACT.Copy).then_inc(x1_moved.sem, 1)
            sec = Section("pro")
            for S in (46, 52, 55):
                start_act(sec, "s0", S)
            for u in range(2):
                for S in range(US):
                    unit_act(sec, u, S)
                    start_act(sec, ("st", u), S)
                    if u == 1 and S == LN2[0][2]:
                        norm_act(sec, ("ln", 0))
            norm_act(sec, ("ln", 1))
            for s in range(9, SL):
                side_act(sec, -1, 0, s)

            def trip(sec):
                for q in range(PH):
                    l = q // 2
                    for s in range(SL):
                        n, g, gn = s // 2, q * SL + s, q * NS + s // 2
                        u, S = slot_of(q, s)
                        b = s % 2
                        if s < 2:
                            act.wait_ge(*sec.after(delta_ready, 2 * (q - 1) + b))
                        act.wait_ge(*sec.after(scanned, g - 1))
                        act.activation(dA_ps[:, :], delta_sb[:, q % 2, b, :], ACT.Exp,
                                       scale=a_sb[:, l, b, n:n + 1]).then_inc(dA_ready.sem, 1)
                        if u in UNITS[sec.kind]:
                            unit_act(sec, u, S)
                        side_act(sec, q, q, s)
                        if q == PH - 2 and s == 2 and sec.kind != "first":
                            act.wait_ge(*sec.after(xo_ready, 0))
                            act.dma_start(out_rows[sec.pair(-1), 0], x2_sb[:, 0]).then_inc(stored.sem, 16)
                        if q in (0, 2) and s == 4 and sec.kind != "last":
                            j = 1 - q // 2
                            act.wait_ge(*sec.after(x1_ready, -1 if q == 0 else 0))
                            rows = x_rows[sec.pair(1 if q == 0 else 2), j]
                            act.dma_start(xin_sb[:, j], rows).then_inc(x_loaded.sem, 16)
                        if q in (0, 2) and s == 3:
                            j = q // 2
                            act.wait_ge(*sec.after(x2_ready, -1 if j == 0 else 0))
                            act.wait_ge(*sec.after(x1_ready, j - 2))
                            act.activation(x1_sb[:, j], x1_new[:, j], ACT.Copy).then_inc(x1_moved.sem, 1)
                        if u in STARTS[sec.kind]:
                            start_act(sec, ("st", u), S)
                        if u in (1, 2) and sec.kind != "last" and S == LN2[0][2]:
                            norm_act(sec, ("ln", u - 1))
                if sec.kind != "first":
                    act.wait_ge(*sec.after(xo_ready, 1))
                    act.dma_start(out_rows[sec.pair(-1), 1], x2_sb[:, 1]).then_inc(stored.sem, 16)
            trip(Section("first"))
            with act.Fori(0, PAIRS - 2) as it:
                trip(Section("body", it))
            trip(Section("last"))
            sec = Section("epi")
            for S in (46, 52, 55):
                start_act(sec, "s2", S)
            for u in (2, 3):
                for S in range(US):
                    unit_act(sec, u, S)
                    if u == 2:
                        start_act(sec, ("st", u), S)

        @block.vector
        def _(dve):
            def norm_dve(sec, key, src, step):
                m = NORM_NO[sec.kind][key]
                if step == 0:
                    for k in range(TB):
                        if k == 0:
                            dve.wait_ge(*sec.after(mv_done, m * TB - 1))
                        dve.bn_stats(bn_sb[:, k, :], src[:, k, :]).then_inc(bn_done.sem, 1)
                    dve.wait_ge(*sec.after(bn_done, m * TB + TB - 1))
                    dve.wait_ge(*sec.after(xtok_ready, m * TB - 1))
                    dve.wait_ge(*sec.after(ve_done, m - 1))
                    dve.memset(carrier[:, :], 0.0)
                    for k in range(TB):
                        dve.bn_aggr(mv_sb[:, k, :], bn_sb[:, k, :]).then_inc(mv_done.sem, 1)
                else:
                    dve.wait_ge(*sec.after(rs_done, m))
                    for k in range(TB):
                        dve.tensor_scalar(xtok[:, k, :], src[:, k, :], mv_sb[:, k, 0:1], rs_sb[:, 1, k:k + 1],
                                          ALU.subtract, ALU.mult).then_inc(xtok_ready.sem, 1)

            def start_dve(sec, key, step):
                a, par = st_no(sec, key), st_par(sec, key)
                src, j = st_src(sec, key)
                R = [a * 17]

                def link(inst):
                    inst.then_inc(rt_step.sem, 1)
                    dve.wait_ge(*sec.after(rt_step, R[0]))
                    R[0] += 1

                if step == 40:
                    if j is None:
                        load_no = {"pro": {0: 0, 1: 1, 2: 2}, "first": {1: 0, 4: 1}, "body": {1: 0, 4: 1}}[sec.kind][served(sec, key)]
                        dve.wait_ge(*sec.after(x_loaded, load_no))
                    else:
                        dve.wait_ge(*sec.after(x2_ready, -1 if j == 0 else 0))
                    norm_dve(sec, key, src, 0)
                elif step == 43:
                    norm_dve(sec, key, src, 1)
                elif step == 51:
                    dve.wait_ge(*filled(sec, key, "lg"))
                    dve.tensor_tensor(lg_sb[:, :, :], sh[:, 0:TB * E].rearrange("p (k e) -> p k e", e=E),
                                      bs_sb[:, :].unsqueeze(1).broadcast_to([128, TB, E]), ALU.add).then_inc(lg_ready.sem, 1)
                    dve.wait_ge(*sec.after(lg_ready, a))
                    dve.memset(carrier[:, :], 0.0)
                    for k in range(TB):
                        dve.max(mx_sb[:, k, :], lg_sb[:, k, :]).then_inc(rt_step.sem, 1)
                    R[0] += TB
                    dve.wait_ge(*sec.after(rt_step, R[0] - 1))
                    dve.tensor_tensor(wt_sb[:, 0, :], mx_sb[:, :, 1], mx_sb[:, :, 0], ALU.subtract).then_inc(dd_ready.sem, 1)
                    for k in range(TB):
                        dve.max_index(mi_sb[:, k, :], mx_sb[:, k, :], lg_sb[:, k, :]).then_inc(rt_step.sem, 1)
                    R[0] += TB
                    dve.wait_ge(*sec.after(rt_step, R[0] - 1))
                    link(dve.tensor_copy(mf_sb[:, :, :], mi_sb[:, :, 0:2]))
                elif step == 53:
                    R[0] = a * 17 + 9
                    dve.wait_ge(*sec.after(we_ready, a))
                    link(dve.tensor_scalar(wt_sb[:, 2, :], wt_sb[:, 1, :], 4.0, 4.0, ALU.mult, ALU.add))
                    link(dve.reciprocal(wt_sb[:, 3, :], wt_sb[:, 2, :]))
                    link(dve.tensor_tensor(wt_sb[:, 4, :], wt_sb[:, 1, :], wt_sb[:, 3, :], ALU.mult))
                    iota = iota_e[:, :].unsqueeze(1).broadcast_to([128, TB, E])
                    for i in range(2):
                        at = mf_sb[:, :, i].unsqueeze(2).broadcast_to([128, TB, E])
                        w = wt_sb[:, 3 + i, :].unsqueeze(2).broadcast_to([128, TB, E])
                        link(dve.tensor_tensor(eq_sb[:, i], iota, at, ALU.is_equal))
                        link(dve.tensor_tensor(eq_sb[:, 2 + i], eq_sb[:, i], w, ALU.mult))
                    dve.tensor_tensor(comb_sb[:, :, :], eq_sb[:, 2], eq_sb[:, 3], ALU.add).then_inc(comb_ready.sem, 1)
                    link(dve.memset(eq_sb[:, 0, 0, 0:1], 0.0))

            def unit_dve(sec, u, S):
                un, par = unit_no(sec, u), start_par(sec, u)
                for e in range(E):
                    x_no = un * E + e
                    if S == EB[e] + 2:
                        dve.wait_ge(*gate_on_chip(sec, x_no))
                        dve.wait_ge(*sec.after(u_full, x_no * 3 - 1))
                        dve.tensor_tensor(xs_sb[:, :], xT_sb[:, par, :], gate_sb[:, e % NGATE, :], ALU.mult).then_inc(xs_ready.sem, 1)
                    for ft, (f0, fn) in enumerate(FT):
                        n = x_no * 3 + ft
                        if S == EB[e] + 3 + 2 * ft:
                            dve.wait_ge(*sec.after(thg_ready, n))
                            dve.wait_ge(*sec.after(hh_ready, n - 2))
                            dve.scalar_tensor_tensor(h1_sb[0:fn, n % 2, :], th_g[0:fn, n % 2, :], 1.0, tile_banks(sec, n)[0][0:fn, :],
                                                     ALU.add, ALU.mult).then_inc(h1_ready.sem, 1)
                    if S == DOWN[e] + 2:
                        dve.wait_ge(*filled(sec, ("u", u), f"down{e}"))
                        dve.wait_ge(*sec.after(acc_ready, x_no - 1))
                        if e == 0:
                            dve.tensor_copy(acc_sb[:, :], sh[:, :]).then_inc(acc_ready.sem, 1)
                        else:
                            dve.tensor_tensor(acc_sb[:, :], acc_sb[:, :], sh[:, :], ALU.add).then_inc(acc_ready.sem, 1)
                if S == 63:
                    dve.wait_ge(*filled(sec, ("u", u), "yt"))
                    y = sh[:, :].rearrange("p (k d) -> p k d", k=TB)
                    if u < 2:
                        if sec.trip:
                            dve.wait_ge(*sec.after(x1_moved, u))
                        dve.tensor_tensor(x1_new[:, u], xin_sb[:, u], y, ALU.add).then_inc(x1_ready.sem, 1)
                    else:
                        dve.tensor_tensor(x2_sb[:, u - 2], x2_sb[:, u - 2], y, ALU.add).then_inc(xo_ready.sem, 1)

            def ln2_dve(sec, j, step):
                if step == 0:
                    dve.wait_ge(*sec.after(x1_ready, j))
                norm_dve(sec, ("ln", j), x1_new[:, j], step)

            def side_dve(sec, q, k, s):
                r = (q + 1) % PH
                l, j, par = r // 2, r % 2, r % 2
                p = (q - 1) % PH
                pl, pj, ppar = p // 2, p % 2, p % 2
                key = ("p", q)
                has_post = sec.kind != "pro"
                if has_post and s in (3, 4):
                    b = s - 3
                    dve.wait_ge(*sec.after(summed, (q * SL if sec.trip else 0) - 2 + b))
                    dve.wait_ge(*sec.after(h_ready, k - 1))
                    dve.scalar_tensor_tensor(y_sb[:, b, :], xc_sb[:, ppar, b, :], dp_sb[:, pl, b:b + 1],
                                             y_ps[b][:, :], ALU.mult, ALU.add).then_inc(y_taken.sem, 1)
                elif has_post and s == 8:
                    dve.wait_ge(*filled(sec, key, "wblk"))
                    if pl == 0:
                        src = hin_sb[:, pj, :]
                        dve.wait_ge(*sec.after(x2_ready, -1 if pj == 0 else 0))
                    else:
                        src = h_sb[:, pj, :]
                    dve.wait_ge(*sec.after(h_ready, k - 1))
                    dve.tensor_tensor(h_sb[:, pj, :], src, sh[:, :], ALU.add).then_inc(h_ready.sem, 1)
                elif s == 11 and q in (0, PH - 1):
                    dve.wait_ge(*filled(sec, key, "attn"))
                    if sec.trip:
                        dve.wait_ge(*sec.after(x1_moved, -1 if q == 0 else 0))
                    dve.wait_ge(*sec.after(stored, -1 if q == 0 or sec.kind == "first" else 0))
                    dve.tensor_tensor(x2_sb[:, pj], x1_sb[:, pj], sh[:, :].rearrange("p (k d) -> p k d", k=TB),
                                      ALU.add).then_inc(x2_ready.sem, 1)
                if not sec.pre_runs(q):
                    return
                if s == 13:
                    dve.wait_ge(*sec.after(rms_ready, k))
                    if l == 0:
                        dve.wait_ge(*sec.after(hin_ready, j - 2 if sec.trip and q == 0 else j))
                        src = hin_sb[:, j, :]
                    else:
                        dve.wait_ge(*sec.after(h_ready, k))
                        src = h_sb[:, j, :]
                    dve.scalar_tensor_tensor(xn_sb[:, :], src, normw_sb[:, l:l + 1], norm_t[:, :],
                                             ALU.mult, ALU.mult).then_inc(xn_ready.sem, 1)
                for b in range(NBLK):
                    if s == 16 + b:
                        for t in range(KC - 1):
                            if t == 0:
                                dve.wait_ge(*sec.after(conv_start, 2 * k + b))
                                dve.wait_ge(*sec.after(xp_ready, 2 * k + b))
                            else:
                                dve.wait_ge(*sec.after(conv_step, 6 * k + 3 * b + t - 1))
                            c = dve.scalar_tensor_tensor(conv_sb[:, b, :], xpad[:, b, t:t + T], cw_sb[:, l, b, t:t + 1],
                                                         conv_sb[:, b, :], ALU.mult, ALU.add)
                            c.then_inc(conv_step.sem, 1)
                    if s == 18 + b:
                        dve.wait_ge(*sec.after(thc_ready, 2 * k + b))
                        if has_post:
                            dve.wait_ge(*sec.after(y_taken, 2 * k + b))
                        dve.scalar_tensor_tensor(xc_sb[:, par, b, :], th_c[:, b, :], 1.0, conv_sb[:, b, :],
                                                 ALU.add, ALU.mult).then_inc(xc_ready.sem, 1)
                    if s == (18, 20)[b]:
                        dve.wait_ge(*sec.after(thz_ready, 2 * k + b))
                        dve.scalar_tensor_tensor(zs_sb[:, par, b, :], th_z[:, :], 1.0, sh[:, :],
                                                 ALU.add, ALU.mult).then_inc(zs_ready.sem, 1)
                    if s == 25 + 2 * b:
                        dve.wait_ge(*filled(sec, key, f"dt{b}"))
                        dve.wait_ge(*sec.after(xc_ready, 2 * k + b))
                        dve.tensor_scalar(sp_x[:, b, :], sh[:, :], bdt_sb[:, l, b:b + 1], None, ALU.add).then_inc(spx_ready.sem, 1)
                        dve.wait_ge(*sec.after(spx_ready, 2 * k + b))
                        dve.tensor_scalar(sp_l[:, b, :], sp_x[:, b, :], SPLUS, None, ALU.min).then_inc(spm_ready.sem, 1)
                    if s == 29 + b:
                        dve.wait_ge(*sec.after(spl_ready, 2 * k + b))
                        dve.tensor_tensor(delta_sb[:, par, b, :], sp_x[:, b, :], sp_l[:, b, :], ALU.max).then_inc(delta_ready.sem, 1)
                if s == 23:
                    dve.wait_ge(*sec.after(bhi_ready, k))
                    dve.wait_ge(*sec.after(dt_ready, k))
                    dve.wait_ge(*sec.after(blo_ready, k - 1))
                    dve.tensor_tensor(rest_sb[0:NS, :], sh[DTR:DTR + NS, :], cs3[32:32 + NS, par, :], ALU.subtract).then_inc(brest_ready.sem, 1)
                if s == 25:
                    dve.wait_ge(*sec.after(bmid_ready, k))
                    dve.tensor_tensor(cs3[64:64 + NS, par, :], rest_sb[0:NS, :], cs3[0:NS, par, :], ALU.subtract).then_inc(blo_ready.sem, 1)

            def read_out(sec, g):
                dve.wait_ge(*sec.after(scanned, g))
                dve.wait_ge(*sec.after(c_full, g // 2))
                dve.wait_ge(*sec.after(summed, g - NPROD))
                dve.tensor_tensor(prod_sb[:, g % NPROD, :], st_sb[:, g % 2, :], c_ps[(g // 2) % 2][:, :], ALU.mult).then_inc(prod_ready.sem, 1)

            dve.memset(mean_w[:, :], 1.0 / D).then_inc(vprep, 1)
            dve.memset(ones_row[:, :], 1.0).then_inc(vprep, 1)
            for e in range(E):
                last = dve.memset(iota_e[:, e:e + 1], float(e))
            last.then_inc(vprep, 1)
            dve.memset(x2_sb[:, :, :, :], 0.0).then_inc(vprep, 1)
            dve.memset(x1_sb[:, :, :, :], 0.0).then_inc(vprep, 1)
            dve.memset(xpad[:, :, :], 0.0).then_inc(vprep, 1)
            dve.memset(xc_sb[:, :, :, :], 0.0).then_inc(vprep, 1)
            dve.memset(zs_sb[:, :, :, :], 0.0).then_inc(vprep, 1)
            dve.memset(cs3[:, :, :], 0.0).then_inc(vprep, 1)
            dve.memset(eps_sb[:, :], EPS).then_inc(vprep, 1)
            dve.memset(st_sb[:, :, :], 0.0).then_inc(scanned.sem, 4)
            dve.memset(prod_sb[:, :, :], 0.0).then_inc(prod_ready.sem, 2)
            dve.memset(h_sb[:, :, :], 0.0).then_inc(h_ready.sem, 1)
            dve.wait_ge(vprep, 10)
            dve.memset(credit[:, 0:1], 0.0).then_inc(x2_ready.sem, 1)
            dve.memset(credit[:, 1:2], 0.0).then_inc(xo_ready.sem, 1)
            dve.memset(credit[:, 2:3], 0.0).then_inc(stored.sem, 16)
            dve.wait_ge(w_loaded, 16 * LOADS)
            dve.wait_ge(aexp, 1)
            dve.tensor_scalar(a_sb[:, :, :, :], a_sb[:, :, :, :], -1.0, None, ALU.mult).then_inc(vprep, 1)
            dve.tensor_scalar(cw_sb[:, :, :, :], cw_sb[:, :, :, :], 0.5, None, ALU.mult).then_inc(vprep, 1)
            dve.tensor_scalar(cb_sb[:, :, :], cb_sb[:, :, :], 0.5, None, ALU.mult).then_inc(vprep, 1)
            dve.tensor_scalar(wblk_sb[:, :, :, :], wblk_sb[:, :, :, :], 0.5, None, ALU.mult).then_inc(vprep, 1)
            dve.wait_ge(vprep, 14)
            sec = Section("pro")
            for S in (40, 43, 51, 53):
                start_dve(sec, "s0", S)
            for u in range(2):
                for S in range(US):
                    unit_dve(sec, u, S)
                    start_dve(sec, ("st", u), S)
                    if u == 1 and S in (0, 3):
                        ln2_dve(sec, 0, S)
            ln2_dve(sec, 1, 0)
            ln2_dve(sec, 1, 3)
            for s in range(13, SL):
                side_dve(sec, -1, 0, s)

            def trip(sec):
                for q in range(PH):
                    for s in range(SL):
                        g = q * SL + s
                        u, S = slot_of(q, s)
                        dve.wait_ge(*sec.after(dA_ready, g))
                        dve.wait_ge(*sec.after(dbu_ready, g))
                        dve.wait_ge(*sec.after(prod_ready, g - 2))
                        dve.tensor_tensor_scan(st_sb[:, g % 2, :], dA_ps[:, :], dbu_sb[:, g % NDBU, :], 0.0,
                                               ALU.mult, ALU.add).then_inc(scanned.sem, 1)
                        if g > 0:
                            read_out(sec, g - 1)
                        if g == SG - 1:
                            read_out(sec, g)
                        side_dve(sec, q, q, s)
                        if u in UNITS[sec.kind]:
                            unit_dve(sec, u, S)
                        if u in STARTS[sec.kind]:
                            start_dve(sec, ("st", u), S)
                        if u in (1, 2) and sec.kind != "last" and S in (0, 3):
                            ln2_dve(sec, u - 1, S)
            trip(Section("first"))
            with dve.Fori(0, PAIRS - 2) as it:
                trip(Section("body", it))
            trip(Section("last"))
            sec = Section("epi")
            for s in (3, 4, 8, 11):
                side_dve(sec, 0, 0, s)
            for S in (40, 43, 51, 53):
                start_dve(sec, "s2", S)
            for u in (2, 3):
                for S in range(US):
                    unit_dve(sec, u, S)
                    if u == 2:
                        start_dve(sec, ("st", u), S)

        @block.gpsimd
        def _(pool):
            def norm_pool(sec, key):
                m = NORM_NO[sec.kind][key]
                pool.wait_ge(*sec.after(mv_done, m * TB + TB - 1))
                pool.wait_ge(*sec.after(rs_done, m - 1))
                pool.tensor_tensor(rs_sb[:, 0, :], mv_sb[:, :, 1], eps4[:, :], ALU.add).then_inc(ve_done.sem, 1)
                pool.wait_ge(*sec.after(ve_done, m))
                pool.wait_ge(*sec.after(xtok_ready, m * TB - 1))
                pool.tensor_tensor(rs_sb[:, 1, :], rs_sb[:, 0, :], neg_half[:, :], ALU.pow).then_inc(rs_done.sem, 1)

            def unit_pool(sec, u, S):
                un = unit_no(sec, u)
                for e in range(E):
                    for ft, (f0, fn) in enumerate(FT):
                        n = (un * E + e) * 3 + ft
                        if S == EB[e] + 6 + 2 * ft:
                            pool.wait_ge(*sec.after(h1_ready, n))
                            pool.wait_ge(*sec.after(uc_ready, n))
                            pool.wait_ge(*sec.after(acc_ready, un * E + e - 2))
                            pool.tensor_tensor(hh_sb[0:fn, (e % 2) * 3 + ft, :], h1_sb[0:fn, n % 2, :],
                                               uc_sb[0:fn, n % 2, :], ALU.mult).then_inc(hh_ready.sem, 1)

            def side_pool(sec, q, k, s):
                par = (q + 1) % 2
                ppar = (q - 1) % 2
                if sec.kind != "pro" and s in (4, 5):
                    b = s - 4
                    pool.wait_ge(*sec.after(y_taken, 2 * k + b))
                    pool.tensor_tensor(y_sb[:, b, :], y_sb[:, b, :], zs_sb[:, ppar, b, :], ALU.mult).then_inc(y_gated.sem, 1)
                if sec.pre_runs(q) and s == 29:
                    for b in range(NBLK):
                        pool.wait_ge(*sec.after(delta_ready, 2 * k + b))
                        if sec.trip:
                            pool.wait_ge(*sec.after(dbu_ready, q * SL - 1 + LEAD))
                        pool.tensor_tensor(du_sb[:, par, b, :], delta_sb[:, par, b, :], xc_sb[:, par, b, :],
                                           ALU.mult).then_inc(du_ready.sem, 1)

            def scale_b(sec, g):
                gn, b = g // 2, g % 2
                if g % SL < 2:
                    pool.wait_ge(*sec.after(du_ready, 2 * (g // SL - 1) + b if sec.trip else b))
                pool.wait_ge(*sec.after(b_spread[gn % NB], gn // NB))
                if sec.trip:
                    pool.wait_ge(*sec.after(scanned, g - NDBU))
                pool.tensor_tensor(dbu_sb[:, g % NDBU, :], du_sb[:, (g // SL) % 2, b, :], b_sb[:, gn % NB, :],
                                   ALU.mult).then_inc(dbu_ready.sem, 1)

            pool.memset(eps4[:, :], EPS).then_inc(consts, 1)
            pool.memset(dbu_sb[:, :, :], 0.0).then_inc(dbu_ready.sem, 1)
            pool.memset(ident[:, :], 0.0).then_inc(cprep, 1)
            pool.memset(sel_c[:, :, :], 0.0).then_inc(cprep, 1)
            pool.wait_ge(cprep, 2)
            pool.affine_select(out=ident[:, :], in_=ident[:, :], compare_op=ALU.not_equal, fill=1.0, base=0,
                               pattern=[[-1, 128]], channel_multiplier=1).then_inc(consts, 1)
            for a in range(3):
                pool.affine_select(out=sel_c[:, :, :], in_=sel_c[:, :, :], compare_op=ALU.not_equal, fill=1.0,
                                   base=-32 * a, pattern=[[-1, NS], [0, 128]], channel_multiplier=1).then_inc(cprep, 1)
                pool.wait_ge(cprep, 3 + a)
            pool.memset(neg_half[:, :], -0.5).then_inc(consts, 3)
            sec = Section("pro")
            norm_pool(sec, "s0")
            for u in range(2):
                for S in range(US):
                    unit_pool(sec, u, S)
                    if S == 41:
                        norm_pool(sec, ("st", u))
                    if u == 1 and S == 1:
                        norm_pool(sec, ("ln", 0))
            norm_pool(sec, ("ln", 1))
            side_pool(sec, -1, 0, 29)
            for g in range(LEAD):
                scale_b(sec, g)

            def trip(sec):
                for q in range(PH):
                    for s in range(SL):
                        g, gn, b = q * SL + s, q * NS + s // 2, s % 2
                        u, S = slot_of(q, s)
                        if g + LEAD < SG or sec.kind != "last":
                            scale_b(sec, g + LEAD)
                        side_pool(sec, q, q, s)
                        if u in UNITS[sec.kind]:
                            unit_pool(sec, u, S)
                        if S == 41 and u in STARTS[sec.kind]:
                            norm_pool(sec, ("st", u))
                        if u in (1, 2) and sec.kind != "last" and S == 1:
                            norm_pool(sec, ("ln", u - 1))
            trip(Section("first"))
            with pool.Fori(0, PAIRS - 2) as it:
                trip(Section("body", it))
            trip(Section("last"))
            sec = Section("epi")
            for s in (4, 5):
                side_pool(sec, 0, 0, s)
            norm_pool(sec, "s2")
            for u in (2, 3):
                for S in range(US):
                    unit_pool(sec, u, S)
                    if u == 2 and S == 41:
                        norm_pool(sec, ("st", u))


def laid_out(name, a):
    import numpy as np

    name = name.split("_", 2)[2]
    if name in ("Win", "Wdt", "Wg", "Wu", "Wd"):
        return a.transpose(1, 0, 2)
    if name == "Wx":
        a = np.concatenate([a[..., :DTR], a[..., DTR + NS:], a[..., DTR:DTR + NS]], -1)
    if name in ("Wx", "Wblk", "conv_w", "A_log"):
        return a.reshape(NL, NBLK, 128, -1).transpose(2, 0, 1, 3)
    if name in ("conv_b", "bdt", "Dp"):
        return a.reshape(NL, NBLK, 128).transpose(2, 0, 1)
    if name == "norm_w":
        return a.T
    if name in ("bout", "bs"):
        return a.reshape(1, -1)
    return a


_ARGS = ["L0_attn_x", "L0_attn_norm_w", "L0_attn_Win", "L0_attn_conv_w", "L0_attn_conv_b", "L0_attn_Wx",
         "L0_attn_Wdt", "L0_attn_bdt", "L0_attn_A_log", "L0_attn_Dp", "L0_attn_Wblk", "L0_attn_Wout",
         "L0_attn_bout", "L0_ffn_Ws", "L0_ffn_bs", "L0_ffn_Wg", "L0_ffn_Wu", "L0_ffn_Wd"]


def kernel(**inputs):
    import numpy as np
    import concourse.bacc as bacc
    from concourse.bass_utils import run_bass_kernel_spmd

    nc = bacc.Bacc("TRN2", target_bir_lowering=False, num_devices=1)
    arrays, args = {}, []
    for name in _ARGS:
        a = np.ascontiguousarray(laid_out(name, np.asarray(inputs[name])))
        arrays[f"in_{name}"] = a
        args.append(nc.dram_tensor(f"in_{name}", a.shape, F32, kind="ExternalInput").ap())
    args.append(nc.dram_tensor("out_0", (B, T, D), F32, kind="ExternalOutput").ap())
    build(nc, *args)
    r = run_bass_kernel_spmd(nc, [arrays], core_ids=[0])
    return r.results[0]["out_0"]
```
